# Optimizing a Trainium2 kernel written in Bass

```python
import numpy as np
import jax
import jax.numpy as jnp

def _softmax(x, axis=-1):
    return jax.nn.softmax(x, axis=axis)

def _gelu(x):
    return jax.nn.gelu(x, approximate=True)

def _silu(x):
    return jax.nn.silu(x)

def _sigmoid(x):
    return jax.nn.sigmoid(x)

def _layernorm(x, axis=-1, eps=1e-05):
    m = jnp.mean(x, axis=axis, keepdims=True)
    v = jnp.var(x, axis=axis, keepdims=True)
    return (x - m) / jnp.sqrt(v + eps)

def _scatter_add(tgt, idx, src, axis=0):
    return tgt.at[idx].add(src)

def _segment_sum(src, seg, n):
    return jax.ops.segment_sum(src, seg, n)
kernel_name = 'mk_flamingo_gated_d1_seqx_r4_ba1ed9'

def setup_inputs(seed: int=0):
    np.random.seed(seed)
    _w = jnp.asarray

    def _rec_inputs():
        import jax
        import jax.numpy as jnp
        _rk = jax.random.key(seed)
        x = -0.000125 + 0.9999 * jax.random.normal(jax.random.fold_in(_rk, 1), (4, 512, 512), jnp.float32)
        _lenS = 512 - jax.random.randint(jax.random.fold_in(_rk, 7), (4,), 0, max(1, 512 // 4) + 1, jnp.int32)
        _lenS2 = 512 - jax.random.randint(jax.random.fold_in(_rk, 8), (4,), 0, max(1, 512 // 4) + 1, jnp.int32)
        fside_BxS2xS2_0 = -3.05549e-07 + 0.0199987 * jax.random.normal(jax.random.fold_in(_rk, 11), (4, 512, 512), jnp.float32)
        _ctx_1024P = jax.random.normal(jax.random.fold_in(_rk, 12), (4, 16, 256), jnp.float32)
        _ctx_1024c = jax.random.dirichlet(jax.random.fold_in(_rk, 512), 0.3 * jnp.ones((16,), jnp.float32), (4, 512))
        _ctx_1024t = jnp.einsum('bsk,bkd->bsd', _ctx_1024c, _ctx_1024P)
        _ctx_1024t = _ctx_1024t * jax.lax.rsqrt(jnp.mean(jnp.square(_ctx_1024t)) + 1e-12) * 0.953939
        ctx_1024 = 6.82029e-06 + 0.0200006 * (_ctx_1024t + 0.3 * jax.random.normal(jax.random.fold_in(_rk, 612), (4, 512, 256), jnp.float32))
        _g = jax.random.normal(jax.random.fold_in(_rk, 9001), (2, 1), jnp.float32)
        _g = jnp.sign(_g) * jnp.maximum(jnp.abs(_g), 1.0) + (_g == 0) * 1.0
        g_xattn = _g[0]
        g_ffn = _g[1]
        return (x, fside_BxS2xS2_0, ctx_1024, g_xattn, g_ffn)
    x, fside_BxS2xS2_0, ctx_1024, g_xattn, g_ffn = _rec_inputs()

    def _L0_xattn_setup():
        import jax, jax.numpy as jnp
        import numpy as np
        EPS = 1e-06
        QMAX = 127.0

        def _smooth_quant_linear(x, w):
            amax_x = jnp.max(jnp.abs(x), axis=0)
            amax_w = jnp.max(jnp.abs(w), axis=0)
            s = jnp.sqrt(jnp.maximum(amax_x, EPS) / jnp.maximum(amax_w, EPS))
            s = jnp.maximum(s, EPS)
            xs = x / s
            ws = w * s
            x_scale = jnp.maximum(jnp.max(jnp.abs(xs), axis=-1, keepdims=True), EPS) / QMAX
            w_scale = jnp.maximum(jnp.max(jnp.abs(ws), axis=-1, keepdims=True), EPS) / QMAX
            x_q = jnp.clip(jnp.round(xs / x_scale), -QMAX, QMAX)
            w_q = jnp.clip(jnp.round(ws / w_scale), -QMAX, QMAX)
            return x_q @ w_q.T * x_scale * w_scale.T

        def _expert_forward(xe, guw, dw):
            h = _smooth_quant_linear(xe, guw)
            gate, up = jnp.split(h, 2, axis=-1)
            a = jax.nn.silu(gate) * up
            return _smooth_quant_linear(a, dw)
        key = jax.random.key(seed)
        k1, k2, k3 = jax.random.split(key, 3)
        E, T, D, I = (8, 512, 512, 256)
        x = jax.random.normal(k1, (E, T, D), dtype=jnp.float32)
        gate_up_weight = jax.random.normal(k2, (E, 2 * I, D), dtype=jnp.float32) * 0.02
        down_weight = jax.random.normal(k3, (E, D, I), dtype=jnp.float32) * 0.02
        return {'x': x, 'gate_up_weight': gate_up_weight, 'down_weight': down_weight}
    _L0_xattn_all = _L0_xattn_setup()
    _L0_xattn_in = {k: v for k, v in _L0_xattn_all.items() if k in ()}
    del _L0_xattn_all

    def _L0_ffn_setup():
        import jax, jax.numpy as jnp
        import numpy as np
        TOP_K = 4
        key = jax.random.key(seed)
        ks = jax.random.split(key, 9)
        B, T, D, H, NE = (2, 256, 512, 352, 16)
        s = 0.02
        return {'x': jax.random.normal(ks[0], (B, T, D), jnp.float32), 'gate_w': jax.random.normal(ks[1], (NE, D), jnp.float32) * s, 'gate_b': jax.random.normal(ks[2], (NE,), jnp.float32) * s, 'w1_shared': jax.random.normal(ks[3], (D, H), jnp.float32) * s, 'w2_shared': jax.random.normal(ks[4], (H, D), jnp.float32) * s, 'w3_shared': jax.random.normal(ks[5], (D, H), jnp.float32) * s, 'w1_routed': jax.random.normal(ks[6], (NE, D, H), jnp.float32) * s, 'w2_routed': jax.random.normal(ks[7], (NE, H, D), jnp.float32) * s, 'w3_routed': jax.random.normal(ks[8], (NE, D, H), jnp.float32) * s}
    _L0_ffn_all = _L0_ffn_setup()
    _L0_ffn_in = {k: v for k, v in _L0_ffn_all.items() if k in ('gate_w', 'gate_b', 'w1_shared', 'w2_shared', 'w3_shared', 'w1_routed', 'w2_routed', 'w3_routed')}
    del _L0_ffn_all
    return {'x': x, 'fside_BxS2xS2_0': fside_BxS2xS2_0, 'ctx_1024': ctx_1024, 'g_xattn': g_xattn, 'g_ffn': g_ffn, 'L0_ffn_gate_w': _L0_ffn_in['gate_w'], 'L0_ffn_gate_b': _L0_ffn_in['gate_b'], 'L0_ffn_w1_shared': _L0_ffn_in['w1_shared'], 'L0_ffn_w2_shared': _L0_ffn_in['w2_shared'], 'L0_ffn_w3_shared': _L0_ffn_in['w3_shared'], 'L0_ffn_w1_routed': _L0_ffn_in['w1_routed'], 'L0_ffn_w2_routed': _L0_ffn_in['w2_routed'], 'L0_ffn_w3_routed': _L0_ffn_in['w3_routed']}

def reference(x, fside_BxS2xS2_0, ctx_1024, g_xattn, g_ffn, L0_ffn_gate_w, L0_ffn_gate_b, L0_ffn_w1_shared, L0_ffn_w2_shared, L0_ffn_w3_shared, L0_ffn_w1_routed, L0_ffn_w2_routed, L0_ffn_w3_routed):
    import jax
    import jax.numpy as jnp

    def _L0_xattn_ref(x, gate_up_weight, down_weight):
        import jax, jax.numpy as jnp
        import numpy as np
        EPS = 1e-06
        QMAX = 127.0

        def _smooth_quant_linear(x, w):
            amax_x = jnp.max(jnp.abs(x), axis=0)
            amax_w = jnp.max(jnp.abs(w), axis=0)
            s = jnp.sqrt(jnp.maximum(amax_x, EPS) / jnp.maximum(amax_w, EPS))
            s = jnp.maximum(s, EPS)
            xs = x / s
            ws = w * s
            x_scale = jnp.maximum(jnp.max(jnp.abs(xs), axis=-1, keepdims=True), EPS) / QMAX
            w_scale = jnp.maximum(jnp.max(jnp.abs(ws), axis=-1, keepdims=True), EPS) / QMAX
            x_q = jnp.clip(jnp.round(xs / x_scale), -QMAX, QMAX)
            w_q = jnp.clip(jnp.round(ws / w_scale), -QMAX, QMAX)
            return x_q @ w_q.T * x_scale * w_scale.T

        def _expert_forward(xe, guw, dw):
            h = _smooth_quant_linear(xe, guw)
            gate, up = jnp.split(h, 2, axis=-1)
            a = jax.nn.silu(gate) * up
            return _smooth_quant_linear(a, dw)
        return jax.vmap(_expert_forward)(x, gate_up_weight, down_weight)

    def _L0_ffn_ref(x, gate_w, gate_b, w1_shared, w2_shared, w3_shared, w1_routed, w2_routed, w3_routed):
        import jax, jax.numpy as jnp
        import numpy as np
        TOP_K = 4
        n_experts = w1_routed.shape[0]
        logits = jnp.einsum('ed,btd->bte', gate_w, x)
        scores = jax.nn.sigmoid(logits) + gate_b
        weights, indices = jax.lax.top_k(scores, TOP_K)
        weights = weights / weights.sum(-1, keepdims=True)
        shared_out = jax.nn.silu(x @ w1_shared) * (x @ w3_shared) @ w2_shared
        one_hot = jax.nn.one_hot(indices, n_experts, dtype=x.dtype)
        router_probs = (weights[..., None] * one_hot).sum(-2)
        h1 = jnp.einsum('btd,edc->btec', x, w1_routed)
        h2 = jnp.einsum('btd,edc->btec', x, w3_routed)
        h3 = jax.nn.silu(h1 * h2)
        experts_out = jnp.einsum('btec,ecd->bted', h3, w2_routed)
        routed_out = jnp.einsum('bted,bte->btd', experts_out, router_probs)
        return shared_out + routed_out
    x = x + jnp.tanh(g_xattn[0]) * _L0_xattn_ref(_layernorm(x, axis=-1), fside_BxS2xS2_0, ctx_1024)
    x = x + jnp.tanh(g_ffn[0]) * _L0_ffn_ref(_layernorm(x, axis=-1), L0_ffn_gate_w, L0_ffn_gate_b, L0_ffn_w1_shared, L0_ffn_w2_shared, L0_ffn_w3_shared, L0_ffn_w1_routed, L0_ffn_w2_routed, L0_ffn_w3_routed)
    return x

_drawn_inputs = setup_inputs


def setup_inputs(seed=0):
    import zlib

    import numpy as np

    out = dict(_drawn_inputs(seed))
    spreads = {}
    factors = {'L0_ffn_gate_w': 3.487,
     'L0_ffn_gate_b': 8.0,
     'L0_ffn_w1_routed': 3.045,
     'L0_ffn_w2_routed': 3.001,
     'L0_ffn_w3_routed': 3.043}
    for name, (base, spread) in spreads.items():
        noise = np.random.default_rng([zlib.crc32(name.encode()), seed]).standard_normal(out[name].shape)
        drawn = base * np.exp(spread * noise) if base else spread * noise
        out[name] = jnp.asarray(drawn.astype(out[name].dtype))
    for name, factor in factors.items():
        out[name] = (out[name] * factor).astype(out[name].dtype)
    return out
```

```python
from contextlib import ExitStack

import concourse.bass as bass
from concourse import mybir

F32 = mybir.dt.float32
F32R = mybir.dt.float32r
BF16 = mybir.dt.bfloat16
I32 = mybir.dt.int32
U32 = mybir.dt.uint32
SIZE = {F32: 4, F32R: 4, BF16: 2, I32: 4, U32: 4}
ALU = mybir.AluOpType
ACT = mybir.ActivationFunctionType
AX = mybir.AxisListType

P = 128
TOPK = 4
QMAX = 127.0
Q_EPS = 1e-6
LN_EPS = 1e-5
ROUND = 1.5 * 2.0**23
ROWS = 4


def flamingo_moe(nc, x, w_gate_up, w_down, g_xattn, g_ffn, gate_w, gate_b, w1_shared, w2_shared,
                 w3_shared, w1_routed, w2_routed, w3_routed, out):
    B, S, D = x.shape
    I = w_down.shape[2]
    NE, _, H = w1_routed.shape
    TOK = B * S
    KC = D // P
    TT = TOK // P
    HSTEP = (H - P) // 2
    HC = [(0, HSTEP), (HSTEP, HSTEP), (2 * HSTEP, P)]
    assert S == ROWS * P and D == 4 * P and I == 2 * P and 2 * P < H < 3 * P and H % 2 == 0 and NE == 16
    TILES = (TOK * TOPK + NE * (P - 1)) // P
    REGION = TOK + P
    W13 = KC * 2 * H
    W2 = len(HC) * D
    SPLITS = 2
    LINEARS = {1: KC, 2: I // P}
    SCATTERS = ROWS * TOPK
    BE = ROWS * TOPK * NE

    x_rows = x.rearrange("b (r p) d -> b p r d", p=P)
    out_rows = out.rearrange("b (r p) d -> (b r) p d", p=P)
    dispatched = nc.dram_tensor("dispatched", [NE * REGION, D], F32, kind="Internal").ap()
    expert_out = nc.dram_tensor("expert_out", [TILES * P, D], F32, kind="Internal").ap()

    with ExitStack() as ctx:
        place = [(nc.sbuf_base + 31) // 32 * 32]

        def sb(name, shape, dt, at=None):
            n = SIZE[dt]
            for s in shape[1:]:
                n *= s
            where = place[0] if at is None else at
            if at is None:
                place[0] += (n + 31) // 32 * 32
            assert where + n <= nc.sbuf_usable_end, (name, where, n)
            return nc.alloc_sbuf_tensor_at(name, shape, dt, offset=where)

        def sem(name):
            return ctx.enter_context(nc.semaphore(name))

        bank = [ctx.enter_context(nc.psum_tensor(f"bank{i}", [P, 512], F32)) for i in range(8)]

        ident = sb("ident", [P, P], F32)
        ident_b = sb("ident_b", [P, P], BF16)
        ones_b = sb("ones_b", [P, P], BF16)
        before_b = sb("before_b", [P, P], BF16)
        iota_e = sb("iota_e", [P, NE], F32)
        region_start = sb("region_start", [P, NE], F32)
        one_e = sb("one_e", [P, NE], F32)
        eps_ln = sb("eps_ln", [P, 1], F32)
        gates = sb("gates", [P, 2], F32)
        bias_e = sb("bias_e", [P, NE], F32)
        gate_rows = sb("gate_rows", [NE, D], F32)
        gate_hi = sb("gate_hi", [P, KC, NE], F32R)
        gate_lo = sb("gate_lo", [P, KC, NE], F32R)

        acc = sb("acc", [P, TT * D], F32)
        ring_at = place[0]
        ring13_hi = sb("ring13_hi", [P, 2 * W13], F32R)
        ring13_lo = sb("ring13_lo", [P, 2 * W13], F32R)
        ring2_hi = sb("ring2_hi", [P, 2 * W2], F32R)
        ring2_lo = sb("ring2_lo", [P, 2 * W2], F32R)
        raw13 = sb("raw13", [P, KC, 2, H], F32)
        raw2 = sb("raw2", [P, len(HC), D], F32)

        onehot_all = sb("onehot_all", [P, TT * TOPK * NE], F32)
        row_all = sb("row_all", [P, TT * TOPK], F32)
        weight_all = sb("weight_all", [P, TT * TOPK], F32)
        score = sb("score", [P, ROWS * NE], F32)
        top8 = sb("top8", [P, ROWS, 8], F32)
        top8_at = sb("top8_at", [P, ROWS, 8], U32)
        top_at = sb("top_at", [P, ROWS * TOPK], F32)
        onehot = sb("onehot", [P, BE], F32)
        taken = sb("taken", [P, ROWS * NE], BF16)
        total4 = sb("total4", [P, ROWS], F32)
        weight = sb("weight", [P, ROWS * TOPK], F32)
        next_row = sb("next_row", [P, NE], F32)
        pos = sb("pos", [P, ROWS * NE], F32)
        picked = sb("picked", [P, BE], F32)
        row_f = sb("row_f", [P, ROWS * TOPK], F32)
        row_u = sb("row_u", [P, ROWS * TOPK], U32)

        xt_hi = sb("xt_hi", [P, ROWS, KC * P], F32R)
        xt_lo = sb("xt_lo", [P, ROWS, KC * P], F32R)
        h1 = [sb(f"h1_{i}", [P, H], F32) for i in range(2)]
        h3 = [sb(f"h3_{i}", [P, H], F32) for i in range(2)]
        ht_hi = [sb(f"ht_hi{i}", [P, len(HC) * P], F32R) for i in range(2)]
        ht_lo = [sb(f"ht_lo{i}", [P, len(HC) * P], F32R) for i in range(2)]

        stage_a = place[0]
        wa1 = sb("wa1", [P, ROWS, D], F32)
        wa2 = sb("wa2", [P, ROWS, I], F32)
        xa_at = place[0]
        xa1 = sb("xa1", [P, ROWS, D], F32)
        xa2 = sb("xa2", [P, ROWS, I], F32, at=xa_at)
        lin2_out = sb("lin2_out", [P, 2, D], F32, at=xa_at + ROWS * I * 4)
        hid = sb("hid", [P, ROWS, D], F32)
        xq = sb("xq", [P, ROWS, D], BF16)
        wq = sb("wq", [P, ROWS, D], BF16)
        xq_t = sb("xq_t", [P, KC, ROWS * P], BF16)
        wq_t = sb("wq_t", [P, KC, ROWS * P], BF16)
        wscale_b = sb("wscale_b", [P, D], F32)
        stats = sb("stats", [P, ROWS, 6], F32)
        mean_var = sb("mean_var", [P, ROWS, 2], F32)
        std = sb("std", [P, ROWS], F32)
        rstd = sb("rstd", [P, ROWS], F32)
        amax = {L: sb(f"amax{L}", [P, 2, k], F32) for L, k in LINEARS.items()}
        ratio = {L: sb(f"ratio{L}", [P, k], F32) for L, k in LINEARS.items()}
        smooth = {L: sb(f"smooth{L}", [P, 2, k], F32) for L, k in LINEARS.items()}
        row_max = sb("row_max", [P, 2, ROWS], F32)
        q_scale = sb("q_scale", [P, 2, ROWS], F32)
        q_inv = sb("q_inv", [P, 2, ROWS], F32)

        end_a = place[0]
        place[0] = stage_a
        x_in = [sb(f"x_in{i}", [P, D], F32) for i in range(2)]
        y_out = [sb(f"y_out{i}", [P, D], F32) for i in range(2)]
        xr_hi = [sb(f"xr_hi{i}", [P, KC * P], F32R) for i in range(2)]
        xr_lo = [sb(f"xr_lo{i}", [P, KC * P], F32R) for i in range(2)]
        zero_rows = sb("zero_rows", [P, D], F32)
        count = sb("count", [P, NE], F32)
        tiles_i = sb("tiles_i", [P, NE], I32)
        tiles_f = sb("tiles_f", [P, NE], F32)
        tile_end = sb("tile_end", [P, NE], F32)
        tile_start = sb("tile_start", [P, NE], F32)
        shift_e = sb("shift_e", [P, NE], F32)
        shifted = sb("shifted", [P, TT * TOPK, NE], F32)
        out_row_f = sb("out_row_f", [P, TT * TOPK], F32)
        out_row = sb("out_row", [P, TT * TOPK], U32)
        iota_t = sb("iota_t", [1, TILES], F32)
        begun = sb("begun", [1, TILES, NE], F32)
        begun_at = sb("begun_at", [1, TILES, NE], F32)
        tile_expert = sb("tile_expert", [1, TILES], F32)
        tile_first = sb("tile_first", [1, TILES], F32)
        tile_live = sb("tile_live", [1, TILES], F32)
        tile_tmp = sb("tile_tmp", [1, TILES], F32)
        tab_row = sb("tab_row", [1, TILES], I32)
        tab_slot = sb("tab_slot", [1, TILES], I32)
        tab_splits = sb("tab_splits", [1, TILES], I32)
        tab_pad = sb("tab_pad", [1, NE], I32)
        tab_start = sb("tab_start", [1, NE], I32)
        place[0] = max(place[0], end_a)
        G_BUFS = 4
        rows_of_4 = [sb(f"rows_of_4_{i}", [P, TOPK, D], F32, at=ring_at + i * TOPK * D * 4)
                     for i in range(G_BUFS)]

        names = (
            "consts gates_in gate_rows_in gates_ready gate_t gate_hi_ready gate_lo_ready "
            "x_loaded wa1_loaded wa2_loaded ln_var ln_std xn_ready "
            "w_t1 w_t2 x_t1 x_t2 w_max1 w_max2 x_max1 x_max2 ratio1 ratio2 s_raw1 s_raw2 "
            "smooth1 smooth2 bc1 bc2 scaled_w1 scaled_w2 scales1 scales2 "
            "wt1 wt2 xs1 xs2 wq_ready1 wq_ready2 xq_ready1 xq_ready2 wq_t1 wq_t2 wq_e1 wq_e2 "
            "xq_t1 xq_t2 xq_e1 xq_e2 wsc1 wsc2 wsc_e1 wsc_e2 mm1 mm2 mm_e1 mm_e2 "
            "silu_gate a_ready x1_done xn2_ready xn2_t xn2_hi xn2_lo logits exp_ready taken_ready prefix "
            "rows_ready scattered dve_chain pool_chain route_chain "
            "raw13_in raw2_in hi13_in hi2_in weights_ready sh_h sh_h1 sh_prod sh_t sh_hi sh_lo sh_y sh_y_e "
            "out_rows_known tables_ready zero_ready pads_written xr_t xr_hi_s xr_lo_s d_h d_h1 d_prod d_act d_t "
            "d_hi d_lo d_y d_y_e out_ready out_stored"
        ).split()
        s = {n: sem("s_" + n) for n in names}
        tile_in = [sem(f"s_tile_in{i}") for i in range(2)]
        y_stored = [sem(f"s_y_stored{i}") for i in range(2)]
        gathered_s = [sem(f"s_gathered{i}") for i in range(G_BUFS)]

        def acc_tile(t):
            return acc[:, bass.ds(t * D, D)]

        def ring13(half, slot_at, c, m):
            return half[:, bass.ds(slot_at + (c * 2 + m) * H, H)]

        def ring2(half, slot_at, c):
            return half[0:HC[c][1], bass.ds(slot_at + c * D, D)]

        block = ctx.enter_context(nc.Block())

        @block.sync
        def _(sp):
            sp.dma_start(gates[:, 0:1], g_xattn.partition_broadcast(P)).then_inc(s["gates_in"], 16)
            sp.dma_start(gates[:, 1:2], g_ffn.partition_broadcast(P)).then_inc(s["gates_in"], 16)
            sp.dma_start(bias_e[:, :], gate_b.partition_broadcast(P)).then_inc(s["gates_in"], 16)
            sp.dma_start(gate_rows[:, :], gate_w).then_inc(s["gate_rows_in"], 16)

            def load_batch(b):
                xb = x_rows[bass.ds(b, 1)].rearrange("a p r d -> (a p) r d")
                sp.dma_start(acc[:, bass.ds(b * ROWS * D, ROWS * D)].rearrange(
                    "p (r d) -> p r d", r=ROWS), xb).then_inc(s["x_loaded"], 16)

            def load_weights(b):
                src = w_gate_up[bass.ds(b, 1)].rearrange("a (r p) d -> p (a r) d", p=P)
                sp.dma_start(wa1[:, :, :], src).then_inc(s["wa1_loaded"], 16)

            def load_down(b):
                src = w_down[bass.ds(b, 1)].rearrange("a (r p) d -> p (a r) d", p=P)
                sp.dma_start(wa2[:, :, :], src).then_inc(s["wa2_loaded"], 16)

            load_batch(0)
            load_weights(0)
            load_down(0)
            with sp.Fori(1, B, 1) as b:
                sp.wait_ge(s["ln_var"], 2 * b - 1)
                load_batch(b)
                sp.wait_ge(s["wq_ready1"], b)
                load_weights(b)
                sp.wait_ge(s["wq_ready2"], b)
                load_down(b)

            sp.wait_ge(s["zero_ready"], 1)
            sp.wait_ge(s["tables_ready"], 1)
            with sp.Fori(0, NE, 1) as e:
                row = sp.value_load(tab_pad[0:1, bass.ds(e, 1)], min_val=0,
                                    max_val=NE * REGION - P)
                sp.dma_start(dispatched[bass.ds(row, P), :], zero_rows[:, :]).then_inc(
                    s["pads_written"], 16)
            sp.wait_ge(s["pads_written"], 16 * NE)
            sp.wait_ge(s["scattered"], 16 * SCATTERS * B)

            def load_tile(t, k):
                row = sp.value_load(tab_row[0:1, bass.ds(t, 1)], min_val=0,
                                    max_val=NE * REGION - P)
                sp.dma_start(x_in[k][:, :], dispatched[bass.ds(row, P), :]).then_inc(tile_in[k], 16)

            def store_tile(t, k):
                sp.dma_start(expert_out[bass.ds(t * P, P), :], y_out[k][:, :]).then_inc(
                    y_stored[k], 16)

            load_tile(0, 0)
            load_tile(1, 1)
            for t in range(2, 4):
                sp.wait_ge(s["xr_t"], t - 1)
                load_tile(t, t % 2)
            with sp.Fori(0, TILES - 5, 2) as t:
                for k in range(2):
                    sp.wait_ge(s["xr_t"], t + (k + 3))
                    load_tile(t + (k + 4), k)
                    sp.wait_ge(s["d_y_e"], t + (k + 1))
                    store_tile(t + k, k)
            for t in range(2 * len(range(0, TILES - 5, 2)), TILES):
                if t + 4 < TILES:
                    sp.wait_ge(s["xr_t"], t + 3)
                    load_tile(t + 4, t % 2)
                sp.wait_ge(s["d_y_e"], t + 1)
                store_tile(t, t % 2)

            for t in range(TT):
                sp.wait_ge(s["out_ready"], t + 1)
                sp.dma_start(out_rows[t], acc_tile(t)).then_inc(s["out_stored"], 16)
            sp.wait_ge(s["out_stored"], 16 * TT)

        @block.gpsimd
        def _(pool):
            g = nc.gpsimd
            own = [0]

            def done(ins):
                own[0] += 1
                ins.then_inc(s["pool_chain"], 1)

            def fence():
                pool.wait_ge(s["pool_chain"], own[0])

            def wait_alone():
                pool.nop(nofuse=True)

            done(g.memset(ident[:, :], 0.0))
            done(g.memset(ident_b[:, :], 0.0))
            done(g.memset(before_b[:, :], 1.0))
            done(g.memset(ones_b[:, :], 1.0))
            done(g.memset(one_e[:, :], 1.0))
            done(g.memset(eps_ln[:, :], LN_EPS))
            done(g.memset(raw2[:, 0:2, :], 0.0))
            fence()
            done(g.affine_select(out=ident[:, :], in_=ident[:, :], compare_op=ALU.not_equal,
                                 fill=1.0, base=0, pattern=[[-1, P]], channel_multiplier=1))
            done(g.affine_select(out=ident_b[:, :], in_=ident_b[:, :], compare_op=ALU.not_equal,
                                 fill=1.0, base=0, pattern=[[-1, P]], channel_multiplier=1))
            done(g.affine_select(out=before_b[:, :], in_=before_b[:, :], compare_op=ALU.is_gt,
                                 fill=0.0, base=0, pattern=[[1, P]], channel_multiplier=-1))
            done(g.iota(iota_e[:, :], [[1, NE]], base=0, channel_multiplier=0,
                        allow_small_or_imprecise_dtypes=True))
            done(g.iota(region_start[:, :], [[REGION, NE]], base=0, channel_multiplier=0,
                        allow_small_or_imprecise_dtypes=True))
            fence()
            g.iota(next_row[:, :], [[REGION, NE]], base=0, channel_multiplier=0,
                   allow_small_or_imprecise_dtypes=True).then_inc(s["consts"], 1)

            def load_expert(w1, w3, w2):
                pool.dma_start(raw13[:, :, 0, :], w1.rearrange("(c p) h -> p c h", p=P)).then_inc(
                    s["raw13_in"], 16)
                pool.dma_start(raw13[:, :, 1, :], w3.rearrange("(c p) h -> p c h", p=P)).then_inc(
                    s["raw13_in"], 16)
                pool.dma_start(raw2[0:HSTEP, 0:2, :], w2[0:2 * HSTEP, :].rearrange(
                    "(c p) n -> p c n", c=2)).then_inc(s["raw2_in"], 16)
                pool.dma_start(raw2[:, 2, :], w2[2 * HSTEP:H, :]).then_inc(s["raw2_in"], 16)

            def load_routed(e):
                w1, w3, w2 = (w[bass.ds(e, 1)].rearrange("a d h -> (a d) h")
                              for w in (w1_routed, w3_routed, w2_routed))
                load_expert(w1, w3, w2)

            def split_expert(n, slot):
                parts = (
                    (raw13[:, :, :, :].rearrange("p c m h -> p (c m h)"), ring13_hi, ring13_lo,
                     slot * W13, W13, "raw13_in", 32, "hi13_in"),
                    (raw2[:, :, :].rearrange("p c n -> p (c n)"), ring2_hi, ring2_lo,
                     slot * W2, W2, "raw2_in", 32, "hi2_in"),
                )
                for raw, hi, lo, at, size, loaded, parts_in, rounded in parts:
                    pool.wait_ge(s[loaded], parts_in * (n + 1))
                    wait_alone()
                    pool.dma_start(hi[:, at:at + size], raw).then_inc(s[rounded], 16)
                for raw, hi, lo, at, size, loaded, parts_in, rounded in parts:
                    pool.wait_ge(s[rounded], 16 * n + 16)
                    g.tensor_tensor(lo[:, at:at + size], raw, hi[:, at:at + size].bitcast(F32),
                                    ALU.subtract).then_inc(s["weights_ready"], 1)
                pool.wait_ge(s["weights_ready"], SPLITS * n + SPLITS)

            load_expert(w1_shared, w3_shared, w2_shared)

            def scatter_batch(b):
                pool.wait_ge(s["rows_ready"], b + 1)
                wait_alone()
                for j in range(SCATTERS):
                    g.indirect_dma_start(
                        out=dispatched, out_offset=bass.IndirectOffsetOnAxis(
                            ap=row_u[:, j:j + 1], axis=0),
                        in_=hid[:, j // TOPK, :], in_offset=None).then_inc(s["scattered"], 16)

            split_expert(0, 0)
            load_routed(0)
            split_expert(1, 1)
            load_routed(1)
            with pool.Fori(0, B, 1) as b:
                scatter_batch(b)

            pool.wait_ge(s["scattered"], 16 * SCATTERS * B)
            g.memset(zero_rows[:, :], 0.0).then_inc(s["zero_ready"], 1)
            g.iota(iota_t[0:1, :], [[1, TILES]], base=0, channel_multiplier=0,
                   allow_small_or_imprecise_dtypes=True).then_inc(s["zero_ready"], 1)

            pool.wait_ge(s["sh_y"], TT)
            split_expert(2, 0)
            load_routed(2)
            pool.wait_ge(s["tables_ready"], 1)

            def refill(n, slot):
                first = pool.value_load(tab_start[0:1, bass.ds(n - 2, 1)], min_val=0,
                                        max_val=TILES)
                pool.wait_ge(s["d_y"], first)
                split_expert(n, slot)

            with pool.Fori(3, NE - 1, 2) as n:
                refill(n, 1)
                load_routed(n)
                refill(n + 1, 0)
                load_routed(n + 1)
            refill(NE - 1, 1)
            load_routed(NE - 1)
            refill(NE, 0)

            pool.wait_ge(s["out_rows_known"], 1)
            for k in range(2):
                pool.wait_ge(y_stored[k], 16 * ((TILES + 1 - k) // 2))
            for t in range(TT):
                if t >= G_BUFS:
                    pool.wait_ge(s["out_ready"], t - G_BUFS + 1)
                for k in range(TOPK):
                    j = t * TOPK + k
                    g.indirect_dma_start(
                        out=rows_of_4[t % G_BUFS][:, k, :], out_offset=None, in_=expert_out,
                        in_offset=bass.IndirectOffsetOnAxis(ap=out_row[:, j:j + 1], axis=0)
                    ).then_inc(gathered_s[t % G_BUFS], 16)

        @block.tensor
        def _(pe):
            mm, transpose = nc.tensor.matmul, nc.tensor.transpose

            pe.wait_ge(s["consts"], 1)
            pe.wait_ge(s["gate_rows_in"], 16)
            for c in range(KC):
                last = transpose(bank[0][:, c * NE:(c + 1) * NE],
                                 gate_rows[:, c * P:(c + 1) * P], ident[0:NE, 0:NE])
            last.then_inc(s["gate_t"], 1)

            def hidden(x_hi, x_lo, slot_at, into1, into3, chunks=range(KC)):
                outs = (into1[:, 0:H], into3[:, 0:H])
                for c in chunks:
                    for half, w, stop in ((x_hi, ring13_hi, False), (x_hi, ring13_lo, False),
                                          (x_lo, ring13_hi, True)):
                        for m in range(2):
                            last = mm(outs[m], half[:, c * P:(c + 1) * P],
                                      ring13(w, slot_at, c, m),
                                      start=(c == 0 and half is x_hi and w is ring13_hi),
                                      stop=(c == KC - 1 and stop))
                return last

            def hidden_t(act, into):
                for c, (at, size) in enumerate(HC):
                    last = transpose(into[0:size, c * P:(c + 1) * P], act[:, at:at + size],
                                     ident[:, :])
                return last

            def project(h_hi, h_lo, slot_at, into):
                n = 0
                for c, (_, size) in enumerate(HC):
                    for half, w in ((h_hi, ring2_hi), (h_hi, ring2_lo), (h_lo, ring2_hi)):
                        last = mm(into[:, :], half[0:size, c * P:(c + 1) * P],
                                  ring2(w, slot_at, c), start=(n == 0), stop=(n == 8))
                        n += 1
                return last

            def rows_t(tile, into, c, w):
                for r in range(ROWS):
                    last = transpose(into[:, r * P:(r + 1) * P], tile[:, r, c * P:(c + 1) * P],
                                     ident[:, :])
                return last

            def spread(into, column, chunks):
                for c in range(chunks):
                    last = transpose(into[:, c * P:(c + 1) * P],
                                     column[:, c:c + 1].to_broadcast([P, P]), ident[:, :])
                return last

            def c1(t, r):
                if r or not isinstance(t, int) or t:
                    pe.wait_ge(s["sh_prod"], t)
                pe.wait_ge(s["xn2_lo"], t + 1)
                hidden(xt_hi[:, r, :], xt_lo[:, r, :], 0, bank[4], bank[5]).then_inc(s["sh_h"], 1)

            def c2(t, r):
                pe.wait_ge(s["sh_prod"], t + 1)
                if r or not isinstance(t, int) or t:
                    pe.wait_ge(s["sh_lo"], t)
                hidden_t(h3[r % 2], bank[6]).then_inc(s["sh_t"], 1)

            def c3(t, r):
                pe.wait_ge(s["sh_lo"], t + 1)
                if r or not isinstance(t, int) or t:
                    pe.wait_ge(s["sh_y_e"], t)
                project(ht_hi[r % 2], ht_lo[r % 2], 0, bank[7]).then_inc(s["sh_y"], 1)

            def smoothing(b, L):
                pe.wait_ge(s[f"smooth{L}"], b + 1)
                for j in (1, 0):
                    spread(bank[2 + j], smooth[L][:, j, :], LINEARS[L]).then_inc(s[f"bc{L}"], 1)

            def quantised_t(b, L):
                pairs = LINEARS[L] // 2
                n = 0
                for q, ready, t_done, t_read in (
                        (wq, f"wq_ready{L}", f"wq_t{L}", f"wq_e{L}"),
                        (xq, f"xq_ready{L}", f"xq_t{L}", f"xq_e{L}")):
                    pe.wait_ge(s[ready], b + 1)
                    for j in range(pairs):
                        into = bank[2 + n % 2][:, :].bitcast(BF16)
                        if q is xq and pairs == 2:
                            pe.wait_ge(s[f"wq_e{L}"], 2 * b + j + 1)
                        for i in range(2):
                            for r in range(ROWS):
                                at = (2 * j + i) * P
                                last = transpose(into[:, (i * ROWS + r) * P:(i * ROWS + r + 1) * P],
                                                 q[:, r, at:at + P], ident_b[:, :])
                        last.then_inc(s[t_done], 1)
                        n += 1

            def quantised_mm(b, L):
                pairs = LINEARS[L] // 2
                pe.wait_ge(s[f"xq_e{L}" if pairs == 2 else f"wq_e{L}"], pairs * b + 1)
                spread(bank[2], q_scale[:, 1, :], ROWS).then_inc(s[f"wsc{L}"], 1)
                for r in range(ROWS):
                    if r == 0:
                        pe.wait_ge(s[f"xq_e{L}"], pairs * b + pairs)
                        pe.wait_ge(s[f"wq_e{L}"], pairs * b + pairs)
                    elif r == 1:
                        pe.wait_ge(s[f"wsc_e{L}"], b + 1)
                    else:
                        pe.wait_ge(s[f"mm_e{L}"], ROWS * b + r - 1)
                    for c in range(LINEARS[L]):
                        last = mm(bank[3 - r % 2][:, :], xq_t[:, c, r * P:(r + 1) * P],
                                  wq_t[:, c, :], start=(c == 0), stop=(c == LINEARS[L] - 1))
                    last.then_inc(s[f"mm{L}"], 1)

            def batch(b, shared):
                t0 = (b - 1) * ROWS
                tiles = [lambda f, r=r: f(t0 + r, r) if shared else None for r in range(ROWS)]
                pe.wait_ge(s["wa1_loaded"], 16 * b + 16)
                for c in range(KC):
                    if c < 2 and shared:
                        pe.wait_ge(s["xn2_lo"], ROWS * b + c - 1)
                    elif c < 2:
                        if c == 0:
                            pe.wait_ge(s["gate_lo_ready"], 1)
                    else:
                        pe.wait_ge(s["w_max1"], KC * b + c - 1)
                    rows_t(wa1, bank[c % 2], c, D).then_inc(s["w_t1"], 1)
                pe.wait_ge(s["wa2_loaded"], 16 * b + 16)
                for c in range(2):
                    pe.wait_ge(s["w_max1"], KC * b + c + 3)
                    rows_t(wa2, bank[c % 2], c, I).then_inc(s["w_t2"], 1)
                tiles[0](c1)
                pe.wait_ge(s["xn_ready"], 4 * b + 4)
                for c in range(KC):
                    if c < 2:
                        pe.wait_ge(s["w_max2"], 2 * b + c + 1)
                    else:
                        pe.wait_ge(s["x_max1"], KC * b + c - 1)
                    rows_t(xa1, bank[c % 2], c, D).then_inc(s["x_t1"], 1)
                smoothing(b, 1)
                tiles[1](c1)
                tiles[0](c2)
                quantised_t(b, 1)
                tiles[1](c2)
                tiles[0](c3)
                quantised_mm(b, 1)
                tiles[2](c1)
                tiles[1](c3)
                pe.wait_ge(s["a_ready"], b + 1)
                for c in range(2):
                    pe.wait_ge(s["x_max1"], KC * b + c + 3)
                    rows_t(xa2, bank[c % 2], c, I).then_inc(s["x_t2"], 1)
                smoothing(b, 2)
                tiles[3](c1)
                tiles[2](c2)
                quantised_t(b, 2)
                quantised_mm(b, 2)
                tiles[3](c2)
                tiles[2](c3)
                for r in range(ROWS):
                    pe.wait_ge(s["xn2_ready"], ROWS * b + r + 1)
                    if r < 2:
                        pe.wait_ge(s["x_max2"], 2 * b + r + 1)
                    else:
                        pe.wait_ge(s["xn2_lo"], ROWS * b + r - 1)
                    for c in range(KC):
                        last = transpose(bank[r % 2][:, c * P:(c + 1) * P],
                                         hid[:, r, c * P:(c + 1) * P], ident[:, :])
                    last.then_inc(s["xn2_t"], 1)
                tiles[3](c3)
                for r in range(ROWS):
                    pe.wait_ge(s["xn2_lo"], ROWS * b + r + 1)
                    n = 0
                    for c in range(KC):
                        for xh, gh in ((xt_hi, gate_hi), (xt_hi, gate_lo), (xt_lo, gate_hi)):
                            last = mm(bank[2][:, r * NE:(r + 1) * NE],
                                      xh[:, r, c * P:(c + 1) * P], gh[:, c, :],
                                      start=(n == 0), stop=(n == 3 * KC - 1))
                            n += 1
                last.then_inc(s["logits"], 1)
                pe.wait_ge(s["taken_ready"], b + 1)
                for r in range(ROWS + 1):
                    into = bank[3][:, r * NE:(r + 1) * NE]
                    for q in range(min(r + 1, ROWS)):
                        last = mm(into, (before_b if q == r else ones_b)[:, :],
                                  taken[:, q * NE:(q + 1) * NE], start=(q == 0),
                                  stop=(q == min(r, ROWS - 1)))
                last.then_inc(s["prefix"], 1)

            batch(0, False)
            pe.wait_ge(s["weights_ready"], SPLITS)
            with pe.Fori(1, B, 1) as b:
                batch(b, True)
            t0 = (B - 1) * ROWS
            c1(t0, 0)
            for r in range(1, ROWS):
                c1(t0 + r, r)
                c2(t0 + r - 1, r - 1)
                if r > 1:
                    c3(t0 + r - 2, r - 2)
            c2(t0 + 3, 3)
            c3(t0 + 2, 2)
            c3(t0 + 3, 3)

            pe.wait_ge(s["tables_ready"], 1)
            hbank = [(bank[4], bank[5]), (bank[0], bank[1])]

            def load_t(t, k):
                pe.wait_ge(tile_in[k], 16 * (t // 2 + 1) if isinstance(t, int) else t * 8 + 16 - 8 * k)
                for c in range(KC):
                    last = transpose(bank[2 + k][:, c * P:(c + 1) * P],
                                     x_in[k][:, c * P:(c + 1) * P], ident[:, :])
                last.then_inc(s["xr_t"], 1)

            def tile_step(t, k):
                fixed = isinstance(t, int)
                slot_at = None
                if not fixed or t < TILES:
                    splits = pe.value_load(tab_splits[0:1, bass.ds(t, 1)], min_val=0,
                                           max_val=SPLITS * (NE + 1))
                    slot_at = pe.value_load(tab_slot[0:1, bass.ds(t, 1)], min_val=0,
                                            max_val=1) * W13
                    pe.wait_ge(s["weights_ready"], splits)
                    pe.wait_ge(s["xr_lo_s"], t + 1)
                    if not fixed or t >= 2:
                        pe.wait_ge(s["d_prod"], t - 1)
                    hidden(xr_hi[k], xr_lo[k], slot_at, *hbank[k], chunks=range(KC // 2))
                if not fixed or t >= 1:
                    pe.wait_ge(s["d_act"], t)
                    if not fixed or t >= 2:
                        pe.wait_ge(s["d_lo"], t - 1)
                    hidden_t(h3[1 - k], bank[6]).then_inc(s["d_t"], 1)
                if not fixed or t < TILES:
                    hidden(xr_hi[k], xr_lo[k], slot_at, *hbank[k],
                           chunks=range(KC // 2, KC)).then_inc(s["d_h"], 1)
                if not fixed or t + 1 < TILES:
                    load_t(t + 1, 1 - k)
                if not fixed or t >= 1:
                    slot = pe.value_load(tab_slot[0:1, bass.ds(t - 1, 1)], min_val=0, max_val=1)
                    pe.wait_ge(s["d_lo"], t)
                    if not fixed or t >= 2:
                        pe.wait_ge(s["d_y_e"], t - 1)
                    project(ht_hi[1 - k], ht_lo[1 - k], slot * W2, bank[7]).then_inc(s["d_y"], 1)

            load_t(0, 0)
            for t in range(3):
                tile_step(t, t % 2)
            with pe.Fori(3, TILES - 2, 2) as t:
                tile_step(t, 1)
                tile_step(t + 1, 0)
            for t in range(3 + 2 * len(range(3, TILES - 2, 2)), TILES + 1):
                tile_step(t, t % 2)

        @block.scalar
        def _(act):
            def copy(out, in_):
                return nc.scalar.activation(out, in_, ACT.Copy)

            act.wait_ge(s["gates_in"], 48)
            nc.scalar.activation(gates[:, :], gates[:, :], ACT.Tanh).then_inc(s["gates_ready"], 1)
            act.wait_ge(s["gate_t"], 1)
            copy(gate_hi[:, :, :].rearrange("p c e -> p (c e)"), bank[0][:, 0:KC * NE]).then_inc(
                s["gate_hi_ready"], 1)

            def norm(b, n):
                act.wait_ge(s["ln_var"], 2 * b + n + 1)
                nc.scalar.activation(std[:, :], mean_var[:, :, 1], ACT.Sqrt,
                                     bias=eps_ln[:, :]).then_inc(s["ln_std"], 1)

            def smooth_root(b, L):
                act.wait_ge(s[f"ratio{L}"], b + 1)
                nc.scalar.activation(ratio[L][:, :], ratio[L][:, :], ACT.Sqrt).then_inc(
                    s[f"s_raw{L}"], 1)

            def over_scales(b, L):
                k = {1: D, 2: I}[L]
                act.wait_ge(s[f"scales{L}"], b + 1)
                for w, t, ready in ((1, {1: wa1, 2: wa2}[L], f"wt{L}"),
                                    (0, {1: xa1, 2: xa2}[L], f"xs{L}")):
                    for r in range(ROWS):
                        last = nc.scalar.activation(t[:, r, 0:k], t[:, r, 0:k], ACT.Copy,
                                                    scale=q_inv[:, w, r:r + 1])
                    last.then_inc(s[ready], 1)

            def quantised_copies(b, L):
                pairs = LINEARS[L] // 2
                n = 0
                for dst, t_done, t_read in ((wq_t, f"wq_t{L}", f"wq_e{L}"),
                                            (xq_t, f"xq_t{L}", f"xq_e{L}")):
                    for j in range(pairs):
                        act.wait_ge(s[t_done], pairs * b + j + 1)
                        copy(dst[:, 2 * j:2 * j + 2, :].rearrange("p c t -> p (c t)"),
                             bank[2 + n % 2][:, :].bitcast(BF16)).then_inc(s[t_read], 1)
                        n += 1
                act.wait_ge(s[f"wsc{L}"], b + 1)
                copy(wscale_b[:, :], bank[2][:, :]).then_inc(s[f"wsc_e{L}"], 1)

            def sh_silu(t, r):
                act.wait_ge(s["sh_h"], t + 1)
                nc.scalar.activation(h1[r % 2][:, :], bank[4][:, 0:H], ACT.Silu).then_inc(
                    s["sh_h1"], 1)

            def a_t(t, r):
                act.wait_ge(s["sh_t"], t + 1)
                copy(ht_hi[r % 2][:, :], bank[6][:, 0:len(HC) * P]).then_inc(s["sh_hi"], 1)

            def batch(b, shared):
                t0 = (b - 1) * ROWS
                tiles = [lambda f, r=r: f(t0 + r, r) if shared else None for r in range(ROWS)]
                norm(b, 0)
                tiles[0](sh_silu)
                smooth_root(b, 1)
                tiles[1](sh_silu)
                tiles[0](a_t)
                over_scales(b, 1)
                quantised_copies(b, 1)
                tiles[1](a_t)
                act.wait_ge(s["mm_e1"], ROWS * b + ROWS)
                nc.scalar.activation(hid[:, :, 0:I], hid[:, :, 0:I], ACT.Silu).then_inc(
                    s["silu_gate"], 1)
                tiles[2](sh_silu)
                smooth_root(b, 2)
                tiles[3](sh_silu)
                tiles[2](a_t)
                over_scales(b, 2)
                quantised_copies(b, 2)
                tiles[3](a_t)
                norm(b, 1)
                for r in range(ROWS):
                    act.wait_ge(s["xn2_t"], ROWS * b + r + 1)
                    if shared:
                        act.wait_ge(s["sh_h"], ROWS * (b - 1) + r + 1)
                    copy(xt_hi[:, r, :], bank[r % 2][:, :]).then_inc(s["xn2_hi"], 1)
                act.wait_ge(s["logits"], b + 1)
                nc.scalar.activation(score[:, :], bank[2][:, 0:ROWS * NE], ACT.Exp,
                                     scale=-1.0).then_inc(s["exp_ready"], 1)

            batch(0, False)
            with act.Fori(1, B, 1) as b:
                batch(b, True)
            t0 = (B - 1) * ROWS
            sh_silu(t0, 0)
            for r in range(1, ROWS):
                sh_silu(t0 + r, r)
                a_t(t0 + r - 1, r - 1)
            a_t(t0 + 3, 3)

            def tile_step(t, k):
                fixed = isinstance(t, int)
                if not fixed or t >= 1:
                    act.wait_ge(s["d_t"], t)
                    copy(ht_hi[1 - k][:, :], bank[6][:, 0:len(HC) * P]).then_inc(s["d_hi"], 1)
                if not fixed or t < TILES:
                    act.wait_ge(s["d_h"], t + 1)
                    copy(h1[k][:, :], [bank[4], bank[0]][k][:, 0:H]).then_inc(s["d_h1"], 1)
                if not fixed or t + 1 < TILES:
                    act.wait_ge(s["xr_t"], t + 2)
                    copy(xr_hi[1 - k][:, :], bank[3 - k][:, :]).then_inc(s["xr_hi_s"], 1)
                if not fixed or t < TILES:
                    act.wait_ge(s["d_prod"], t + 1)
                    nc.scalar.activation(h3[k][:, :], h1[k][:, :], ACT.Silu).then_inc(
                        s["d_act"], 1)

            act.wait_ge(s["xr_t"], 1)
            act.wait_ge(s["tables_ready"], 1)
            copy(xr_hi[0][:, :], bank[2][:, :]).then_inc(s["xr_hi_s"], 1)
            for t in range(3):
                tile_step(t, t % 2)
            with act.Fori(3, TILES - 2, 2) as t:
                tile_step(t, 1)
                tile_step(t + 1, 0)
            for t in range(3 + 2 * len(range(3, TILES - 2, 2)), TILES + 1):
                tile_step(t, t % 2)

        @block.vector
        def _(dve):
            v = nc.vector
            chain = {"at": 0, "n": 0}

            def step(ins):
                chain["n"] += 1
                ins.then_inc(s["dve_chain"], 1)

            def settle():
                dve.wait_ge(s["dve_chain"], chain["at"] + chain["n"])

            def link(ins):
                step(ins)
                settle()

            def wait_alone():
                dve.nop(nofuse=True)

            dve.wait_ge(s["gate_hi_ready"], 1)
            v.tensor_tensor(gate_lo[:, :, :].rearrange("p c e -> p (c e)"), bank[0][:, 0:KC * NE],
                            gate_hi[:, :, :].rearrange("p c e -> p (c e)").bitcast(F32),
                            ALU.subtract).then_inc(s["gate_lo_ready"], 1)
            link(v.memset(bank[6][:, 0:3 * P], 0.0))

            def norm(b, n, dst, ready):
                for r in range(ROWS):
                    last = v.bn_stats(stats[:, r, :], acc_tile(b * ROWS + r))
                link(last)
                wait_alone()
                for r in range(ROWS):
                    last = v.bn_aggr(mean_var[:, r, :], stats[:, r, :])
                last.then_inc(s["ln_var"], 1)
                dve.wait_ge(s["ln_std"], 2 * b + n + 1)
                link(v.reciprocal(rstd[:, :], std[:, :]))
                for r in range(ROWS):
                    v.tensor_scalar(dst[:, r, :], acc_tile(b * ROWS + r), mean_var[:, r, 0:1],
                                    rstd[:, r:r + 1], ALU.subtract, ALU.mult).then_inc(s[ready], 1)

            def column_max(b, which, L):
                for c in range(LINEARS[L]):
                    dve.wait_ge(s[f"{which}_t{L}"], LINEARS[L] * b + c + 1)
                    j = {"x": 0, "w": 1}[which]
                    v.tensor_reduce(amax[L][:, j, c:c + 1], bank[c % 2][:, :], AX.X, ALU.max,
                                    apply_absolute_value=True).then_inc(s[f"{which}_max{L}"], 1)

            def smoothing(b, L):
                dve.wait_ge(s[f"w_max{L}"], LINEARS[L] * (b + 1))
                dve.wait_ge(s[f"x_max{L}"], LINEARS[L] * (b + 1))
                link(v.tensor_scalar(amax[L][:, :, :], amax[L][:, :, :], Q_EPS, None, ALU.max))
                link(v.reciprocal(amax[L][:, 1, :], amax[L][:, 1, :]))
                v.tensor_tensor(ratio[L][:, :], amax[L][:, 0, :], amax[L][:, 1, :],
                                ALU.mult).then_inc(s[f"ratio{L}"], 1)
                dve.wait_ge(s[f"s_raw{L}"], b + 1)
                link(v.tensor_scalar(smooth[L][:, 0, :], ratio[L][:, :], Q_EPS, None, ALU.max))
                v.reciprocal(smooth[L][:, 1, :], smooth[L][:, 0, :]).then_inc(s[f"smooth{L}"], 1)

            def smooth_and_scale(b, L):
                k = {1: D, 2: I}[L]
                xt, wt = {1: (xa1, wa1), 2: (xa2, wa2)}[L]
                dve.wait_ge(s[f"bc{L}"], 2 * b + 2)
                step(v.tensor_tensor(wt[:, :, :], wt[:, :, :],
                                     bank[2][:, 0:k].unsqueeze(1).to_broadcast([P, ROWS, k]),
                                     ALU.mult))
                link(v.tensor_tensor(xt[:, :, :], xt[:, :, :],
                                     bank[3][:, 0:k].unsqueeze(1).to_broadcast([P, ROWS, k]),
                                     ALU.mult))
                step(v.tensor_reduce(row_max[:, 1, :], wt[:, :, :], AX.X, ALU.max,
                                     apply_absolute_value=True))
                link(v.tensor_reduce(row_max[:, 0, :], xt[:, :, :], AX.X, ALU.max,
                                     apply_absolute_value=True))
                link(v.tensor_scalar(q_scale[:, :, :], row_max[:, :, :], Q_EPS, 1.0 / QMAX,
                                     ALU.max, ALU.mult))
                v.reciprocal(q_inv[:, :, :], q_scale[:, :, :]).then_inc(s[f"scales{L}"], 1)

            def quantise(b, L):
                k = {1: D, 2: I}[L]
                for t, q, scaled, ready in (({1: wa1, 2: wa2}[L], wq, f"wt{L}", f"wq_ready{L}"),
                                            ({1: xa1, 2: xa2}[L], xq, f"xs{L}", f"xq_ready{L}")):
                    dve.wait_ge(s[scaled], b + 1)
                    link(v.tensor_scalar(t[:, :, :], t[:, :, :], -QMAX, ROUND, ALU.max, ALU.add))
                    v.tensor_scalar(q[:, :, 0:k], t[:, :, :], ROUND, QMAX, ALU.subtract,
                                    ALU.min).then_inc(s[ready], 1)

            def sh_product(t, r):
                dve.wait_ge(s["sh_h1"], t + 1)
                v.tensor_tensor(h3[r % 2][:, :], h1[r % 2][:, :], bank[5][:, 0:H],
                                ALU.mult).then_inc(s["sh_prod"], 1)

            def sh_low(t, r):
                dve.wait_ge(s["sh_hi"], t + 1)
                v.tensor_tensor(ht_lo[r % 2][:, :], bank[6][:, 0:len(HC) * P],
                                ht_hi[r % 2][:, :].bitcast(F32), ALU.subtract).then_inc(
                                    s["sh_lo"], 1)

            def sh_add(t, r):
                dve.wait_ge(s["sh_y"], t + 1)
                v.scalar_tensor_tensor(acc_tile(t), bank[7][:, :], gates[:, 1:2], acc_tile(t),
                                       ALU.mult, ALU.add).then_inc(s["sh_y_e"], 1)

            def route(b):
                dve.wait_ge(s["exp_ready"], b + 1)
                by_expert = score[:, :].rearrange("p (r e) -> p r e", r=ROWS)
                link(v.tensor_scalar(score[:, :], score[:, :], 1.0, None, ALU.add))
                link(v.reciprocal(score[:, :], score[:, :]))
                link(v.tensor_tensor(by_expert, by_expert,
                                     bias_e[:, :].unsqueeze(1).to_broadcast([P, ROWS, NE]),
                                     ALU.add))
                wait_alone()
                for r in range(ROWS):
                    step(v.max(top8[:, r, :], by_expert[:, r, :]))
                settle()
                wait_alone()
                for r in range(ROWS):
                    step(v.max_index(top8_at[:, r, :], top8[:, r, :], by_expert[:, r, :]))
                settle()
                link(v.tensor_copy(top_at[:, :].rearrange("p (r k) -> p r k", r=ROWS),
                                   top8_at[:, :, 0:TOPK]))
                link(v.tensor_tensor(
                    onehot[:, :].rearrange("p (j e) -> p j e", e=NE),
                    iota_e[:, :].unsqueeze(1).to_broadcast([P, ROWS * TOPK, NE]),
                    top_at[:, :].unsqueeze(2).to_broadcast([P, ROWS * TOPK, NE]),
                    ALU.is_equal))
                with nc.allow_low_precision("zeros and ones"):
                    v.tensor_reduce(
                        taken[:, :].rearrange("p (r e) -> p r e", r=ROWS),
                        onehot[:, :].rearrange("p (r k e) -> p r e k", r=ROWS, k=TOPK),
                        AX.X, ALU.add).then_inc(s["taken_ready"], 1)
                step(v.tensor_copy(onehot_all[:, bass.ds(b * BE, BE)], onehot[:, :]))
                link(v.tensor_reduce(total4[:, :], top8[:, :, 0:TOPK], AX.X, ALU.add))
                link(v.reciprocal(total4[:, :], total4[:, :]))
                link(v.tensor_tensor(weight[:, :].rearrange("p (r k) -> p r k", r=ROWS),
                                     top8[:, :, 0:TOPK],
                                     total4[:, :].unsqueeze(2).to_broadcast([P, ROWS, TOPK]),
                                     ALU.mult))
                step(v.tensor_scalar(weight_all[:, bass.ds(b * ROWS * TOPK, ROWS * TOPK)],
                                     weight[:, :], gates[:, 1:2], None, ALU.mult))
                dve.wait_ge(s["prefix"], b + 1)
                link(v.tensor_tensor(pos[:, :].rearrange("p (r e) -> p r e", r=ROWS),
                                     bank[3][:, 0:ROWS * NE].rearrange("p (r e) -> p r e", r=ROWS),
                                     next_row[:, :].unsqueeze(1).to_broadcast([P, ROWS, NE]),
                                     ALU.add))
                step(v.tensor_tensor(next_row[:, :], next_row[:, :],
                                     bank[3][:, ROWS * NE:(ROWS + 1) * NE], ALU.add))
                for r in range(ROWS):
                    at = r * TOPK * NE
                    step(v.tensor_tensor(
                        picked[:, at:at + TOPK * NE].rearrange("p (k e) -> p k e", k=TOPK),
                        onehot[:, at:at + TOPK * NE].rearrange("p (k e) -> p k e", k=TOPK),
                        pos[:, r * NE:(r + 1) * NE].unsqueeze(1).to_broadcast([P, TOPK, NE]),
                        ALU.mult))
                settle()
                link(v.tensor_reduce(row_f[:, :],
                                     picked[:, :].rearrange("p (j e) -> p j e", e=NE),
                                     AX.X, ALU.add))
                v.tensor_copy(row_u[:, :], row_f[:, :]).then_inc(s["rows_ready"], 1)
                link(v.tensor_copy(row_all[:, bass.ds(b * ROWS * TOPK, ROWS * TOPK)],
                                   row_f[:, :]))

            def batch(b, shared):
                t0 = (b - 1) * ROWS
                tiles = [lambda f, r=r: f(t0 + r, r) if shared else None for r in range(ROWS)]
                dve.wait_ge(s["x_loaded"], 16 * b + 16)
                norm(b, 0, xa1, "xn_ready")
                column_max(b, "w", 1)
                column_max(b, "w", 2)
                tiles[0](sh_product)
                column_max(b, "x", 1)
                smoothing(b, 1)
                smooth_and_scale(b, 1)
                tiles[1](sh_product)
                tiles[0](sh_low)
                quantise(b, 1)
                tiles[1](sh_low)
                tiles[0](sh_add)
                if shared:
                    dve.wait_ge(s["scattered"], 16 * SCATTERS * b)
                dve.wait_ge(s["wsc_e1"], b + 1)
                for r in range(ROWS):
                    dve.wait_ge(s["mm1"], ROWS * b + r + 1)
                    v.scalar_tensor_tensor(hid[:, r, :], bank[3 - r % 2][:, :],
                                           q_scale[:, 0, r:r + 1], wscale_b[:, :], ALU.mult,
                                           ALU.mult).then_inc(s["mm_e1"], 1)
                tiles[2](sh_product)
                tiles[1](sh_add)
                dve.wait_ge(s["silu_gate"], b + 1)
                v.tensor_tensor(xa2[:, :, :], hid[:, :, 0:I], hid[:, :, I:2 * I],
                                ALU.mult).then_inc(s["a_ready"], 1)
                column_max(b, "x", 2)
                smoothing(b, 2)
                smooth_and_scale(b, 2)
                tiles[3](sh_product)
                tiles[2](sh_low)
                quantise(b, 2)
                dve.wait_ge(s["wsc_e2"], b + 1)
                for r in range(ROWS):
                    dve.wait_ge(s["mm2"], ROWS * b + r + 1)
                    v.scalar_tensor_tensor(lin2_out[:, r % 2, :], bank[3 - r % 2][:, :],
                                           q_scale[:, 0, r:r + 1], wscale_b[:, :], ALU.mult,
                                           ALU.mult).then_inc(s["mm_e2"], 1)
                    dve.wait_ge(s["mm_e2"], ROWS * b + r + 1)
                    step(v.scalar_tensor_tensor(acc_tile(b * ROWS + r), lin2_out[:, r % 2, :],
                                                gates[:, 0:1], acc_tile(b * ROWS + r), ALU.mult,
                                                ALU.add))
                settle()
                tiles[3](sh_low)
                tiles[2](sh_add)
                norm(b, 1, hid, "xn2_ready")
                for r in range(ROWS):
                    dve.wait_ge(s["xn2_hi"], ROWS * b + r + 1)
                    v.tensor_tensor(xt_lo[:, r, :], bank[r % 2][:, :],
                                    xt_hi[:, r, :].bitcast(F32), ALU.subtract).then_inc(
                                        s["xn2_lo"], 1)
                tiles[3](sh_add)
                route(b)

            dve.wait_ge(s["gates_ready"], 1)
            dve.wait_ge(s["consts"], 1)
            chain["at"] = chain["n"]
            chain["n"] = 0
            batch(0, False)
            per_batch, start = chain["n"], chain["at"]
            chain["n"] = 0
            with dve.Fori(1, B, 1) as b:
                chain["at"] = start + b * per_batch
                batch(b, True)
                assert chain["n"] == per_batch
            chain["at"], chain["n"] = start + B * per_batch, 0

            dve.wait_ge(s["zero_ready"], 2)
            link(v.tensor_tensor(count[:, :], next_row[:, :], region_start[:, :], ALU.subtract))
            link(v.tensor_scalar(tiles_i[:, :], count[:, :], float(P - 1), None, ALU.add))
            link(v.tensor_scalar(tiles_i[:, :], tiles_i[:, :], 7, None,
                                 ALU.arith_shift_right))
            link(v.tensor_scalar(tiles_f[:, :], tiles_i[:, :], 1.0, None, ALU.max))
            link(v.tensor_tensor_scan(tile_end[:, :], one_e[:, :], tiles_f[:, :], 0.0, ALU.mult,
                                      ALU.add))
            link(v.tensor_tensor(tile_start[:, :], tile_end[:, :], tiles_f[:, :], ALU.subtract))
            link(v.tensor_copy(tab_start[:, :], tile_start[0:1, :]))
            link(v.tensor_copy(tab_pad[:, :], next_row[0:1, :]))
            row3 = [1, TILES, NE]
            link(v.tensor_tensor(begun[:, :, :], tile_start[0:1, :].unsqueeze(1).to_broadcast(row3),
                                 iota_t[:, :].unsqueeze(2).to_broadcast(row3), ALU.is_le))
            link(v.tensor_tensor(begun_at[:, :, :], begun[:, :, :],
                                 tile_start[0:1, :].unsqueeze(1).to_broadcast(row3), ALU.mult))
            link(v.tensor_reduce(tile_expert[:, :], begun[:, :, :], AX.X, ALU.add))
            link(v.tensor_reduce(tile_first[:, :], begun_at[:, :, :], AX.X, ALU.max))
            link(v.tensor_scalar(tab_splits[:, :], tile_expert[:, :], 1.0, float(SPLITS), ALU.add,
                                 ALU.mult))
            link(v.tensor_copy(tab_slot[:, :], tile_expert[:, :]))
            link(v.tensor_scalar(tab_slot[:, :], tab_slot[:, :], 1, None, ALU.bitwise_and))
            link(v.tensor_scalar(tile_live[:, :], iota_t[:, :], tile_end[0:1, NE - 1:NE], float(P),
                                 ALU.is_lt, ALU.mult))
            link(v.tensor_tensor(tile_tmp[:, :], iota_t[:, :], tile_first[:, :], ALU.subtract))
            link(v.tensor_tensor(tile_tmp[:, :], tile_tmp[:, :], tile_live[:, :], ALU.mult))
            link(v.tensor_scalar(tile_expert[:, :], tile_expert[:, :], 1.0, float(REGION),
                                 ALU.subtract, ALU.mult))
            v.tensor_tensor(tab_row[:, :], tile_tmp[:, :], tile_expert[:, :],
                            ALU.add).then_inc(s["tables_ready"], 1)

            t0 = (B - 1) * ROWS
            sh_product(t0, 0)
            for r in range(1, ROWS):
                sh_product(t0 + r, r)
                sh_low(t0 + r - 1, r - 1)
                if r > 1:
                    sh_add(t0 + r - 2, r - 2)
            sh_low(t0 + 3, 3)
            sh_add(t0 + 2, 2)
            sh_add(t0 + 3, 3)

            link(v.tensor_scalar(shift_e[:, :], tile_start[:, :], float(P), None, ALU.mult))
            link(v.tensor_tensor(shift_e[:, :], shift_e[:, :], region_start[:, :], ALU.subtract))
            link(v.tensor_tensor(
                shifted[:, :, :], onehot_all[:, :].rearrange("p (j e) -> p j e", e=NE),
                shift_e[:, :].unsqueeze(1).to_broadcast([P, TT * TOPK, NE]), ALU.mult))
            link(v.tensor_reduce(out_row_f[:, :], shifted[:, :, :], AX.X, ALU.add))
            link(v.tensor_tensor(out_row_f[:, :], out_row_f[:, :], row_all[:, :], ALU.add))
            v.tensor_copy(out_row[:, :], out_row_f[:, :]).then_inc(s["out_rows_known"], 1)

            def low_rows(t, k):
                dve.wait_ge(s["xr_hi_s"], t + 1)
                v.tensor_tensor(xr_lo[k][:, :], bank[2 + k][:, :], xr_hi[k][:, :].bitcast(F32),
                                ALU.subtract).then_inc(s["xr_lo_s"], 1)

            def tile_step(t, k):
                fixed = isinstance(t, int)
                if not fixed or t >= 1:
                    dve.wait_ge(s["d_hi"], t)
                    v.tensor_tensor(ht_lo[1 - k][:, :], bank[6][:, 0:len(HC) * P],
                                    ht_hi[1 - k][:, :].bitcast(F32), ALU.subtract).then_inc(
                                        s["d_lo"], 1)
                if not fixed or t < TILES:
                    dve.wait_ge(s["d_h1"], t + 1)
                    v.tensor_tensor(h1[k][:, :], h1[k][:, :], [bank[5], bank[1]][k][:, 0:H],
                                    ALU.mult).then_inc(s["d_prod"], 1)
                if not fixed or t + 1 < TILES:
                    low_rows(t + 1, 1 - k)
                if not fixed or t >= 1:
                    dve.wait_ge(s["d_y"], t)
                    if not fixed or t >= 3:
                        dve.wait_ge(y_stored[1 - k], (t + (k - 2)) * 8)
                    v.tensor_copy(y_out[1 - k][:, :], bank[7][:, :]).then_inc(s["d_y_e"], 1)

            low_rows(0, 0)
            for t in range(3):
                tile_step(t, t % 2)
            with dve.Fori(3, TILES - 2, 2) as t:
                tile_step(t, 1)
                tile_step(t + 1, 0)
            for t in range(3 + 2 * len(range(3, TILES - 2, 2)), TILES + 1):
                tile_step(t, t % 2)

            chain["at"], chain["n"] = chain["at"] + chain["n"], 0
            for t in range(TT):
                dve.wait_ge(gathered_s[t % G_BUFS], 16 * TOPK * (t // G_BUFS + 1))
                for k in range(TOPK):
                    j = t * TOPK + k
                    ins = v.scalar_tensor_tensor(acc_tile(t), rows_of_4[t % G_BUFS][:, k, :],
                                                 weight_all[:, j:j + 1], acc_tile(t), ALU.mult,
                                                 ALU.add)
                    if k < TOPK - 1:
                        link(ins)
                    else:
                        ins.then_inc(s["out_ready"], 1)


_INS = ["x", "fside_BxS2xS2_0", "ctx_1024", "g_xattn", "g_ffn", "L0_ffn_gate_w", "L0_ffn_gate_b",
        "L0_ffn_w1_shared", "L0_ffn_w2_shared", "L0_ffn_w3_shared", "L0_ffn_w1_routed",
        "L0_ffn_w2_routed", "L0_ffn_w3_routed"]
_OUTS = [((4, 512, 512), "float32")]


def kernel(**inputs):
    import numpy as _np
    import concourse.bacc as _bacc
    from concourse import mybir as _mybir
    from concourse.bass_utils import run_bass_kernel_spmd as _run

    nc = _bacc.Bacc("TRN2", target_bir_lowering=False, num_devices=1)
    arrays, args = {}, []
    for name in _INS:
        a = _np.ascontiguousarray(inputs[name])
        arrays[f"in_{name}_dram"] = a
        args.append(nc.dram_tensor(f"in_{name}_dram", a.shape, _mybir.dt.from_np(a.dtype),
                                   kind="ExternalInput").ap())
    for i, (shape, dtype) in enumerate(_OUTS):
        args.append(nc.dram_tensor(f"out_{i}_dram", shape, _mybir.dt.from_np(_np.dtype(dtype)),
                                   kind="ExternalOutput").ap())
    flamingo_moe(nc, *args)
    r = _run(nc, [arrays], core_ids=[0])
    return r.results[0]["out_0_dram"]
```

```python
from contextlib import ExitStack

import concourse.bass as bass
from concourse import mybir

F32 = mybir.dt.float32
F32R = mybir.dt.float32r
BF16 = mybir.dt.bfloat16
I32 = mybir.dt.int32
U32 = mybir.dt.uint32
SIZE = {F32: 4, F32R: 4, BF16: 2, I32: 4, U32: 4}
ALU = mybir.AluOpType
ACT = mybir.ActivationFunctionType
AX = mybir.AxisListType

P = 128
TOPK = 4
QMAX = 127.0
Q_EPS = 1e-6
LN_EPS = 1e-5
ROUND = 1.5 * 2.0**23
ROWS = 4


def flamingo_moe(nc, x, w_gate_up, w_down, g_xattn, g_ffn, gate_w, gate_b, w1_shared, w2_shared,
                 w3_shared, w1_routed, w2_routed, w3_routed, out):
    B, S, D = x.shape
    I = w_down.shape[2]
    NE, _, H = w1_routed.shape
    TOK = B * S
    KC = D // P
    TT = TOK // P
    HSTEP = (H - P) // 2
    HC = [(0, HSTEP), (HSTEP, HSTEP), (2 * HSTEP, P)]
    assert S == ROWS * P and D == 4 * P and I == 2 * P and 2 * P < H < 3 * P and H % 2 == 0 and NE == 16
    TILES = (TOK * TOPK + NE * (P - 1)) // P
    CLEARS = 3 * (B - 1)
    CLEAR = (TILES + CLEARS - 1) // CLEARS
    REGION = TOK + P
    W13 = KC * 2 * H
    W2 = len(HC) * D
    ROW = D + NE
    LINEARS = {1: KC, 2: I // P}
    SCATTERS = ROWS * TOPK
    BE = ROWS * TOPK * NE

    x_rows = x.rearrange("b (r p) d -> b p r d", p=P)
    out_rows = out.rearrange("b (r p) d -> (b r) p d", p=P)
    dispatched = nc.dram_tensor("dispatched", [NE * REGION, ROW], F32, kind="Internal").ap()
    expert_out = nc.dram_tensor("expert_out", [CLEARS * CLEAR * P, D], F32, kind="Internal").ap()

    with ExitStack() as ctx:
        place = [(nc.sbuf_base + 31) // 32 * 32]

        def sb(name, shape, dt, at=None):
            n = SIZE[dt]
            for s in shape[1:]:
                n *= s
            where = place[0] if at is None else at
            if at is None:
                place[0] += (n + 31) // 32 * 32
            assert where + n <= nc.sbuf_usable_end, (name, where, n)
            return nc.alloc_sbuf_tensor_at(name, shape, dt, offset=where)

        def sem(name):
            return ctx.enter_context(nc.semaphore(name))

        bank = [ctx.enter_context(nc.psum_tensor(f"bank{i}", [P, 512], F32)) for i in range(8)]
        beside = bank[6][:, len(HC) * P:512]

        ident = sb("ident", [P, P], F32)
        ident_b = sb("ident_b", [P, P], BF16)
        ones_b = sb("ones_b", [P, P], BF16)
        before_b = sb("before_b", [P, P], BF16)
        iota_e = sb("iota_e", [P, NE], F32)
        region_start = sb("region_start", [P, NE], F32)
        one_e = sb("one_e", [P, NE], F32)
        not_first = sb("not_first", [P, ROWS, NE], F32)
        iota_k = sb("iota_k", [P, TOPK], F32)
        eps_ln = sb("eps_ln", [P, 1], F32)
        gates = sb("gates", [P, 2], F32)
        bias_e = sb("bias_e", [P, NE], F32)
        gate_rows = sb("gate_rows", [NE, D], F32)
        gate_hi = sb("gate_hi", [P, KC, NE], F32R)
        gate_lo = sb("gate_lo", [P, KC, NE], F32R)

        acc = sb("acc", [P, TT * D], F32)
        ring_at = place[0]
        ring13_hi = sb("ring13_hi", [P, 2 * W13], F32R)
        ring13_lo = sb("ring13_lo", [P, 2 * W13], F32R)
        ring2_hi = sb("ring2_hi", [P, 2 * W2], F32R)
        ring2_lo = sb("ring2_lo", [P, 2 * W2], F32R)
        raw13 = sb("raw13", [P, KC, 2, H], F32)
        raw2 = sb("raw2", [P, len(HC), D], F32)

        onehot_all = sb("onehot_all", [P, TT * TOPK * NE], F32)
        row_all = sb("row_all", [P, TT * TOPK], F32)
        score = sb("score", [P, ROWS * NE], F32)
        top8 = sb("top8", [P, ROWS, 8], F32)
        top8_at = sb("top8_at", [P, ROWS, 8], U32)
        top_at = sb("top_at", [P, ROWS * TOPK], F32)
        onehot = sb("onehot", [P, BE], F32)
        taken = sb("taken", [P, ROWS * NE], BF16)
        total4 = sb("total4", [P, ROWS], F32)
        rank = sb("rank", [P, ROWS * NE], F32)
        weight = sb("weight", [P, ROWS, NE], F32)
        next_row = sb("next_row", [P, NE], F32)
        pos = sb("pos", [P, ROWS * NE], F32)
        picked = sb("picked", [P, BE], F32)
        row_f = sb("row_f", [P, ROWS * TOPK], F32)
        row_u = sb("row_u", [P, ROWS * TOPK], U32)

        xt_hi = sb("xt_hi", [P, ROWS, KC * P], F32R)
        xt_lo = sb("xt_lo", [P, ROWS, KC * P], F32R)
        h1 = [sb(f"h1_{i}", [P, H], F32) for i in range(2)]
        h3 = [sb(f"h3_{i}", [P, H], F32) for i in range(2)]
        ht_hi = [sb(f"ht_hi{i}", [P, len(HC) * P], F32R) for i in range(2)]
        ht_lo = [sb(f"ht_lo{i}", [P, len(HC) * P], F32R) for i in range(2)]

        slot1 = [ring_at + W13 * 4, ring_at + 3 * W13 * 4, ring_at + (4 * W13 + W2) * 4,
                 ring_at + (4 * W13 + 3 * W2) * 4]
        xa1 = sb("xa1", [P, ROWS, D], F32, at=slot1[0])
        wscale1 = sb("wscale1", [P, D], F32, at=slot1[0] + ROWS * D * 4)
        wa1 = sb("wa1", [P, ROWS, D], F32, at=slot1[1])
        s_row1 = sb("s_row1", [P, D], F32, at=slot1[1] + ROWS * D * 4)
        xq1 = sb("xq1", [P, ROWS, D], BF16, at=slot1[2])
        wq1 = sb("wq1", [P, ROWS, D], BF16, at=slot1[3])
        assert ROWS * D * 4 + D * 4 <= W13 * 4 and ROWS * D * 2 <= W2 * 4
        hid_at = place[0]
        hid = sb("hid", [P, ROWS, D], F32)
        xq_t1 = sb("xq_t1", [P, KC, ROWS * P], BF16)
        wq_t1 = sb("wq_t1", [P, KC, ROWS * P], BF16)

        second = place[0]
        wa2 = sb("wa2", [P, ROWS, I], F32)
        xa2 = sb("xa2", [P, ROWS, I], F32)
        lin2_out = sb("lin2_out", [P, 2, D], F32)
        xq2 = sb("xq2", [P, ROWS, I], BF16)
        wq2 = sb("wq2", [P, ROWS, I], BF16)
        xq_t2 = sb("xq_t2", [P, 2, ROWS * P], BF16)
        wq_t2 = sb("wq_t2", [P, 2, ROWS * P], BF16)
        wscale2 = sb("wscale2", [P, D], F32)
        s_row2 = sb("s_row2", [P, I], F32)
        end_second = place[0]
        xn2 = sb("xn2", [P, ROWS, ROW], F32)

        small = {}
        for L, k in LINEARS.items():
            small[L] = {
                "stats": sb(f"stats{L}", [P, ROWS, 6], F32),
                "mean_var": sb(f"mean_var{L}", [P, ROWS, 2], F32),
                "std": sb(f"std{L}", [P, ROWS], F32),
                "rstd": sb(f"rstd{L}", [P, ROWS], F32),
                "amax": sb(f"amax{L}", [P, 2, k], F32),
                "ratio": sb(f"ratio{L}", [P, k], F32),
                "smooth": sb(f"smooth{L}", [P, 2, k], F32),
                "row_max": sb(f"row_max{L}", [P, 2, ROWS], F32),
                "q_scale": sb(f"q_scale{L}", [P, 2, ROWS], F32),
                "q_inv": sb(f"q_inv{L}", [P, 2, ROWS], F32),
            }
        wide = {1: D, 2: I}
        xa, wa = {1: xa1, 2: xa2}, {1: wa1, 2: wa2}
        xq, wq = {1: xq1, 2: xq2}, {1: wq1, 2: wq2}
        xq_t, wq_t = {1: xq_t1, 2: xq_t2}, {1: wq_t1, 2: wq_t2}
        wscale, s_row = {1: wscale1, 2: wscale2}, {1: s_row1, 2: s_row2}

        zero_rows = sb("zero_rows", [P, ROW], F32)
        tile_weight = sb("tile_weight", [P, TILES], F32)
        iota_t = sb("iota_t", [1, TILES], F32)
        end = place[0]
        place[0] = hid_at
        shifted = sb("shifted", [P, TT * TOPK, NE], F32)
        count = sb("count", [P, NE], F32)
        tiles_i = sb("tiles_i", [P, NE], I32)
        tiles_f = sb("tiles_f", [P, NE], F32)
        tile_end = sb("tile_end", [P, NE], F32)
        tile_start = sb("tile_start", [P, NE], F32)
        shift_e = sb("shift_e", [P, NE], F32)
        out_row_f = sb("out_row_f", [P, TT * TOPK], F32)
        out_row = sb("out_row", [P, TT * TOPK], U32)
        tile_expert = sb("tile_expert", [1, TILES], F32)
        tile_first = sb("tile_first", [1, TILES], F32)
        tile_live = sb("tile_live", [1, TILES], F32)
        tile_tmp = sb("tile_tmp", [1, TILES], F32)
        tab_row = sb("tab_row", [1, TILES], I32)
        tab_slot = sb("tab_slot", [1, TILES], I32)
        tab_need = sb("tab_need", [1, TILES], I32)
        tab_pad = sb("tab_pad", [1, NE], I32)
        tab_start = sb("tab_start", [1, NE], I32)
        tab_expert = sb("tab_expert", [1, TILES], I32)
        tab_stored = sb("tab_stored", [1, 2, NE], I32)
        assert place[0] <= second
        place[0] = end

        end = place[0]
        place[0] = second
        x_in = [sb(f"x_in{i}", [P, ROW], F32) for i in range(2)]
        y_out = [sb(f"y_out{i}", [P, D], F32) for i in range(2)]
        xr_hi = [sb(f"xr_hi{i}", [P, KC * P], F32R) for i in range(2)]
        xr_lo = [sb(f"xr_lo{i}", [P, KC * P], F32R) for i in range(2)]
        begun = sb("begun", [1, TILES, NE], F32)
        assert place[0] <= end_second
        place[0] = end

        names = (
            "consts gates_in gate_rows_in gates_ready gate_t gate_hi_ready gate_lo_ready "
            "x_loaded wa1_loaded wa2_loaded ln_var1 ln_var2 ln_std1 ln_std2 xn_ready "
            "w_t1 w_t2 x_t1 x_t2 w_max1 w_max2 x_max1 x_max2 ratio1 ratio2 s_raw1 s_raw2 "
            "smooth1 smooth2 bc1 bc2 s_copied1 s_copied2 ws_ready1 ws_ready2 scales1 scales2 "
            "wt1 wt2 xs1 xs2 wq_ready1 wq_ready2 xq_ready1 xq_ready2 wq_t1 wq_t2 wq_e1 wq_e2 "
            "xq_t1 xq_t2 xq_e1 xq_e2 wsc1 wsc2 wsc_e1 wsc_e2 mm1 mm2 mm_e1 mm_e2 "
            "gate_half up_half silu_gate a_ready x1_done xn2_ready xn2_t xn2_hi xn2_lo logits "
            "exp_ready taken_ready prefix rows_ready scattered xn2_free dve_chain pool_chain "
            "raw13_in raw2_in hi13_in hi2_in ready13 ready2 sh_h sh_h1 sh_prod sh_t sh_hi sh_lo "
            "sh_y sh_y_e pads_known out_rows_known tables_ready pads_written xr_t xr_hi_s xr_lo_s "
            "d_h d_h1 d_prod d_act d_t d_hi d_lo d_y d_y_e weight_picked cleared gathered out_stored"
        ).split()
        s = {n: sem("s_" + n) for n in names}
        tile_in = [sem(f"s_tile_in{i}") for i in range(2)]
        y_stored = [sem(f"s_y_stored{i}") for i in range(2)]
        last_gathered = [sem(f"s_last_gathered{i}") for i in range(TT)]

        def acc_tile(t):
            return acc[:, bass.ds(t * D, D)]

        def ring13(half, slot_at, c, m):
            return half[:, bass.ds(slot_at + (c * 2 + m) * H, H)]

        def ring2(half, slot_at, c):
            return half[0:HC[c][1], bass.ds(slot_at + c * D, D)]

        block = ctx.enter_context(nc.Block())

        @block.sync
        def _(sp):
            sp.dma_start(gates[:, 0:1], g_xattn.partition_broadcast(P)).then_inc(s["gates_in"], 16)
            sp.dma_start(gates[:, 1:2], g_ffn.partition_broadcast(P)).then_inc(s["gates_in"], 16)
            sp.dma_start(bias_e[:, :], gate_b.partition_broadcast(P)).then_inc(s["gates_in"], 16)
            sp.dma_start(gate_rows[:, :], gate_w).then_inc(s["gate_rows_in"], 16)

            def load_batch(b):
                xb = x_rows[bass.ds(b, 1)].rearrange("a p r d -> (a p) r d")
                sp.dma_start(acc[:, bass.ds(b * ROWS * D, ROWS * D)].rearrange(
                    "p (r d) -> p r d", r=ROWS), xb).then_inc(s["x_loaded"], 16)

            def load_weights(b):
                src = w_gate_up[bass.ds(b, 1)].rearrange("a (r p) d -> p (a r) d", p=P)
                sp.dma_start(wa1[:, :, :], src).then_inc(s["wa1_loaded"], 16)

            def load_down(b):
                src = w_down[bass.ds(b, 1)].rearrange("a (r p) d -> p (a r) d", p=P)
                sp.dma_start(wa2[:, :, :], src).then_inc(s["wa2_loaded"], 16)

            load_batch(0)
            load_weights(0)
            load_down(0)
            with sp.Fori(1, B, 1) as b:
                sp.wait_ge(s["ln_var1"], b)
                load_batch(b)
                sp.wait_ge(s["wq_ready1"], b)
                load_weights(b)
                sp.wait_ge(s["wq_ready2"], b)
                load_down(b)

            sp.wait_ge(s["pads_known"], 1)
            PADS = 4
            with sp.Fori(0, NE // PADS, 1) as e:
                rows = [sp.value_load(tab_pad[0:1, bass.ds(e * PADS + i, 1)], min_val=0,
                                      max_val=NE * REGION - P) for i in range(PADS)]
                for row in rows:
                    sp.dma_start(dispatched[bass.ds(row, P), :], zero_rows[:, :]).then_inc(
                        s["pads_written"], 16)
            sp.wait_ge(s["tables_ready"], 1)
            sp.wait_ge(s["pads_written"], 16 * NE)
            sp.wait_ge(s["scattered"], 16 * SCATTERS * B)
            sp.wait_ge(s["cleared"], 16 * CLEARS)

            def load_tile(t, k):
                row = sp.value_load(tab_row[0:1, bass.ds(t, 1)], min_val=0,
                                    max_val=NE * REGION - P)
                sp.dma_start(x_in[k][:, :], dispatched[bass.ds(row, P), :]).then_inc(tile_in[k], 16)

            def store_tile(t, k):
                sp.dma_start(expert_out[bass.ds(t * P, P), :], y_out[k][:, :]).then_inc(
                    y_stored[k], 16)

            load_tile(0, 0)
            load_tile(1, 1)
            for t in range(2, 4):
                sp.wait_ge(s["xr_t"], t - 1)
                sp.wait_ge(s["weight_picked"], t - 1)
                load_tile(t, t % 2)
            with sp.Fori(0, TILES - 5, 2) as t:
                for k in range(2):
                    sp.wait_ge(s["xr_t"], t + (k + 3))
                    sp.wait_ge(s["weight_picked"], t + (k + 3))
                    load_tile(t + (k + 4), k)
                    sp.wait_ge(s["d_y_e"], t + (k + 1))
                    store_tile(t + k, k)
            for t in range(2 * len(range(0, TILES - 5, 2)), TILES):
                if t + 4 < TILES:
                    sp.wait_ge(s["xr_t"], t + 3)
                    sp.wait_ge(s["weight_picked"], t + 3)
                    load_tile(t + 4, t % 2)
                sp.wait_ge(s["d_y_e"], t + 1)
                store_tile(t, t % 2)

            for t in range(TT):
                sp.wait_ge(last_gathered[t], 16)
                sp.dma_start(out_rows[t], acc_tile(t)).then_inc(s["out_stored"], 16)
            sp.wait_ge(s["out_stored"], 16 * TT)

        @block.gpsimd
        def _(pool):
            g = nc.gpsimd
            own = [0]

            def done(ins):
                own[0] += 1
                ins.then_inc(s["pool_chain"], 1)

            def fence():
                pool.wait_ge(s["pool_chain"], own[0])

            def wait_alone():
                pool.nop(nofuse=True)

            done(g.memset(ident[:, :], 0.0))
            done(g.memset(ident_b[:, :], 0.0))
            done(g.memset(before_b[:, :], 1.0))
            done(g.memset(ones_b[:, :], 1.0))
            done(g.memset(one_e[:, :], 1.0))
            done(g.memset(eps_ln[:, :], LN_EPS))
            done(g.memset(not_first[:, :, :], 1.0))
            done(g.memset(raw2[:, 0:2, :], 0.0))
            fence()
            done(g.affine_select(out=ident[:, :], in_=ident[:, :], compare_op=ALU.not_equal,
                                 fill=1.0, base=0, pattern=[[-1, P]], channel_multiplier=1))
            done(g.affine_select(out=ident_b[:, :], in_=ident_b[:, :], compare_op=ALU.not_equal,
                                 fill=1.0, base=0, pattern=[[-1, P]], channel_multiplier=1))
            done(g.affine_select(out=before_b[:, :], in_=before_b[:, :], compare_op=ALU.is_gt,
                                 fill=0.0, base=0, pattern=[[1, P]], channel_multiplier=-1))
            done(g.iota(iota_e[:, :], [[1, NE]], base=0, channel_multiplier=0,
                        allow_small_or_imprecise_dtypes=True))
            done(g.iota(region_start[:, :], [[REGION, NE]], base=0, channel_multiplier=0,
                        allow_small_or_imprecise_dtypes=True))
            fence()
            done(g.memset(not_first[:, :, 0:1], 0.0))
            done(g.iota(iota_k[:, :], [[1, TOPK]], base=1, channel_multiplier=0,
                        allow_small_or_imprecise_dtypes=True))
            done(g.memset(zero_rows[:, :], 0.0))
            done(g.iota(iota_t[0:1, :], [[1, TILES]], base=0, channel_multiplier=0,
                        allow_small_or_imprecise_dtypes=True))
            fence()
            g.iota(next_row[:, :], [[REGION, NE]], base=0, channel_multiplier=0,
                   allow_small_or_imprecise_dtypes=True).then_inc(s["consts"], 1)

            def load_hidden(w1, w3):
                pool.dma_start(raw13[:, :, 0, :], w1.rearrange("(c p) h -> p c h", p=P)).then_inc(
                    s["raw13_in"], 16)
                pool.dma_start(raw13[:, :, 1, :], w3.rearrange("(c p) h -> p c h", p=P)).then_inc(
                    s["raw13_in"], 16)

            def load_out(w2):
                pool.dma_start(raw2[0:HSTEP, 0:2, :], w2[0:2 * HSTEP, :].rearrange(
                    "(c p) n -> p c n", c=2)).then_inc(s["raw2_in"], 16)
                pool.dma_start(raw2[:, 2, :], w2[2 * HSTEP:H, :]).then_inc(s["raw2_in"], 16)

            def load_routed(e):
                def part(which):
                    w1, w3, w2 = (w[bass.ds(e, 1)].rearrange("a d h -> (a d) h")
                                  for w in (w1_routed, w3_routed, w2_routed))
                    load_out(w2) if which else load_hidden(w1, w3)
                return part

            def round_half(hi, raw, at, size, rounded):
                pool.dma_start(hi[:, at:at + size], raw).then_inc(s[rounded], 16)

            def fill(n, slot, free13, free2, load_next):
                raw = raw13[:, :, :, :].rearrange("p c m h -> p (c m h)")
                raw_2 = raw2[:, :, :].rearrange("p c n -> p (c n)")
                at, at2 = slot * W13, slot * W2
                pool.wait_ge(s["raw13_in"], 32 * n + 32)
                free13()
                wait_alone()
                round_half(ring13_hi, raw, at, W13, "hi13_in")
                pool.wait_ge(s["hi13_in"], 16 * n + 16)
                g.tensor_tensor(ring13_lo[:, at:at + W13], raw,
                                ring13_hi[:, at:at + W13].bitcast(F32),
                                ALU.subtract).then_inc(s["ready13"], 1)
                pool.wait_ge(s["raw2_in"], 32 * n + 32)
                free2()
                wait_alone()
                round_half(ring2_hi, raw_2, at2, W2, "hi2_in")
                pool.wait_ge(s["ready13"], n + 1)
                wait_alone()
                load_next(0)
                pool.wait_ge(s["hi2_in"], 16 * n + 16)
                g.tensor_tensor(ring2_lo[:, at2:at2 + W2], raw_2,
                                ring2_hi[:, at2:at2 + W2].bitcast(F32),
                                ALU.subtract).then_inc(s["ready2"], 1)
                pool.wait_ge(s["ready2"], n + 1)
                wait_alone()
                load_next(1)

            def free():
                pass

            load_hidden(w1_shared, w3_shared)
            load_out(w2_shared)
            def smoothed_weights(b, L):
                k = wide[L]
                pool.wait_ge(s[f"s_copied{L}"], b + 1)
                g.tensor_tensor(wa[L][:, :, :], wa[L][:, :, :],
                                s_row[L][:, :].unsqueeze(1).to_broadcast([P, ROWS, k]),
                                ALU.mult).then_inc(s[f"ws_ready{L}"], 1)

            def hidden_rows(b):
                pool.wait_ge(s["wsc_e1"], b + 1)
                pool.wait_ge(s["mm_e1"], ROWS * b + ROWS)
                for at, ready in ((0, "gate_half"), (I, "up_half")):
                    g.tensor_tensor(hid[:, :, at:at + I], hid[:, :, at:at + I],
                                    wscale1[:, at:at + I].unsqueeze(1).to_broadcast([P, ROWS, I]),
                                    ALU.mult).then_inc(s[ready], 1)
                pool.wait_ge(s["up_half"], b + 1)
                pool.wait_ge(s["silu_gate"], b + 1)
                g.tensor_tensor(xa2[:, :, :], hid[:, :, 0:I], hid[:, :, I:2 * I],
                                ALU.mult).then_inc(s["a_ready"], 1)

            def residual(b):
                for r in range(ROWS):
                    pool.wait_ge(s["mm_e2"], ROWS * b + r + 1)
                    wait_alone()
                    t = b * ROWS + r
                    g.tensor_tensor(acc_tile(t), lin2_out[:, r % 2, :], acc_tile(t),
                                    ALU.add).then_inc(s["x1_done"], 1)

            def scatter_batch(b):
                pool.wait_ge(s["rows_ready"], b + 1)
                wait_alone()
                for j in range(SCATTERS):
                    g.indirect_dma_start(
                        out=dispatched, out_offset=bass.IndirectOffsetOnAxis(
                            ap=row_u[:, j:j + 1], axis=0),
                        in_=xn2[:, j // TOPK, :], in_offset=None).then_inc(s["scattered"], 16)

            def iteration(i, first, second, shared, then=None):
                if second:
                    smoothed_weights(i - 1, 2)
                if first:
                    smoothed_weights(i, 1)
                if then:
                    then()
                if second:
                    residual(i - 1)
                if shared:
                    scatter_batch(i - 2)
                if first:
                    hidden_rows(i)
                if shared:
                    pool.wait_ge(s["scattered"], 16 * SCATTERS * (i - 1))
                    wait_alone()
                    pool.nop(nofuse=True).then_inc(s["xn2_free"], 1)

            pool.nop(nofuse=True).then_inc(s["xn2_free"], 1)
            iteration(0, True, False, False)
            iteration(1, True, True, False, lambda: fill(0, 0, free, free, load_routed(0)))
            with pool.Fori(2, B, 1) as i:
                iteration(i, True, True, True)
            iteration(B, False, True, True, lambda: fill(1, 1, free, free, load_routed(1)))
            iteration(B + 1, False, False, True)

            fill(2, 0, lambda: pool.wait_ge(s["sh_h"], TT), lambda: pool.wait_ge(s["sh_y"], TT),
                 load_routed(2))
            pool.wait_ge(s["tables_ready"], 1)

            def refill(n, slot, load_next):
                first = pool.value_load(tab_start[0:1, bass.ds(n - 2, 1)], min_val=0,
                                        max_val=TILES)
                fill(n, slot, lambda: pool.wait_ge(s["d_h"], first),
                     lambda: pool.wait_ge(s["d_y"], first), load_next)

            with pool.Fori(3, NE - 1, 2) as n:
                refill(n, 1, load_routed(n))
                refill(n + 1, 0, load_routed(n + 1))
            refill(NE - 1, 1, load_routed(NE - 1))

            def add_rows(k):
                after = NE - TOPK + k + 1
                for parity in range(2):
                    if after < NE:
                        tiles = pool.value_load(tab_stored[0:1, parity, after:after + 1],
                                                min_val=0, max_val=16 * TILES)
                    else:
                        tiles = 16 * ((TILES + 1 - parity) // 2)
                    pool.wait_ge(y_stored[parity], tiles)
                    wait_alone()
                if k:
                    pool.wait_ge(s["gathered"], 16 * TT * k)
                for t in range(TT):
                    j = t * TOPK + k
                    g.indirect_dma_start(
                        out=acc_tile(t), out_offset=None, in_=expert_out,
                        in_offset=bass.IndirectOffsetOnAxis(ap=out_row[:, j:j + 1], axis=0),
                        compute_op=ALU.add).then_inc(
                            s["gathered"] if k < TOPK - 1 else last_gathered[t], 16)

            pool.wait_ge(s["out_rows_known"], 1)
            add_rows(0)
            refill(NE, 0, lambda which: None)
            for k in range(1, TOPK):
                add_rows(k)

        @block.tensor
        def _(pe):
            mm, transpose = nc.tensor.matmul, nc.tensor.transpose

            pe.wait_ge(s["consts"], 1)
            pe.wait_ge(s["gate_rows_in"], 16)
            for c in range(KC):
                last = transpose(bank[0][:, c * NE:(c + 1) * NE],
                                 gate_rows[:, c * P:(c + 1) * P], ident[0:NE, 0:NE])
            last.then_inc(s["gate_t"], 1)

            def hidden(x_hi, x_lo, slot_at, into1, into3, chunks=range(KC)):
                outs = (into1[:, 0:H], into3[:, 0:H])
                for c in chunks:
                    for half, w, stop in ((x_hi, ring13_hi, False), (x_hi, ring13_lo, False),
                                          (x_lo, ring13_hi, True)):
                        for m in range(2):
                            last = mm(outs[m], half[:, c * P:(c + 1) * P],
                                      ring13(w, slot_at, c, m),
                                      start=(c == 0 and half is x_hi and w is ring13_hi),
                                      stop=(c == KC - 1 and stop))
                return last

            def hidden_t(act, into):
                for c, (at, size) in enumerate(HC):
                    last = transpose(into[0:size, c * P:(c + 1) * P], act[:, at:at + size],
                                     ident[:, :])
                return last

            def project(h_hi, h_lo, slot_at, into):
                n = 0
                for c, (_, size) in enumerate(HC):
                    for half, w in ((h_hi, ring2_hi), (h_hi, ring2_lo), (h_lo, ring2_hi)):
                        last = mm(into[:, :], half[0:size, c * P:(c + 1) * P],
                                  ring2(w, slot_at, c), start=(n == 0), stop=(n == 8))
                        n += 1
                return last

            def rows_t(tile, into, c, w):
                for r in range(ROWS):
                    last = transpose(into[:, r * P:(r + 1) * P], tile[:, r, c * P:(c + 1) * P],
                                     ident[:, :])
                return last

            def spread(into, column, chunks):
                for c in range(chunks):
                    last = transpose(into[:, c * P:(c + 1) * P],
                                     column[:, c:c + 1].to_broadcast([P, P]), ident[:, :])
                return last

            def c1(t, r):
                if r:
                    pe.wait_ge(s["sh_prod"], t + ROWS)
                pe.wait_ge(s["xn2_lo"], t + 1)
                hidden(xt_hi[:, r, :], xt_lo[:, r, :], 0, bank[4], bank[5]).then_inc(s["sh_h"], 1)

            def c2(t, r):
                pe.wait_ge(s["sh_prod"], t + ROWS + 1)
                if r:
                    pe.wait_ge(s["sh_lo"], t)
                hidden_t(h3[r % 2], bank[6]).then_inc(s["sh_t"], 1)

            def c3(t, r):
                pe.wait_ge(s["sh_lo"], t + 1)
                if r:
                    pe.wait_ge(s["sh_y_e"], t)
                project(ht_hi[r % 2], ht_lo[r % 2], 0, bank[7]).then_inc(s["sh_y"], 1)

            def w_columns(b, L):
                pe.wait_ge(s[f"wa{L}_loaded"], 16 * b + 16)
                if L == 1:
                    if isinstance(b, int) and b == 0:
                        pe.wait_ge(s["gate_lo_ready"], 1)
                    else:
                        pe.wait_ge(s["mm_e1"], ROWS * b)
                elif not (isinstance(b, int) and b == 0):
                    pe.wait_ge(s["mm_e2"], ROWS * b)
                for c in range(LINEARS[L]):
                    if c >= 2:
                        pe.wait_ge(s[f"w_max{L}"], LINEARS[L] * b + c - 1)
                    rows_t(wa[L], bank[2 * (L - 1) + c % 2], c, 0).then_inc(s[f"w_t{L}"], 1)

            def x_columns(b, L):
                if L == 1:
                    pe.wait_ge(s["xn_ready"], ROWS * b + ROWS)
                else:
                    pe.wait_ge(s["a_ready"], b + 1)
                chunks = LINEARS[L]
                for c in range(chunks):
                    if c < 2:
                        pe.wait_ge(s[f"w_max{L}"], chunks * (b + 1) - 1 + c)
                    else:
                        pe.wait_ge(s[f"x_max{L}"], chunks * b + c - 1)
                    rows_t(xa[L], bank[2 * (L - 1) + c % 2], c, 0).then_inc(s[f"x_t{L}"], 1)

            def smoothing(b, L):
                pe.wait_ge(s[f"smooth{L}"], b + 1)
                for j in (1, 0):
                    spread(bank[2 * (L - 1) + j], small[L]["smooth"][:, j, :],
                           LINEARS[L]).then_inc(s[f"bc{L}"], 1)

            def quantised_t(b, L):
                pairs = LINEARS[L] // 2
                n = 0
                for q, ready, t_done in ((wq[L], f"wq_ready{L}", f"wq_t{L}"),
                                         (xq[L], f"xq_ready{L}", f"xq_t{L}")):
                    pe.wait_ge(s[ready], b + 1)
                    for j in range(pairs):
                        into = bank[2 * (L - 1) + n % 2][:, :].bitcast(BF16)
                        if n >= 2:
                            pe.wait_ge(s[f"wq_e{L}"], 2 * b + j + 1)
                        for i in range(2):
                            for r in range(ROWS):
                                at = (2 * j + i) * P
                                last = transpose(into[:, (i * ROWS + r) * P:(i * ROWS + r + 1) * P],
                                                 q[:, r, at:at + P], ident_b[:, :])
                        last.then_inc(s[t_done], 1)
                        n += 1

            def quantised_mm(b, L):
                pairs = LINEARS[L] // 2
                even, odd = bank[2 * (L - 1)], bank[2 * (L - 1) + 1]
                pe.wait_ge(s[f"xq_e{L}" if pairs == 2 else f"wq_e{L}"], pairs * b + 1)
                spread(even, small[L]["q_scale"][:, 1, :], ROWS).then_inc(s[f"wsc{L}"], 1)
                for r in range(ROWS):
                    if r == 0:
                        pe.wait_ge(s[f"xq_e{L}"], pairs * b + pairs)
                        pe.wait_ge(s[f"wq_e{L}"], pairs * b + pairs)
                    elif r == 1:
                        pe.wait_ge(s[f"wsc_e{L}"], b + 1)
                    else:
                        pe.wait_ge(s[f"mm_e{L}"], ROWS * b + r - 1)
                    for c in range(LINEARS[L]):
                        last = mm((even if r % 2 else odd)[:, :], xq_t[L][:, c, r * P:(r + 1) * P],
                                  wq_t[L][:, c, :], start=(c == 0), stop=(c == LINEARS[L] - 1))
                    last.then_inc(s[f"mm{L}"], 1)

            def normed_t(b):
                pe.wait_ge(s["sh_prod"], ROWS * (b + 1))
                for r in range(ROWS):
                    pe.wait_ge(s["xn2_ready"], ROWS * b + r + 1)
                    if r >= 2:
                        pe.wait_ge(s["xn2_lo"], ROWS * b + r - 1)
                    for c in range(KC):
                        last = transpose(bank[4 + r % 2][:, c * P:(c + 1) * P],
                                         xn2[:, r, c * P:(c + 1) * P], ident[:, :])
                    last.then_inc(s["xn2_t"], 1)

            def router(b):
                pe.wait_ge(s["xn2_lo"], ROWS * b + ROWS)
                for r in range(ROWS):
                    n = 0
                    for c in range(KC):
                        for xh, gh in ((xt_hi, gate_hi), (xt_hi, gate_lo), (xt_lo, gate_hi)):
                            last = mm(beside[:, r * NE:(r + 1) * NE],
                                      xh[:, r, c * P:(c + 1) * P], gh[:, c, :],
                                      start=(n == 0), stop=(n == 3 * KC - 1))
                            n += 1
                last.then_inc(s["logits"], 1)

            def tokens_before(b):
                pe.wait_ge(s["taken_ready"], b + 1)
                for r in range(ROWS + 1):
                    into = beside[:, r * NE:(r + 1) * NE]
                    for q in range(min(r + 1, ROWS)):
                        last = mm(into, (before_b if q == r else ones_b)[:, :],
                                  taken[:, q * NE:(q + 1) * NE], start=(q == 0),
                                  stop=(q == min(r, ROWS - 1)))
                last.then_inc(s["prefix"], 1)

            def iteration(i, first, second, shared):
                b = i - 2
                t = b * ROWS
                if second:
                    w_columns(i - 1, 2)
                if shared:
                    normed_t(b)
                if second:
                    x_columns(i - 1, 2)
                if first:
                    w_columns(i, 1)
                    x_columns(i, 1)
                if second:
                    smoothing(i - 1, 2)
                if first:
                    smoothing(i, 1)
                if shared:
                    router(b)
                    c1(t, 0)
                if second:
                    quantised_t(i - 1, 2)
                if shared:
                    tokens_before(b)
                    c1(t + 1, 1)
                if second:
                    quantised_mm(i - 1, 2)
                if first:
                    quantised_t(i, 1)
                if shared:
                    pe.wait_ge(s["rows_ready"], b + 1)
                    c2(t, 0)
                    c2(t + 1, 1)
                    c3(t, 0)
                    c1(t + 2, 2)
                if first:
                    quantised_mm(i, 1)
                if shared:
                    c3(t + 1, 1)
                    c1(t + 3, 3)
                    c2(t + 2, 2)
                    c2(t + 3, 3)
                    c3(t + 2, 2)
                    c3(t + 3, 3)

            iteration(0, True, False, False)
            iteration(1, True, True, False)
            pe.wait_ge(s["ready2"], 1)
            with pe.Fori(2, B, 1) as i:
                iteration(i, True, True, True)
            iteration(B, False, True, True)
            iteration(B + 1, False, False, True)

            pe.wait_ge(s["tables_ready"], 1)
            hbank = [(bank[4], bank[5]), (bank[0], bank[1])]

            def load_t(t, k):
                pe.wait_ge(tile_in[k], 16 * (t // 2 + 1) if isinstance(t, int) else t * 8 + 16 - 8 * k)
                for c in range(KC):
                    last = transpose(bank[2 + k][:, c * P:(c + 1) * P],
                                     x_in[k][:, c * P:(c + 1) * P], ident[:, :])
                last.then_inc(s["xr_t"], 1)

            def tile_step(t, k):
                fixed = isinstance(t, int)
                slot_at = None
                if not fixed or t < TILES:
                    need = pe.value_load(tab_need[0:1, bass.ds(t, 1)], min_val=0,
                                         max_val=NE + 1)
                    slot_at = pe.value_load(tab_slot[0:1, bass.ds(t, 1)], min_val=0,
                                            max_val=1) * W13
                    pe.wait_ge(s["ready13"], need)
                    pe.wait_ge(s["xr_lo_s"], t + 1)
                    if not fixed or t >= 2:
                        pe.wait_ge(s["d_prod"], t - 1)
                    hidden(xr_hi[k], xr_lo[k], slot_at, *hbank[k], chunks=range(KC // 2))
                if not fixed or t >= 1:
                    pe.wait_ge(s["d_act"], t)
                    if not fixed or t >= 2:
                        pe.wait_ge(s["d_lo"], t - 1)
                    hidden_t(h3[1 - k], bank[6]).then_inc(s["d_t"], 1)
                if not fixed or t < TILES:
                    hidden(xr_hi[k], xr_lo[k], slot_at, *hbank[k],
                           chunks=range(KC // 2, KC)).then_inc(s["d_h"], 1)
                if not fixed or t + 1 < TILES:
                    load_t(t + 1, 1 - k)
                if not fixed or t >= 1:
                    slot = pe.value_load(tab_slot[0:1, bass.ds(t - 1, 1)], min_val=0, max_val=1)
                    need = pe.value_load(tab_need[0:1, bass.ds(t - 1, 1)], min_val=0,
                                         max_val=NE + 1)
                    pe.wait_ge(s["ready2"], need)
                    pe.wait_ge(s["d_lo"], t)
                    if not fixed or t >= 2:
                        pe.wait_ge(s["d_y_e"], t - 1)
                    project(ht_hi[1 - k], ht_lo[1 - k], slot * W2, bank[7]).then_inc(s["d_y"], 1)

            load_t(0, 0)
            for t in range(3):
                tile_step(t, t % 2)
            with pe.Fori(3, TILES - 2, 2) as t:
                tile_step(t, 1)
                tile_step(t + 1, 0)
            for t in range(3 + 2 * len(range(3, TILES - 2, 2)), TILES + 1):
                tile_step(t, t % 2)

        @block.scalar
        def _(act):
            def copy(out, in_):
                return nc.scalar.activation(out, in_, ACT.Copy)

            act.wait_ge(s["consts"], 1)
            act.wait_ge(s["gates_in"], 48)
            nc.scalar.activation(gates[:, :], gates[:, :], ACT.Tanh).then_inc(s["gates_ready"], 1)
            act.wait_ge(s["gate_t"], 1)
            copy(gate_hi[:, :, :].rearrange("p c e -> p (c e)"), bank[0][:, 0:KC * NE]).then_inc(
                s["gate_hi_ready"], 1)

            def norm(b, n):
                act.wait_ge(s[f"ln_var{n}"], b + 1)
                nc.scalar.activation(small[n]["std"][:, :], small[n]["mean_var"][:, :, 1],
                                     ACT.Sqrt, bias=eps_ln[:, :]).then_inc(s[f"ln_std{n}"], 1)

            def smooth_root(b, L):
                act.wait_ge(s[f"ratio{L}"], b + 1)
                nc.scalar.activation(small[L]["ratio"][:, :], small[L]["ratio"][:, :],
                                     ACT.Sqrt).then_inc(s[f"s_raw{L}"], 1)

            def copy_s(b, L):
                act.wait_ge(s[f"bc{L}"], 2 * b + 2)
                copy(s_row[L][:, :], bank[2 * (L - 1)][:, 0:wide[L]]).then_inc(
                    s[f"s_copied{L}"], 1)

            def over_scales(b, L):
                act.wait_ge(s[f"scales{L}"], b + 1)
                for w, t, ready in ((1, wa[L], f"wt{L}"), (0, xa[L], f"xs{L}")):
                    for r in range(ROWS):
                        last = nc.scalar.activation(t[:, r, :], t[:, r, :], ACT.Copy,
                                                    scale=small[L]["q_inv"][:, w, r:r + 1])
                    last.then_inc(s[ready], 1)

            def quantised_copies(b, L):
                pairs = LINEARS[L] // 2
                n = 0
                for dst, t_done, t_read in ((wq_t[L], f"wq_t{L}", f"wq_e{L}"),
                                            (xq_t[L], f"xq_t{L}", f"xq_e{L}")):
                    for j in range(pairs):
                        act.wait_ge(s[t_done], pairs * b + j + 1)
                        copy(dst[:, 2 * j:2 * j + 2, :].rearrange("p c t -> p (c t)"),
                             bank[2 * (L - 1) + n % 2][:, :].bitcast(BF16)).then_inc(s[t_read], 1)
                        n += 1

            def weight_scales(b, L):
                act.wait_ge(s[f"wsc{L}"], b + 1)
                if L == 1:
                    copy(wscale1[:, :], bank[0][:, :]).then_inc(s["wsc_e1"], 1)
                else:
                    nc.scalar.activation(wscale2[:, :], bank[2][:, :], ACT.Copy,
                                         scale=gates[:, 0:1]).then_inc(s["wsc_e2"], 1)

            def first_out(b):
                for r in range(ROWS):
                    act.wait_ge(s["mm1"], ROWS * b + r + 1)
                    nc.scalar.activation(hid[:, r, :], bank[1 - r % 2][:, :], ACT.Copy,
                                         scale=small[1]["q_scale"][:, 0, r:r + 1]).then_inc(
                                             s["mm_e1"], 1)

            def silu_gate(b):
                act.wait_ge(s["gate_half"], b + 1)
                nc.scalar.activation(hid[:, :, 0:I], hid[:, :, 0:I], ACT.Silu).then_inc(
                    s["silu_gate"], 1)

            def normed_halves(b):
                for r in range(ROWS):
                    act.wait_ge(s["xn2_t"], ROWS * b + r + 1)
                    copy(xt_hi[:, r, :], bank[4 + r % 2][:, :]).then_inc(s["xn2_hi"], 1)

            def scores(b):
                act.wait_ge(s["logits"], b + 1)
                nc.scalar.activation(score[:, :], beside[:, 0:ROWS * NE], ACT.Exp,
                                     scale=-1.0).then_inc(s["exp_ready"], 1)

            def a1(t, r):
                act.wait_ge(s["sh_h"], t + 1)
                nc.scalar.activation(h1[r % 2][:, :], bank[4][:, 0:H], ACT.Silu).then_inc(
                    s["sh_h1"], 1)

            def a2(t, r):
                act.wait_ge(s["sh_t"], t + 1)
                copy(ht_hi[r % 2][:, :], bank[6][:, 0:len(HC) * P]).then_inc(s["sh_hi"], 1)

            expert_rows = expert_out.rearrange("(n t p) d -> n p t d", t=CLEAR, p=P)

            def clear_results(n):
                act.dma_start(expert_rows[bass.ds(n, 1)].rearrange("n p t d -> p (n t) d"),
                              zero_rows[:, 0:D].unsqueeze(1).to_broadcast([P, CLEAR, D])).then_inc(
                                  s["cleared"], 16)

            def iteration(i, first, second, shared):
                t = (i - 2) * ROWS
                linears = [2] * second + [1] * first
                if first and second:
                    for part in range(3):
                        clear_results((i - 1) * 3 + part)
                if shared:
                    norm(i - 2, 2)
                if first:
                    norm(i, 1)
                if shared:
                    normed_halves(i - 2)
                for L in linears:
                    smooth_root(i + 1 - L, L)
                for L in linears:
                    copy_s(i + 1 - L, L)
                if second:
                    over_scales(i - 1, 2)
                if shared:
                    scores(i - 2)
                    a1(t, 0)
                if first:
                    over_scales(i, 1)
                if second:
                    quantised_copies(i - 1, 2)
                if shared:
                    a1(t + 1, 1)
                if second:
                    weight_scales(i - 1, 2)
                if first:
                    quantised_copies(i, 1)
                if shared:
                    a2(t, 0)
                    a2(t + 1, 1)
                    a1(t + 2, 2)
                if first:
                    weight_scales(i, 1)
                    first_out(i)
                if shared:
                    a1(t + 3, 3)
                    a2(t + 2, 2)
                    a2(t + 3, 3)
                if first:
                    silu_gate(i)

            iteration(0, True, False, False)
            iteration(1, True, True, False)
            with act.Fori(2, B, 1) as i:
                iteration(i, True, True, True)
            iteration(B, False, True, True)
            iteration(B + 1, False, False, True)

            def tile_step(t, k):
                fixed = isinstance(t, int)
                if not fixed or t >= 1:
                    act.wait_ge(s["d_t"], t)
                    copy(ht_hi[1 - k][:, :], bank[6][:, 0:len(HC) * P]).then_inc(s["d_hi"], 1)
                if not fixed or t < TILES:
                    act.wait_ge(s["d_h"], t + 1)
                    copy(h1[k][:, :], [bank[4], bank[0]][k][:, 0:H]).then_inc(s["d_h1"], 1)
                if not fixed or t + 1 < TILES:
                    act.wait_ge(s["xr_t"], t + 2)
                    copy(xr_hi[1 - k][:, :], bank[3 - k][:, :]).then_inc(s["xr_hi_s"], 1)
                if not fixed or t < TILES:
                    act.wait_ge(s["d_prod"], t + 1)
                    nc.scalar.activation(h3[k][:, :], h1[k][:, :], ACT.Silu).then_inc(
                        s["d_act"], 1)

            act.wait_ge(s["xr_t"], 1)
            act.wait_ge(s["tables_ready"], 1)
            copy(xr_hi[0][:, :], bank[2][:, :]).then_inc(s["xr_hi_s"], 1)
            for t in range(3):
                tile_step(t, t % 2)
            with act.Fori(3, TILES - 2, 2) as t:
                tile_step(t, 1)
                tile_step(t + 1, 0)
            for t in range(3 + 2 * len(range(3, TILES - 2, 2)), TILES + 1):
                tile_step(t, t % 2)

        @block.vector
        def _(dve):
            v = nc.vector
            chain = {"at": 0, "n": 0}
            LINKED = 49

            def step(ins):
                chain["n"] += 1
                ins.then_inc(s["dve_chain"], 1)

            def settle():
                dve.wait_ge(s["dve_chain"], chain["at"] + chain["n"])

            def link(ins):
                step(ins)
                settle()

            def wait_alone():
                dve.nop(nofuse=True)

            dve.wait_ge(s["gate_hi_ready"], 1)
            v.tensor_tensor(gate_lo[:, :, :].rearrange("p c e -> p (c e)"), bank[0][:, 0:KC * NE],
                            gate_hi[:, :, :].rearrange("p c e -> p (c e)").bitcast(F32),
                            ALU.subtract).then_inc(s["gate_lo_ready"], 1)
            link(v.memset(bank[6][:, 0:3 * P], 0.0))

            def norm(b, n, dst, ready):
                m = small[n]
                for r in range(ROWS):
                    last = v.bn_stats(m["stats"][:, r, :], acc_tile(b * ROWS + r))
                link(last)
                wait_alone()
                for r in range(ROWS):
                    last = v.bn_aggr(m["mean_var"][:, r, :], m["stats"][:, r, :])
                last.then_inc(s[f"ln_var{n}"], 1)
                dve.wait_ge(s[f"ln_std{n}"], b + 1)
                link(v.reciprocal(m["rstd"][:, :], m["std"][:, :]))
                for r in range(ROWS):
                    v.tensor_scalar(dst[:, r, 0:D], acc_tile(b * ROWS + r), m["mean_var"][:, r, 0:1],
                                    m["rstd"][:, r:r + 1], ALU.subtract, ALU.mult).then_inc(
                                        s[ready], 1)

            def column_max(b, which, L):
                for c in range(LINEARS[L]):
                    dve.wait_ge(s[f"{which}_t{L}"], LINEARS[L] * b + c + 1)
                    j = {"x": 0, "w": 1}[which]
                    v.tensor_reduce(small[L]["amax"][:, j, c:c + 1],
                                    bank[2 * (L - 1) + c % 2][:, :], AX.X, ALU.max,
                                    apply_absolute_value=True).then_inc(s[f"{which}_max{L}"], 1)

            def smoothing(b, L):
                m = small[L]
                dve.wait_ge(s[f"w_max{L}"], LINEARS[L] * (b + 1))
                dve.wait_ge(s[f"x_max{L}"], LINEARS[L] * (b + 1))
                link(v.tensor_scalar(m["amax"][:, :, :], m["amax"][:, :, :], Q_EPS, None, ALU.max))
                link(v.reciprocal(m["amax"][:, 1, :], m["amax"][:, 1, :]))
                v.tensor_tensor(m["ratio"][:, :], m["amax"][:, 0, :], m["amax"][:, 1, :],
                                ALU.mult).then_inc(s[f"ratio{L}"], 1)

            def smoothed(b, L):
                m = small[L]
                dve.wait_ge(s[f"s_raw{L}"], b + 1)
                link(v.tensor_scalar(m["smooth"][:, 0, :], m["ratio"][:, :], Q_EPS, None, ALU.max))
                v.reciprocal(m["smooth"][:, 1, :], m["smooth"][:, 0, :]).then_inc(
                    s[f"smooth{L}"], 1)

            def smooth_and_scale(b, L):
                k, m = wide[L], small[L]
                dve.wait_ge(s[f"bc{L}"], 2 * b + 1)
                link(v.tensor_tensor(xa[L][:, :, :], xa[L][:, :, :],
                                     bank[2 * L - 1][:, 0:k].unsqueeze(1).to_broadcast(
                                         [P, ROWS, k]), ALU.mult))
                step(v.tensor_reduce(m["row_max"][:, 0, :], xa[L][:, :, :], AX.X, ALU.max,
                                     apply_absolute_value=True))
                dve.wait_ge(s[f"ws_ready{L}"], b + 1)
                link(v.tensor_reduce(m["row_max"][:, 1, :], wa[L][:, :, :], AX.X, ALU.max,
                                     apply_absolute_value=True))
                link(v.tensor_scalar(m["q_scale"][:, :, :], m["row_max"][:, :, :], Q_EPS,
                                     1.0 / QMAX, ALU.max, ALU.mult))
                v.reciprocal(m["q_inv"][:, :, :], m["q_scale"][:, :, :]).then_inc(
                    s[f"scales{L}"], 1)

            def quantise(b, L):
                for t, q, scaled, ready in ((wa[L], wq[L], f"wt{L}", f"wq_ready{L}"),
                                            (xa[L], xq[L], f"xs{L}", f"xq_ready{L}")):
                    dve.wait_ge(s[scaled], b + 1)
                    link(v.tensor_scalar(t[:, :, :], t[:, :, :], -QMAX, ROUND, ALU.max, ALU.add))
                    v.tensor_scalar(q[:, :, :], t[:, :, :], ROUND, QMAX, ALU.subtract,
                                    ALU.min).then_inc(s[ready], 1)

            def second_out(b):
                dve.wait_ge(s["wsc_e2"], b + 1)
                for r in range(ROWS):
                    dve.wait_ge(s["mm2"], ROWS * b + r + 1)
                    if r >= 2:
                        dve.wait_ge(s["x1_done"], ROWS * b + r - 1)
                    elif not (isinstance(b, int) and b == 0):
                        dve.wait_ge(s["x1_done"], ROWS * b + r - 1)
                    v.scalar_tensor_tensor(lin2_out[:, r % 2, :], bank[3 - r % 2][:, :],
                                           small[2]["q_scale"][:, 0, r:r + 1], wscale2[:, :],
                                           ALU.mult, ALU.mult).then_inc(s["mm_e2"], 1)

            def normed(b):
                dve.wait_ge(s["x1_done"], ROWS * b + ROWS)
                dve.wait_ge(s["xn2_free"], b + 1)
                norm(b, 2, xn2, "xn2_ready")

            def low_halves(b):
                for r in range(ROWS):
                    dve.wait_ge(s["xn2_hi"], ROWS * b + r + 1)
                    v.tensor_tensor(xt_lo[:, r, :], bank[4 + r % 2][:, :],
                                    xt_hi[:, r, :].bitcast(F32), ALU.subtract).then_inc(
                                        s["xn2_lo"], 1)

            def sh_product(t, r):
                dve.wait_ge(s["sh_h1"], t + 1)
                v.tensor_tensor(h3[r % 2][:, :], h1[r % 2][:, :], bank[5][:, 0:H],
                                ALU.mult).then_inc(s["sh_prod"], 1)

            def sh_low(t, r):
                dve.wait_ge(s["sh_hi"], t + 1)
                v.tensor_tensor(ht_lo[r % 2][:, :], bank[6][:, 0:len(HC) * P],
                                ht_hi[r % 2][:, :].bitcast(F32), ALU.subtract).then_inc(
                                    s["sh_lo"], 1)

            def sh_add(t, r):
                dve.wait_ge(s["sh_y"], t + 1)
                v.scalar_tensor_tensor(acc_tile(t), bank[7][:, :], gates[:, 1:2], acc_tile(t),
                                       ALU.mult, ALU.add).then_inc(s["sh_y_e"], 1)

            def choose(b):
                dve.wait_ge(s["exp_ready"], b + 1)
                by_expert = score[:, :].rearrange("p (r e) -> p r e", r=ROWS)
                link(v.tensor_scalar(score[:, :], score[:, :], 1.0, None, ALU.add))
                link(v.reciprocal(score[:, :], score[:, :]))
                link(v.tensor_tensor(by_expert, by_expert,
                                     bias_e[:, :].unsqueeze(1).to_broadcast([P, ROWS, NE]),
                                     ALU.add))
                wait_alone()
                for r in range(ROWS):
                    step(v.max(top8[:, r, :], by_expert[:, r, :]))
                settle()
                wait_alone()
                for r in range(ROWS):
                    step(v.max_index(top8_at[:, r, :], top8[:, r, :], by_expert[:, r, :]))
                settle()
                link(v.tensor_copy(top_at[:, :].rearrange("p (r k) -> p r k", r=ROWS),
                                   top8_at[:, :, 0:TOPK]))
                link(v.tensor_tensor(
                    onehot[:, :].rearrange("p (j e) -> p j e", e=NE),
                    iota_e[:, :].unsqueeze(1).to_broadcast([P, ROWS * TOPK, NE]),
                    top_at[:, :].unsqueeze(2).to_broadcast([P, ROWS * TOPK, NE]),
                    ALU.is_equal))
                with nc.allow_low_precision("zeros and ones"):
                    v.tensor_reduce(
                        taken[:, :].rearrange("p (r e) -> p r e", r=ROWS),
                        onehot[:, :].rearrange("p (r k e) -> p r e k", r=ROWS, k=TOPK),
                        AX.X, ALU.add).then_inc(s["taken_ready"], 1)
                link(v.tensor_reduce(total4[:, :], top8[:, :, 0:TOPK], AX.X, ALU.add))

            def place_rows(b):
                by_expert = score[:, :].rearrange("p (r e) -> p r e", r=ROWS)
                by_taken = taken[:, :].rearrange("p (r e) -> p r e", r=ROWS)
                dve.wait_ge(s["taken_ready"], b + 1)
                wait_alone()
                link(v.reciprocal(total4[:, :], total4[:, :]))
                link(v.tensor_tensor(weight[:, :, :], by_expert,
                                     total4[:, :].unsqueeze(2).to_broadcast([P, ROWS, NE]),
                                     ALU.mult))
                link(v.tensor_tensor(weight[:, :, :], weight[:, :, :], by_taken, ALU.mult))
                step(v.tensor_scalar(xn2[:, :, D:ROW], weight[:, :, :], gates[:, 1:2], None,
                                     ALU.mult))
                link(v.tensor_tensor_scan(rank[:, :], not_first[:, :, :].rearrange(
                    "p r e -> p (r e)"), taken[:, :], 0.0, ALU.mult, ALU.add))
                link(v.tensor_tensor(rank[:, :], rank[:, :], taken[:, :], ALU.mult))
                shape = [P, ROWS, TOPK, NE]
                link(v.tensor_tensor(
                    onehot[:, :].rearrange("p (r k e) -> p r k e", r=ROWS, k=TOPK),
                    rank[:, :].rearrange("p (r e) -> p r e", r=ROWS).unsqueeze(2).to_broadcast(
                        shape),
                    iota_k[:, :].unsqueeze(1).unsqueeze(3).to_broadcast(shape), ALU.is_equal))
                step(v.tensor_copy(onehot_all[:, bass.ds(b * BE, BE)], onehot[:, :]))
                dve.wait_ge(s["prefix"], b + 1)
                link(v.tensor_tensor(pos[:, :].rearrange("p (r e) -> p r e", r=ROWS),
                                     beside[:, 0:ROWS * NE].rearrange("p (r e) -> p r e", r=ROWS),
                                     next_row[:, :].unsqueeze(1).to_broadcast([P, ROWS, NE]),
                                     ALU.add))
                step(v.tensor_tensor(next_row[:, :], next_row[:, :],
                                     beside[:, ROWS * NE:(ROWS + 1) * NE], ALU.add))
                step(v.tensor_tensor(
                    picked[:, :].rearrange("p (r k e) -> p r k e", r=ROWS, k=TOPK),
                    onehot[:, :].rearrange("p (r k e) -> p r k e", r=ROWS, k=TOPK),
                    pos[:, :].rearrange("p (r e) -> p r e", r=ROWS).unsqueeze(2).to_broadcast(
                        shape), ALU.mult))
                settle()
                link(v.tensor_reduce(row_f[:, :],
                                     picked[:, :].rearrange("p (j e) -> p j e", e=NE),
                                     AX.X, ALU.add))
                v.tensor_copy(row_u[:, :], row_f[:, :]).then_inc(s["rows_ready"], 1)
                link(v.tensor_copy(row_all[:, bass.ds(b * ROWS * TOPK, ROWS * TOPK)],
                                   row_f[:, :]))

            def iteration(i, first, second, shared, then=None):
                b = i - 2
                t = b * ROWS
                linears = [2] * second + [1] * first
                if shared:
                    normed(b)
                if second:
                    column_max(i - 1, "w", 2)
                if first:
                    dve.wait_ge(s["x_loaded"], 16 * i + 16)
                    norm(i, 1, xa1, "xn_ready")
                if shared:
                    low_halves(b)
                if second:
                    column_max(i - 1, "x", 2)
                if first:
                    column_max(i, "w", 1)
                    column_max(i, "x", 1)
                for L in linears:
                    smoothing(i + 1 - L, L)
                for L in linears:
                    smoothed(i + 1 - L, L)
                if second:
                    smooth_and_scale(i - 1, 2)
                if first:
                    smooth_and_scale(i, 1)
                if shared:
                    sh_product(t, 0)
                if second:
                    quantise(i - 1, 2)
                if shared:
                    choose(b)
                if first:
                    quantise(i, 1)
                if second:
                    second_out(i - 1)
                if shared:
                    place_rows(b)
                    if then:
                        v.tensor_copy(tab_pad[:, :], next_row[0:1, :]).then_inc(
                            s["pads_known"], 1)
                    sh_product(t + 1, 1)
                    sh_low(t, 0)
                if then:
                    then()
                if shared:
                    sh_low(t + 1, 1)
                    sh_product(t + 2, 2)
                    sh_add(t, 0)
                    sh_add(t + 1, 1)
                    sh_product(t + 3, 3)
                    sh_low(t + 2, 2)
                    sh_low(t + 3, 3)
                    sh_add(t + 2, 2)
                    sh_add(t + 3, 3)

            dve.nop(nofuse=True).then_inc(s["sh_prod"], ROWS)
            dve.wait_ge(s["gates_ready"], 1)
            dve.wait_ge(s["consts"], 1)
            chain["at"], chain["n"] = chain["n"], 0
            iteration(0, True, False, False)
            chain["at"], chain["n"] = chain["at"] + chain["n"], 0
            iteration(1, True, True, False)
            steps = LINKED
            start = chain["at"] + chain["n"]
            with dve.Fori(2, B, 1) as i:
                chain["at"], chain["n"] = start + (i - 2) * steps, 0
                iteration(i, True, True, True)
                assert chain["n"] == steps, chain["n"]
            chain["at"], chain["n"] = start + (B - 2) * steps, 0
            iteration(B, False, True, True)

            def tables():
                link(v.tensor_tensor(count[:, :], next_row[:, :], region_start[:, :], ALU.subtract))
                link(v.tensor_scalar(tiles_i[:, :], count[:, :], float(P - 1), None, ALU.add))
                link(v.tensor_scalar(tiles_i[:, :], tiles_i[:, :], 7, None,
                                     ALU.arith_shift_right))
                link(v.tensor_scalar(tiles_f[:, :], tiles_i[:, :], 1.0, None, ALU.max))
                link(v.tensor_tensor_scan(tile_end[:, :], one_e[:, :], tiles_f[:, :], 0.0, ALU.mult,
                                          ALU.add))
                link(v.tensor_tensor(tile_start[:, :], tile_end[:, :], tiles_f[:, :], ALU.subtract))
                link(v.tensor_copy(tab_start[:, :], tile_start[0:1, :]))
                link(v.tensor_scalar(tab_stored[:, 0, :], tab_start[:, :], 1.0, None, ALU.add))
                link(v.tensor_copy(tab_stored[:, 1, :], tab_start[:, :]))
                link(v.tensor_scalar(tab_stored[:, :, :], tab_stored[:, :, :], 1, 4,
                                     ALU.arith_shift_right, ALU.logical_shift_left))
                row3 = [1, TILES, NE]
                link(v.tensor_tensor(begun[:, :, :], tile_start[0:1, :].unsqueeze(1).to_broadcast(row3),
                                     iota_t[:, :].unsqueeze(2).to_broadcast(row3), ALU.is_le))
                link(v.tensor_reduce(tile_expert[:, :], begun[:, :, :], AX.X, ALU.add))
                link(v.tensor_tensor(begun[:, :, :], begun[:, :, :],
                                     tile_start[0:1, :].unsqueeze(1).to_broadcast(row3), ALU.mult))
                link(v.tensor_reduce(tile_first[:, :], begun[:, :, :], AX.X, ALU.max))
                link(v.tensor_scalar(tab_need[:, :], tile_expert[:, :], 1.0, None, ALU.add))
                link(v.tensor_scalar(tab_expert[:, :], tile_expert[:, :], 1.0, None, ALU.subtract))
                link(v.tensor_copy(tab_slot[:, :], tile_expert[:, :]))
                link(v.tensor_scalar(tab_slot[:, :], tab_slot[:, :], 1, None, ALU.bitwise_and))
                link(v.tensor_scalar(tile_live[:, :], iota_t[:, :], tile_end[0:1, NE - 1:NE], float(P),
                                     ALU.is_lt, ALU.mult))
                link(v.tensor_tensor(tile_tmp[:, :], iota_t[:, :], tile_first[:, :], ALU.subtract))
                link(v.tensor_tensor(tile_tmp[:, :], tile_tmp[:, :], tile_live[:, :], ALU.mult))
                link(v.tensor_scalar(tile_expert[:, :], tile_expert[:, :], 1.0, float(REGION),
                                     ALU.subtract, ALU.mult))
                v.tensor_tensor(tab_row[:, :], tile_tmp[:, :], tile_expert[:, :],
                                ALU.add).then_inc(s["tables_ready"], 1)

            iteration(B + 1, False, False, True, tables)

            link(v.tensor_scalar(shift_e[:, :], tile_start[:, :], float(P), None, ALU.mult))
            link(v.tensor_tensor(shift_e[:, :], shift_e[:, :], region_start[:, :], ALU.subtract))
            link(v.tensor_tensor(
                shifted[:, :, :], onehot_all[:, :].rearrange("p (j e) -> p j e", e=NE),
                shift_e[:, :].unsqueeze(1).to_broadcast([P, TT * TOPK, NE]), ALU.mult))
            link(v.tensor_reduce(out_row_f[:, :], shifted[:, :, :], AX.X, ALU.add))
            link(v.tensor_tensor(out_row_f[:, :], out_row_f[:, :], row_all[:, :], ALU.add))
            v.tensor_copy(out_row[:, :], out_row_f[:, :]).then_inc(s["out_rows_known"], 1)

            def low_rows(t, k):
                expert = dve.value_load(tab_expert[0:1, bass.ds(t, 1)], min_val=0, max_val=NE - 1)
                dve.wait_ge(s["xr_hi_s"], t + 1)
                v.tensor_tensor(xr_lo[k][:, :], bank[2 + k][:, :], xr_hi[k][:, :].bitcast(F32),
                                ALU.subtract).then_inc(s["xr_lo_s"], 1)
                v.tensor_copy(tile_weight[:, bass.ds(t, 1)],
                              x_in[k][:, bass.ds(expert + D, 1)]).then_inc(s["weight_picked"], 1)

            def tile_step(t, k):
                fixed = isinstance(t, int)
                if not fixed or t >= 1:
                    dve.wait_ge(s["d_hi"], t)
                    v.tensor_tensor(ht_lo[1 - k][:, :], bank[6][:, 0:len(HC) * P],
                                    ht_hi[1 - k][:, :].bitcast(F32), ALU.subtract).then_inc(
                                        s["d_lo"], 1)
                if not fixed or t < TILES:
                    dve.wait_ge(s["d_h1"], t + 1)
                    v.tensor_tensor(h1[k][:, :], h1[k][:, :], [bank[5], bank[1]][k][:, 0:H],
                                    ALU.mult).then_inc(s["d_prod"], 1)
                if not fixed or t + 1 < TILES:
                    low_rows(t + 1, 1 - k)
                if not fixed or t >= 1:
                    dve.wait_ge(s["d_y"], t)
                    if not fixed or t >= 3:
                        dve.wait_ge(y_stored[1 - k], (t + (k - 2)) * 8)
                    dve.wait_ge(s["weight_picked"], t)
                    wait_alone()
                    v.tensor_scalar(y_out[1 - k][:, :], bank[7][:, :],
                                    tile_weight[:, bass.ds(t - 1, 1)], None, ALU.mult).then_inc(
                                        s["d_y_e"], 1)

            low_rows(0, 0)
            for t in range(3):
                tile_step(t, t % 2)
            with dve.Fori(3, TILES - 2, 2) as t:
                tile_step(t, 1)
                tile_step(t + 1, 0)
            for t in range(3 + 2 * len(range(3, TILES - 2, 2)), TILES + 1):
                tile_step(t, t % 2)


_INS = ["x", "fside_BxS2xS2_0", "ctx_1024", "g_xattn", "g_ffn", "L0_ffn_gate_w", "L0_ffn_gate_b",
        "L0_ffn_w1_shared", "L0_ffn_w2_shared", "L0_ffn_w3_shared", "L0_ffn_w1_routed",
        "L0_ffn_w2_routed", "L0_ffn_w3_routed"]
_OUTS = [((4, 512, 512), "float32")]


def kernel(**inputs):
    import numpy as _np
    import concourse.bacc as _bacc
    from concourse import mybir as _mybir
    from concourse.bass_utils import run_bass_kernel_spmd as _run

    nc = _bacc.Bacc("TRN2", target_bir_lowering=False, num_devices=1)
    arrays, args = {}, []
    for name in _INS:
        a = _np.ascontiguousarray(inputs[name])
        arrays[f"in_{name}_dram"] = a
        args.append(nc.dram_tensor(f"in_{name}_dram", a.shape, _mybir.dt.from_np(a.dtype),
                                   kind="ExternalInput").ap())
    for i, (shape, dtype) in enumerate(_OUTS):
        args.append(nc.dram_tensor(f"out_{i}_dram", shape, _mybir.dt.from_np(_np.dtype(dtype)),
                                   kind="ExternalOutput").ap())
    flamingo_moe(nc, *args)
    r = _run(nc, [arrays], core_ids=[0])
    return r.results[0]["out_0_dram"]
```

```python
from contextlib import ExitStack

import concourse.bass as bass
from concourse import mybir

F32 = mybir.dt.float32
F32R = mybir.dt.float32r
BF16 = mybir.dt.bfloat16
I32 = mybir.dt.int32
U32 = mybir.dt.uint32
SIZE = {F32: 4, F32R: 4, BF16: 2, I32: 4, U32: 4}
ALU = mybir.AluOpType
ACT = mybir.ActivationFunctionType
AX = mybir.AxisListType

P = 128
TOPK = 4
QMAX = 127.0
Q_EPS = 1e-6
LN_EPS = 1e-5
ROUND = 1.5 * 2.0**23
ROWS = 4


def flamingo_moe(nc, x, w_gate_up, w_down, g_xattn, g_ffn, gate_w, gate_b, w1_shared, w2_shared,
                 w3_shared, w1_routed, w2_routed, w3_routed, out):
    B, S, D = x.shape
    I = w_down.shape[2]
    NE, _, H = w1_routed.shape
    TOK = B * S
    KC = D // P
    TT = TOK // P
    HSTEP = (H - P) // 2
    HC = [(0, HSTEP), (HSTEP, HSTEP), (2 * HSTEP, P)]
    assert S == ROWS * P and D == 4 * P and I == 2 * P
    assert 2 * P < H < 3 * P and H % 2 == 0 and NE == 16
    TILES = (TOK * TOPK + NE * (P - 1)) // P
    CLEARS = 3 * (B - 1)
    CLEAR = (TILES + CLEARS - 1) // CLEARS
    REGION = P + TOK
    W13 = KC * 2 * H
    W2 = len(HC) * D
    ROW = D + NE
    LINEARS = {1: KC, 2: I // P}
    SCATTERS = ROWS * TOPK
    BE = ROWS * TOPK * NE

    x_rows = x.rearrange("b (r p) d -> b p r d", p=P)
    out_rows = out.rearrange("b (r p) d -> (b r) p d", p=P)
    dispatched = nc.dram_tensor("dispatched", [NE * REGION, ROW], F32, kind="Internal").ap()
    expert_out = nc.dram_tensor("expert_out", [CLEARS * CLEAR * P, D], F32, kind="Internal").ap()

    with ExitStack() as ctx:
        place = [(nc.sbuf_base + 31) // 32 * 32]

        def sb(name, shape, dt, at=None):
            n = SIZE[dt]
            for s in shape[1:]:
                n *= s
            where = place[0] if at is None else at
            if at is None:
                place[0] += (n + 31) // 32 * 32
            assert where + n <= nc.sbuf_usable_end, (name, where, n)
            return nc.alloc_sbuf_tensor_at(name, shape, dt, offset=where)

        def sem(name):
            return ctx.enter_context(nc.semaphore(name))

        bank = [ctx.enter_context(nc.psum_tensor(f"bank{i}", [P, 512], F32)) for i in range(8)]
        beside = bank[6][:, len(HC) * P:512]

        ident = sb("ident", [P, P], F32)
        ident_b = sb("ident_b", [P, P], BF16)
        ones_b = sb("ones_b", [P, P], BF16)
        before_b = sb("before_b", [P, P], BF16)
        iota_e = sb("iota_e", [P, NE], F32)
        first_row = sb("first_row", [P, NE], F32)
        one_e = sb("one_e", [P, NE], F32)
        not_first = sb("not_first", [P, ROWS, NE], F32)
        iota_k = sb("iota_k", [P, TOPK], F32)
        eps_ln = sb("eps_ln", [P, 1], F32)
        gates = sb("gates", [P, 2], F32)
        bias_e = sb("bias_e", [P, NE], F32)
        gate_rows_at = place[0]
        gate_rows = sb("gate_rows", [NE, D], F32)
        gate_hi = sb("gate_hi", [P, KC, NE], F32R)
        gate_lo = sb("gate_lo", [P, KC, NE], F32R)

        acc = sb("acc", [P, TT * D], F32)
        ring_at = place[0]
        ring13_hi = sb("ring13_hi", [P, 2 * W13], F32R)
        ring13_lo = sb("ring13_lo", [P, 2 * W13], F32R)
        ring2_hi = sb("ring2_hi", [P, 2 * W2], F32R)
        ring2_lo = sb("ring2_lo", [P, 2 * W2], F32R)
        raw13 = sb("raw13", [P, KC, 2, H], F32)
        raw2 = sb("raw2", [P, len(HC), D], F32)

        onehot_all = sb("onehot_all", [P, TT * TOPK * NE], F32)
        row_all = sb("row_all", [P, TT * TOPK], F32)
        logits_t = sb("logits_t", [NE, ROWS * P], F32, at=gate_rows_at)
        score = sb("score", [P, ROWS * NE], F32)
        top8 = sb("top8", [P, ROWS, 8], F32)
        top8_at = sb("top8_at", [P, ROWS, 8], U32)
        top_at = sb("top_at", [P, ROWS * TOPK], F32)
        onehot = sb("onehot", [P, BE], F32)
        taken = sb("taken", [P, ROWS * NE], BF16)
        total4 = sb("total4", [P, ROWS], F32)
        rank = sb("rank", [P, ROWS * NE], F32)
        weight = sb("weight", [P, ROWS, NE], F32)
        next_row = sb("next_row", [P, NE], F32)
        pos = sb("pos", [P, ROWS * NE], F32)
        picked = sb("picked", [P, BE], F32)
        row_f = sb("row_f", [P, ROWS * TOPK], F32)
        row_u = sb("row_u", [P, ROWS * TOPK], U32)

        shifted_at = place[0]
        xt_hi = sb("xt_hi", [P, ROWS, KC * P], F32R)
        xt_lo = sb("xt_lo", [P, ROWS, KC * P], F32R)
        h1 = [sb(f"h1_{i}", [P, H], F32) for i in range(2)]
        h3 = [sb(f"h3_{i}", [P, H], F32) for i in range(2)]
        ht_hi = [sb(f"ht_hi{i}", [P, len(HC) * P], F32R) for i in range(2)]
        ht_lo = [sb(f"ht_lo{i}", [P, len(HC) * P], F32R) for i in range(2)]

        slot1 = [ring_at + W13 * 4, ring_at + 3 * W13 * 4, ring_at + (4 * W13 + W2) * 4,
                 ring_at + (4 * W13 + 3 * W2) * 4]
        xa1 = sb("xa1", [P, ROWS, D], F32, at=slot1[0])
        wscale1 = sb("wscale1", [P, D], F32, at=slot1[0] + ROWS * D * 4)
        wa1 = sb("wa1", [P, ROWS, D], F32, at=slot1[1])
        s_row1 = sb("s_row1", [P, D], F32, at=slot1[1] + ROWS * D * 4)
        xq1 = sb("xq1", [P, ROWS, D], BF16, at=slot1[2])
        wq1 = sb("wq1", [P, ROWS, D], BF16, at=slot1[3])
        assert ROWS * D * 4 + D * 4 <= W13 * 4 and ROWS * D * 2 <= W2 * 4
        hid_at = place[0]
        hid = sb("hid", [P, ROWS, D], F32)
        xq_t1 = sb("xq_t1", [P, KC, ROWS * P], BF16)
        wq_t1 = sb("wq_t1", [P, KC, ROWS * P], BF16)

        second = place[0]
        wa2 = sb("wa2", [P, ROWS, I], F32)
        xa2 = sb("xa2", [P, ROWS, I], F32)
        lin2_out = sb("lin2_out", [P, 2, D], F32)
        xq2 = sb("xq2", [P, ROWS, I], BF16)
        wq2 = sb("wq2", [P, ROWS, I], BF16)
        xq_t2 = sb("xq_t2", [P, 2, ROWS * P], BF16)
        wq_t2 = sb("wq_t2", [P, 2, ROWS * P], BF16)
        wscale2 = sb("wscale2", [P, D], F32)
        s_row2 = sb("s_row2", [P, I], F32)
        end_second = place[0]
        more_out = xa2[:, :, :].rearrange("p r i -> p (r i)").rearrange("p (r d) -> p r d", d=D)
        out2 = [lin2_out[:, 0, :], lin2_out[:, 1, :], more_out[:, 0, :], more_out[:, 1, :]]
        xn2 = sb("xn2", [P, ROWS, ROW], F32)

        small = {}
        for L, k in LINEARS.items():
            small[L] = {
                "stats": sb(f"stats{L}", [P, ROWS, 6], F32),
                "mean_var": sb(f"mean_var{L}", [P, ROWS, 2], F32),
                "std": sb(f"std{L}", [P, ROWS], F32),
                "rstd": sb(f"rstd{L}", [P, ROWS], F32),
                "amax": sb(f"amax{L}", [P, 2, k], F32),
                "ratio": sb(f"ratio{L}", [P, k], F32),
                "smooth": sb(f"smooth{L}", [P, 2, k], F32),
                "row_max": sb(f"row_max{L}", [P, 2, ROWS], F32),
                "q_scale": sb(f"q_scale{L}", [P, 2, ROWS], F32),
                "q_inv": sb(f"q_inv{L}", [P, 2, ROWS], F32),
            }
        wide = {1: D, 2: I}
        xa, wa = {1: xa1, 2: xa2}, {1: wa1, 2: wa2}
        xq, wq = {1: xq1, 2: xq2}, {1: wq1, 2: wq2}
        xq_t, wq_t = {1: xq_t1, 2: xq_t2}, {1: wq_t1, 2: wq_t2}
        wscale, s_row = {1: wscale1, 2: wscale2}, {1: s_row1, 2: s_row2}

        zero_rows = sb("zero_rows", [P, ROW], F32)
        tile_weight = sb("tile_weight", [P, TILES], F32)
        iota_t = sb("iota_t", [1, TILES], F32)
        end = place[0]
        place[0] = hid_at
        shifted = sb("shifted", [P, TT * TOPK, NE], F32, at=shifted_at)
        count = sb("count", [P, NE], F32)
        tiles_i = sb("tiles_i", [P, NE], I32)
        tiles_f = sb("tiles_f", [P, NE], F32)
        tile_end = sb("tile_end", [P, NE], F32)
        tile_start = sb("tile_start", [P, NE], F32)
        row_base = sb("row_base", [P, NE], F32)
        out_row_f = sb("out_row_f", [P, TT * TOPK], F32)
        out_row = sb("out_row", [P, TT * TOPK], U32)
        tile_expert = sb("tile_expert", [1, TILES], F32)
        tile_base = sb("tile_base", [1, TILES], F32)
        last_tile = sb("last_tile", [1, 1], F32)
        tab_row = sb("tab_row", [1, TILES], I32)
        tab_slot = sb("tab_slot", [1, TILES], I32)
        tab_need = sb("tab_need", [1, TILES], I32)
        tab_start = sb("tab_start", [1, NE], I32)
        tab_expert = sb("tab_expert", [1, TILES], I32)
        tab_stored = sb("tab_stored", [1, 2, NE], I32)
        xn2_last = sb("xn2_last", [P, ROWS, ROW], F32)
        assert place[0] <= second
        place[0] = end

        end = place[0]
        place[0] = second
        x_in = [sb(f"x_in{i}", [P, ROW], F32) for i in range(2)]
        y_out = [sb(f"y_out{i}", [P, D], F32) for i in range(2)]
        xr_hi = [sb(f"xr_hi{i}", [P, KC * P], F32R) for i in range(2)]
        xr_lo = [sb(f"xr_lo{i}", [P, KC * P], F32R) for i in range(2)]
        begun = sb("begun", [1, TILES, NE], F32)
        assert place[0] <= end_second
        place[0] = end

        names = (
            "consts gates_in gate_rows_in gates_ready gate_t gate_hi_ready gate_lo_ready "
            "x_loaded wa1_loaded wa2_loaded ln_var1 ln_var2 ln_std1 ln_std2 xn_ready "
            "w_t1 w_t2 x_t1 x_t2 w_max1 w_max2 x_max1 x_max2 ratio1 ratio2 s_raw1 s_raw2 "
            "smooth1 smooth2 bc1 bc2 s_copied1 s_copied2 ws_ready1 ws_ready2 scales1 scales2 "
            "wt1 wt2 xs1 xs2 wq_ready1 wq_ready2 xq_ready1 xq_ready2 wq_t1 wq_t2 wq_e1 wq_e2 "
            "xq_t1 xq_t2 xq_e1 xq_e2 wsc1 wsc2 wsc_e1 wsc_e2 mm1 mm2 mm_e1 mm_e2 "
            "gate_half up_half silu_gate a_ready x1_done xn2_ready xn2_t xn2_hi xn2_lo "
            "logits_by_expert logits_copied logits "
            "exp_ready taken_ready prefix rows_ready scattered dve_chain pool_chain "
            "raw1_in raw3_in raw2_in hi1_in hi3_in hi2_in ready1 ready3 ready2 "
            "sh_h sh_h1 sh_prod sh_t sh_hi sh_lo "
            "sh_y sh_y_e out_rows_known tables_ready pads_written xr_t xr_hi_s xr_lo_s "
            "d_h d_h1 d_prod d_act d_t d_hi d_lo d_y d_y_e weight_picked cleared gathered out_stored"
        ).split()
        s = {n: sem("s_" + n) for n in names}
        tile_in = [sem(f"s_tile_in{i}") for i in range(2)]
        y_stored = [sem(f"s_y_stored{i}") for i in range(2)]
        last_gathered = [sem(f"s_last_gathered{i}") for i in range(TT)]

        def xn2_of(b):
            return xn2_last if b == B - 1 else xn2

        def acc_tile(t):
            return acc[:, bass.ds(t * D, D)]

        def ring13(half, slot_at, c, m):
            return half[:, bass.ds(slot_at + (c * 2 + m) * H, H)]

        def ring2(half, slot_at, c):
            return half[0:HC[c][1], bass.ds(slot_at + c * D, D)]

        STEPS = B + 3

        def parts(i):
            return i < B, 1 <= i <= B, 2 <= i <= B + 1, i >= 3

        block = ctx.enter_context(nc.Block())

        @block.sync
        def _(sp):
            sp.dma_start(gates[:, 0:1], g_xattn.partition_broadcast(P)).then_inc(s["gates_in"], 16)
            sp.dma_start(gates[:, 1:2], g_ffn.partition_broadcast(P)).then_inc(s["gates_in"], 16)
            sp.dma_start(bias_e[:, :], gate_b.partition_broadcast(P)).then_inc(s["gates_in"], 16)
            sp.dma_start(gate_rows[:, :], gate_w).then_inc(s["gate_rows_in"], 16)

            def load_batch(b):
                xb = x_rows[bass.ds(b, 1)].rearrange("a p r d -> (a p) r d")
                sp.dma_start(acc[:, bass.ds(b * ROWS * D, ROWS * D)].rearrange(
                    "p (r d) -> p r d", r=ROWS), xb).then_inc(s["x_loaded"], 16)

            def load_weights(b):
                src = w_gate_up[bass.ds(b, 1)].rearrange("a (r p) d -> p (a r) d", p=P)
                sp.dma_start(wa1[:, :, :], src).then_inc(s["wa1_loaded"], 16)

            def load_down(b):
                src = w_down[bass.ds(b, 1)].rearrange("a (r p) d -> p (a r) d", p=P)
                sp.dma_start(wa2[:, :, :], src).then_inc(s["wa2_loaded"], 16)

            load_batch(0)
            load_weights(0)
            sp.wait_ge(s["consts"], 1)
            load_down(0)
            with sp.Fori(1, B, 1) as b:
                sp.wait_ge(s["ln_var1"], b)
                load_batch(b)
                sp.wait_ge(s["wq_ready1"], b)
                load_weights(b)
                sp.wait_ge(s["wq_ready2"], b)
                load_down(b)

            sp.dma_start(dispatched.rearrange("(e q) d -> q e d", e=NE)[0:P, :, :],
                         zero_rows[:, :].unsqueeze(1).to_broadcast([P, NE, ROW])).then_inc(
                             s["pads_written"], 16)
            sp.wait_ge(s["tables_ready"], 1)
            sp.wait_ge(s["pads_written"], 16)
            sp.wait_ge(s["scattered"], 16 * SCATTERS * B)
            sp.wait_ge(s["cleared"], 16 * CLEARS)

            def load_tile(t, k):
                row = sp.value_load(tab_row[0:1, bass.ds(t, 1)], min_val=0,
                                    max_val=NE * REGION - P)
                sp.dma_start(x_in[k][:, :], dispatched[bass.ds(row, P), :]).then_inc(tile_in[k], 16)

            def store_tile(t, k):
                sp.dma_start(expert_out[bass.ds(t * P, P), :], y_out[k][:, :]).then_inc(
                    y_stored[k], 16)

            load_tile(0, 0)
            load_tile(1, 1)
            for t in range(2, 4):
                sp.wait_ge(s["xr_t"], t - 1)
                sp.wait_ge(s["weight_picked"], t - 1)
                load_tile(t, t % 2)
            with sp.Fori(0, TILES - 5, 2) as t:
                for k in range(2):
                    sp.wait_ge(s["xr_t"], t + (k + 3))
                    sp.wait_ge(s["weight_picked"], t + (k + 3))
                    load_tile(t + (k + 4), k)
                    sp.wait_ge(s["d_y_e"], t + (k + 1))
                    store_tile(t + k, k)
            for t in range(2 * len(range(0, TILES - 5, 2)), TILES):
                if t + 4 < TILES:
                    sp.wait_ge(s["xr_t"], t + 3)
                    sp.wait_ge(s["weight_picked"], t + 3)
                    load_tile(t + 4, t % 2)
                sp.wait_ge(s["d_y_e"], t + 1)
                store_tile(t, t % 2)

            for k in range(2):
                sp.wait_ge(y_stored[k], 16 * ((TILES + 1 - k) // 2))
            sp.wait_ge(s["out_stored"], 16 * TT)

        @block.gpsimd
        def _(pool):
            g = nc.gpsimd
            own = [0]

            def done(ins):
                own[0] += 1
                ins.then_inc(s["pool_chain"], 1)

            def fence():
                pool.wait_ge(s["pool_chain"], own[0])

            def wait_alone():
                pool.nop(nofuse=True)

            done(g.memset(ident[:, :], 0.0))
            done(g.memset(ident_b[:, :], 0.0))
            done(g.memset(before_b[:, :], 1.0))
            done(g.memset(ones_b[:, :], 1.0))
            done(g.memset(one_e[:, :], 1.0))
            done(g.memset(eps_ln[:, :], LN_EPS))
            done(g.memset(not_first[:, :, :], 1.0))
            done(g.memset(raw2[:, 0:2, :], 0.0))
            fence()
            done(g.affine_select(out=ident[:, :], in_=ident[:, :], compare_op=ALU.not_equal,
                                 fill=1.0, base=0, pattern=[[-1, P]], channel_multiplier=1))
            done(g.affine_select(out=ident_b[:, :], in_=ident_b[:, :], compare_op=ALU.not_equal,
                                 fill=1.0, base=0, pattern=[[-1, P]], channel_multiplier=1))
            done(g.affine_select(out=before_b[:, :], in_=before_b[:, :], compare_op=ALU.is_gt,
                                 fill=0.0, base=0, pattern=[[1, P]], channel_multiplier=-1))
            done(g.iota(iota_e[:, :], [[1, NE]], base=0, channel_multiplier=0,
                        allow_small_or_imprecise_dtypes=True))
            done(g.iota(first_row[:, :], [[REGION, NE]], base=P, channel_multiplier=0,
                        allow_small_or_imprecise_dtypes=True))
            fence()
            done(g.memset(not_first[:, :, 0:1], 0.0))
            done(g.iota(iota_k[:, :], [[1, TOPK]], base=1, channel_multiplier=0,
                        allow_small_or_imprecise_dtypes=True))
            done(g.memset(zero_rows[:, :], 0.0))
            done(g.iota(iota_t[0:1, :], [[1, TILES]], base=0, channel_multiplier=0,
                        allow_small_or_imprecise_dtypes=True))
            fence()
            g.iota(next_row[:, :], [[REGION, NE]], base=P, channel_multiplier=0,
                   allow_small_or_imprecise_dtypes=True).then_inc(s["consts"], 1)

            def load_hidden(m, w):
                pool.dma_start(raw13[:, :, m, :], w.rearrange("(c p) h -> p c h", p=P)).then_inc(
                    s[("raw1_in", "raw3_in")[m]], 16)

            def load_out(w2):
                pool.dma_start(raw2[0:HSTEP, 0:2, :], w2[0:2 * HSTEP, :].rearrange(
                    "(c p) n -> p c n", c=2)).then_inc(s["raw2_in"], 16)
                pool.dma_start(raw2[:, 2, :], w2[2 * HSTEP:H, :]).then_inc(s["raw2_in"], 16)

            def load_routed(e):
                def part(which):
                    w = {1: w1_routed, 3: w3_routed, 2: w2_routed}[which]
                    w = w[bass.ds(e, 1)].rearrange("a d h -> (a d) h")
                    load_out(w) if which == 2 else load_hidden(which // 2, w)
                return part

            def split_hidden(n, slot, m):
                hi, lo = (ring[:, slot * W13:(slot + 1) * W13].rearrange(
                    "p (c m h) -> p c m h", c=KC, m=2)[:, :, m, :]
                    for ring in (ring13_hi, ring13_lo))
                pool.wait_ge(s[("hi1_in", "hi3_in")[m]], 16 * n + 16)
                g.tensor_tensor(lo, raw13[:, :, m, :], hi.bitcast(F32),
                                ALU.subtract).then_inc(s[("ready1", "ready3")[m]], 1)

            def fill(n, slot, free13, free2, load_next):
                raw_2 = raw2[:, :, :].rearrange("p c n -> p (c n)")
                at2 = slot * W2
                free13()
                wait_alone()
                for m in range(2):
                    pool.wait_ge(s[("raw1_in", "raw3_in")[m]], 16 * n + 16)
                    wait_alone()
                    pool.dma_start(ring13_hi[:, slot * W13:(slot + 1) * W13].rearrange(
                        "p (c m h) -> p c m h", c=KC, m=2)[:, :, m, :],
                        raw13[:, :, m, :]).then_inc(s[("hi1_in", "hi3_in")[m]], 16)
                split_hidden(n, slot, 0)
                pool.wait_ge(s["raw2_in"], 32 * n + 32)
                free2()
                wait_alone()
                pool.dma_start(ring2_hi[:, at2:at2 + W2], raw_2).then_inc(s["hi2_in"], 16)
                split_hidden(n, slot, 1)
                pool.wait_ge(s["ready1"], n + 1)
                wait_alone()
                load_next(1)
                pool.wait_ge(s["ready3"], n + 1)
                wait_alone()
                load_next(3)
                pool.wait_ge(s["hi2_in"], 16 * n + 16)
                g.tensor_tensor(ring2_lo[:, at2:at2 + W2], raw_2,
                                ring2_hi[:, at2:at2 + W2].bitcast(F32),
                                ALU.subtract).then_inc(s["ready2"], 1)
                pool.wait_ge(s["ready2"], n + 1)
                wait_alone()
                load_next(2)

            def free():
                pass

            load_hidden(0, w1_shared)
            load_hidden(1, w3_shared)
            load_out(w2_shared)

            def smoothed_weights(b, L):
                k = wide[L]
                pool.wait_ge(s[f"s_copied{L}"], b + 1)
                g.tensor_tensor(wa[L][:, :, :], wa[L][:, :, :],
                                s_row[L][:, :].unsqueeze(1).to_broadcast([P, ROWS, k]),
                                ALU.mult).then_inc(s[f"ws_ready{L}"], 1)

            def hidden_rows(b):
                pool.wait_ge(s["wsc_e1"], b + 1)
                pool.wait_ge(s["mm_e1"], ROWS * b + ROWS)
                for at, ready in ((0, "gate_half"), (I, "up_half")):
                    g.tensor_tensor(hid[:, :, at:at + I], hid[:, :, at:at + I],
                                    wscale1[:, at:at + I].unsqueeze(1).to_broadcast([P, ROWS, I]),
                                    ALU.mult).then_inc(s[ready], 1)
                pool.wait_ge(s["up_half"], b + 1)
                pool.wait_ge(s["silu_gate"], b + 1)
                g.tensor_tensor(xa2[:, :, :], hid[:, :, 0:I], hid[:, :, I:2 * I],
                                ALU.mult).then_inc(s["a_ready"], 1)

            def residual(b):
                for r in range(ROWS):
                    pool.wait_ge(s["mm_e2"], ROWS * b + r + 1)
                    t = b * ROWS + r
                    g.tensor_tensor(acc_tile(t), out2[r], acc_tile(t),
                                    ALU.add).then_inc(s["x1_done"], 1)

            def scatter(b, these):
                pool.wait_ge(s["rows_ready"], b + 1)
                for j in these:
                    g.indirect_dma_start(
                        out=dispatched, out_offset=bass.IndirectOffsetOnAxis(
                            ap=row_u[:, j:j + 1], axis=0),
                        in_=xn2_of(b)[:, j // TOPK, :], in_offset=None).then_inc(s["scattered"], 16)

            for i in range(STEPS):
                first, second, shared, _ = parts(i)
                if second:
                    smoothed_weights(i - 1, 2)
                if first:
                    smoothed_weights(i, 1)
                if i == 0:
                    fill(0, 0, free, free, load_routed(0))
                if i == B:
                    fill(1, 1, free, free, load_routed(1))
                at_once = SCATTERS // 2 if first else 0
                if shared:
                    scatter(i - 2, range(at_once))
                if second:
                    residual(i - 1)
                if shared:
                    scatter(i - 2, range(at_once, SCATTERS))
                if first:
                    hidden_rows(i)

            pool.wait_ge(tile_in[0], 16)
            fill(2, 0, lambda: pool.wait_ge(s["sh_h"], TT), lambda: pool.wait_ge(s["sh_y"], TT),
                 load_routed(2))
            pool.wait_ge(s["tables_ready"], 1)

            def refill(n, slot, load_next):
                first = pool.value_load(tab_start[0:1, bass.ds(n - 2, 1)], min_val=1,
                                        max_val=TILES)
                fill(n, slot, lambda: pool.wait_ge(s["d_h"], first),
                     lambda: pool.wait_ge(s["d_y"], first), load_next)

            with pool.Fori(3, NE - 1, 2) as n:
                refill(n, 1, load_routed(n))
                refill(n + 1, 0, load_routed(n + 1))
            refill(NE - 1, 1, load_routed(NE - 1))

            def add_rows(k):
                for parity in range(2):
                    last = NE - TOPK + k
                    stored = pool.value_load(tab_stored[0:1, parity, last:last + 1], min_val=0,
                                             max_val=16 * TILES)
                    pool.wait_ge(y_stored[parity], stored)
                    wait_alone()
                if k:
                    pool.wait_ge(s["gathered"], 16 * TT * k)
                for t in range(TT):
                    j = t * TOPK + k
                    g.indirect_dma_start(
                        out=acc_tile(t), out_offset=None, in_=expert_out,
                        in_offset=bass.IndirectOffsetOnAxis(ap=out_row[:, j:j + 1], axis=0),
                        compute_op=ALU.add).then_inc(
                            s["gathered"] if k < TOPK - 1 else last_gathered[t], 16)
                    if k == TOPK - 1 and t >= BEHIND:
                        store_out(t - BEHIND)

            BEHIND = 3

            def store_out(t):
                pool.wait_ge(last_gathered[t], 16)
                pool.dma_start(out_rows[t], acc_tile(t)).then_inc(s["out_stored"], 16)

            pool.wait_ge(s["out_rows_known"], 1)
            add_rows(0)
            refill(NE, 0, lambda which: None)
            for k in range(1, TOPK):
                add_rows(k)
            for t in range(TT - BEHIND, TT):
                store_out(t)

        @block.tensor
        def _(pe):
            mm, transpose = nc.tensor.matmul, nc.tensor.transpose

            pe.wait_ge(s["consts"], 1)
            pe.wait_ge(s["gate_rows_in"], 16)
            for c in range(KC):
                last = transpose(bank[0][:, c * NE:(c + 1) * NE],
                                 gate_rows[:, c * P:(c + 1) * P], ident[0:NE, 0:NE])
            last.then_inc(s["gate_t"], 1)

            def hidden(x_hi, x_lo, slot_at, into1, into3, chunks=range(KC)):
                outs = (into1[:, 0:H], into3[:, 0:H])
                for c in chunks:
                    for half, w, stop in ((x_hi, ring13_hi, False), (x_hi, ring13_lo, False),
                                          (x_lo, ring13_hi, True)):
                        for m in range(2):
                            last = mm(outs[m], half[:, c * P:(c + 1) * P],
                                      ring13(w, slot_at, c, m),
                                      start=(c == 0 and half is x_hi and w is ring13_hi),
                                      stop=(c == KC - 1 and stop))
                return last

            def hidden_t(act, into):
                for c, (at, size) in enumerate(HC):
                    last = transpose(into[0:size, c * P:(c + 1) * P], act[:, at:at + size],
                                     ident[:, :])
                return last

            def project(h_hi, h_lo, slot_at, into):
                n = 0
                for c, (_, size) in enumerate(HC):
                    for half, w in ((h_hi, ring2_hi), (h_hi, ring2_lo), (h_lo, ring2_hi)):
                        last = mm(into[:, :], half[0:size, c * P:(c + 1) * P],
                                  ring2(w, slot_at, c), start=(n == 0), stop=(n == 8))
                        n += 1
                return last

            def rows_t(tile, into, c, w):
                for r in range(ROWS):
                    last = transpose(into[:, r * P:(r + 1) * P], tile[:, r, c * P:(c + 1) * P],
                                     ident[:, :])
                return last

            def spread(into, column, chunks):
                for c in range(chunks):
                    last = transpose(into[:, c * P:(c + 1) * P],
                                     column[:, c:c + 1].to_broadcast([P, P]), ident[:, :])
                return last

            def c1(t, r):
                if r:
                    pe.wait_ge(s["sh_prod"], t)
                pe.wait_ge(s["xn2_lo"], t + 1)
                hidden(xt_hi[:, r, :], xt_lo[:, r, :], 0, bank[4], bank[5]).then_inc(s["sh_h"], 1)

            def c2(t, r):
                pe.wait_ge(s["sh_prod"], t + 1)
                if r:
                    pe.wait_ge(s["sh_lo"], t)
                hidden_t(h3[r % 2], bank[6]).then_inc(s["sh_t"], 1)

            def c3(t, r):
                pe.wait_ge(s["sh_lo"], t + 1)
                if r:
                    pe.wait_ge(s["sh_y_e"], t)
                project(ht_hi[r % 2], ht_lo[r % 2], 0, bank[7]).then_inc(s["sh_y"], 1)

            def w_columns(b, L):
                pe.wait_ge(s[f"wa{L}_loaded"], 16 * b + 16)
                if L == 1:
                    if b == 0:
                        pe.wait_ge(s["gate_lo_ready"], 1)
                    else:
                        pe.wait_ge(s["mm_e1"], ROWS * b)
                elif b:
                    pe.wait_ge(s["mm_e2"], ROWS * b)
                for c in range(LINEARS[L]):
                    if c >= 2:
                        pe.wait_ge(s[f"w_max{L}"], LINEARS[L] * b + c - 1)
                    rows_t(wa[L], bank[2 * (L - 1) + c % 2], c, 0).then_inc(s[f"w_t{L}"], 1)

            def x_columns(b, L):
                if L == 1:
                    pe.wait_ge(s["xn_ready"], ROWS * b + ROWS)
                else:
                    pe.wait_ge(s["a_ready"], b + 1)
                chunks = LINEARS[L]
                for c in range(chunks):
                    if c < 2:
                        pe.wait_ge(s[f"w_max{L}"], chunks * (b + 1) - 1 + c)
                    else:
                        pe.wait_ge(s[f"x_max{L}"], chunks * b + c - 1)
                    rows_t(xa[L], bank[2 * (L - 1) + c % 2], c, 0).then_inc(s[f"x_t{L}"], 1)

            def smoothing(b, L):
                pe.wait_ge(s[f"smooth{L}"], b + 1)
                for j in (1, 0):
                    spread(bank[2 * (L - 1) + j], small[L]["smooth"][:, j, :],
                           LINEARS[L]).then_inc(s[f"bc{L}"], 1)

            def quantised_t(b, L):
                pairs = LINEARS[L] // 2
                n = 0
                for q, ready, t_done in ((wq[L], f"wq_ready{L}", f"wq_t{L}"),
                                         (xq[L], f"xq_ready{L}", f"xq_t{L}")):
                    pe.wait_ge(s[ready], b + 1)
                    for j in range(pairs):
                        into = bank[2 * (L - 1) + n % 2][:, :].bitcast(BF16)
                        if n >= 2:
                            pe.wait_ge(s[f"wq_e{L}"], 2 * b + j + 1)
                        for i in range(2):
                            for r in range(ROWS):
                                at = (2 * j + i) * P
                                last = transpose(into[:, (i * ROWS + r) * P:(i * ROWS + r + 1) * P],
                                                 q[:, r, at:at + P], ident_b[:, :])
                        last.then_inc(s[t_done], 1)
                        n += 1

            def quantised_mm(b, L):
                pairs = LINEARS[L] // 2
                even, odd = bank[2 * (L - 1)], bank[2 * (L - 1) + 1]
                pe.wait_ge(s[f"xq_e{L}" if pairs == 2 else f"wq_e{L}"], pairs * b + 1)
                spread(even, small[L]["q_scale"][:, 1, :], ROWS).then_inc(s[f"wsc{L}"], 1)
                for r in range(ROWS):
                    if r == 0:
                        pe.wait_ge(s[f"xq_e{L}"], pairs * b + pairs)
                        pe.wait_ge(s[f"wq_e{L}"], pairs * b + pairs)
                    elif r == 1:
                        pe.wait_ge(s[f"wsc_e{L}"], b + 1)
                    else:
                        pe.wait_ge(s[f"mm_e{L}"], ROWS * b + r - 1)
                    for c in range(LINEARS[L]):
                        last = mm((even if r % 2 else odd)[:, :], xq_t[L][:, c, r * P:(r + 1) * P],
                                  wq_t[L][:, c, :], start=(c == 0), stop=(c == LINEARS[L] - 1))
                    last.then_inc(s[f"mm{L}"], 1)

            def normed_t(b):
                if b:
                    pe.wait_ge(s["sh_prod"], ROWS * b)
                for r in range(ROWS):
                    pe.wait_ge(s["xn2_ready"], ROWS * b + r + 1)
                    if r >= 2:
                        pe.wait_ge(s["xn2_lo"], ROWS * b + r - 1)
                    for c in range(KC):
                        last = transpose(bank[4 + r % 2][:, c * P:(c + 1) * P],
                                         xn2_of(b)[:, r, c * P:(c + 1) * P], ident[:, :])
                    last.then_inc(s["xn2_t"], 1)

            def router(b):
                pe.wait_ge(s["xn2_lo"], ROWS * b + ROWS)
                n = 0
                for c in range(KC):
                    for xh, gh in ((xt_hi, gate_hi), (xt_lo, gate_hi), (xt_hi, gate_lo)):
                        last = mm(bank[4][0:NE, :], gh[:, c, :], xh[:, :, c * P:(c + 1) * P],
                                  start=(n == 0), stop=(n == 3 * KC - 1))
                        n += 1
                last.then_inc(s["logits_by_expert"], 1)

            def logits_by_token(b):
                if b:
                    pe.wait_ge(s["sh_lo"], ROWS * b)
                pe.wait_ge(s["logits_copied"], b + 1)
                for r in range(ROWS):
                    last = transpose(beside[:, r * NE:(r + 1) * NE],
                                     logits_t[:, r * P:(r + 1) * P], ident[0:NE, 0:NE])
                last.then_inc(s["logits"], 1)

            def tokens_before(b):
                pe.wait_ge(s["taken_ready"], b + 1)
                for r in range(ROWS + 1):
                    into = beside[:, r * NE:(r + 1) * NE]
                    for q in range(min(r + 1, ROWS)):
                        last = mm(into, (before_b if q == r else ones_b)[:, :],
                                  taken[:, q * NE:(q + 1) * NE], start=(q == 0),
                                  stop=(q == min(r, ROWS - 1)))
                last.then_inc(s["prefix"], 1)

            for i in range(STEPS):
                first, second, shared, late = parts(i)
                b = i - 2
                t = b * ROWS
                if second:
                    w_columns(i - 1, 2)
                if first:
                    w_columns(i, 1)
                if late:
                    c3(t - 3, 1)
                    c1(t - 2, 2)
                if second:
                    x_columns(i - 1, 2)
                if late:
                    c1(t - 1, 3)
                if first:
                    x_columns(i, 1)
                if i == B + 1:
                    normed_t(b)
                if late:
                    c2(t - 2, 2)
                    c2(t - 1, 3)
                if shared and i <= B:
                    normed_t(b)
                if late:
                    c3(t - 2, 2)
                if shared:
                    router(b)
                if second:
                    smoothing(i - 1, 2)
                if first:
                    smoothing(i, 1)
                if late and i != B + 1:
                    c3(t - 1, 3)
                if shared:
                    logits_by_token(b)
                    if b == 0:
                        pe.wait_ge(s["ready2"], 1)
                    c1(t, 0)
                if second:
                    quantised_t(i - 1, 2)
                if shared:
                    tokens_before(b)
                if i == B + 1:
                    c3(t - 1, 3)
                if shared:
                    c1(t + 1, 1)
                if second:
                    quantised_mm(i - 1, 2)
                if first:
                    quantised_t(i, 1)
                if shared:
                    pe.wait_ge(s["rows_ready"], b + 1)
                    c2(t, 0)
                    c2(t + 1, 1)
                if first:
                    quantised_mm(i, 1)
                if shared:
                    c3(t, 0)

            pe.wait_ge(s["tables_ready"], 1)
            hbank = [(bank[4], bank[5]), (bank[0], bank[1])]

            def load_t(t, k):
                pe.wait_ge(tile_in[k], (t + 2 - k) * 8)
                for c in range(KC):
                    last = transpose(bank[2 + k][:, c * P:(c + 1) * P],
                                     x_in[k][:, c * P:(c + 1) * P], ident[:, :])
                last.then_inc(s["xr_t"], 1)

            def tile_step(t, k):
                fixed = isinstance(t, int)
                slot_at = None
                if not fixed or t < TILES:
                    need = pe.value_load(tab_need[0:1, bass.ds(t, 1)], min_val=0,
                                         max_val=NE + 1)
                    slot_at = pe.value_load(tab_slot[0:1, bass.ds(t, 1)], min_val=0,
                                            max_val=1) * W13
                    pe.wait_ge(s["ready3"], need)
                    pe.wait_ge(s["xr_lo_s"], t + 1)
                    if not fixed or t >= 2:
                        pe.wait_ge(s["d_prod"], t - 1)
                    hidden(xr_hi[k], xr_lo[k], slot_at, *hbank[k], chunks=range(KC // 2))
                if not fixed or t >= 1:
                    pe.wait_ge(s["d_act"], t)
                    if not fixed or t >= 2:
                        pe.wait_ge(s["d_lo"], t - 1)
                    hidden_t(h3[1 - k], bank[6]).then_inc(s["d_t"], 1)
                if not fixed or t < TILES:
                    hidden(xr_hi[k], xr_lo[k], slot_at, *hbank[k],
                           chunks=range(KC // 2, KC)).then_inc(s["d_h"], 1)
                if not fixed or t + 1 < TILES:
                    load_t(t + 1, 1 - k)
                if not fixed or t >= 1:
                    slot = pe.value_load(tab_slot[0:1, bass.ds(t - 1, 1)], min_val=0, max_val=1)
                    need = pe.value_load(tab_need[0:1, bass.ds(t - 1, 1)], min_val=0,
                                         max_val=NE + 1)
                    pe.wait_ge(s["ready2"], need)
                    pe.wait_ge(s["d_lo"], t)
                    if not fixed or t >= 2:
                        pe.wait_ge(s["d_y_e"], t - 1)
                    project(ht_hi[1 - k], ht_lo[1 - k], slot * W2, bank[7]).then_inc(s["d_y"], 1)

            load_t(0, 0)
            for t in range(3):
                tile_step(t, t % 2)
            with pe.Fori(3, TILES - 2, 2) as t:
                tile_step(t, 1)
                tile_step(t + 1, 0)
            for t in range(3 + 2 * len(range(3, TILES - 2, 2)), TILES + 1):
                tile_step(t, t % 2)

        @block.scalar
        def _(act):
            def copy(out, in_):
                return nc.scalar.activation(out, in_, ACT.Copy)

            act.wait_ge(s["consts"], 1)
            act.wait_ge(s["gates_in"], 48)
            nc.scalar.activation(gates[:, :], gates[:, :], ACT.Tanh).then_inc(s["gates_ready"], 1)
            act.wait_ge(s["gate_t"], 1)
            copy(gate_hi[:, :, :].rearrange("p c e -> p (c e)"), bank[0][:, 0:KC * NE]).then_inc(
                s["gate_hi_ready"], 1)

            def norm(b, n):
                act.wait_ge(s[f"ln_var{n}"], b + 1)
                nc.scalar.activation(small[n]["std"][:, :], small[n]["mean_var"][:, :, 1],
                                     ACT.Sqrt, bias=eps_ln[:, :]).then_inc(s[f"ln_std{n}"], 1)

            def smooth_root(b, L):
                act.wait_ge(s[f"ratio{L}"], b + 1)
                nc.scalar.activation(small[L]["ratio"][:, :], small[L]["ratio"][:, :],
                                     ACT.Sqrt).then_inc(s[f"s_raw{L}"], 1)

            def copy_s(b, L):
                act.wait_ge(s[f"bc{L}"], 2 * b + 2)
                copy(s_row[L][:, :], bank[2 * (L - 1)][:, 0:wide[L]]).then_inc(
                    s[f"s_copied{L}"], 1)

            def over_scales(b, L):
                act.wait_ge(s[f"scales{L}"], b + 1)
                for w, t, ready in ((1, wa[L], f"wt{L}"), (0, xa[L], f"xs{L}")):
                    for r in range(ROWS):
                        last = nc.scalar.activation(t[:, r, :], t[:, r, :], ACT.Copy,
                                                    scale=small[L]["q_inv"][:, w, r:r + 1])
                    last.then_inc(s[ready], 1)

            def quantised_copies(b, L):
                pairs = LINEARS[L] // 2
                n = 0
                for dst, t_done, t_read in ((wq_t[L], f"wq_t{L}", f"wq_e{L}"),
                                            (xq_t[L], f"xq_t{L}", f"xq_e{L}")):
                    for j in range(pairs):
                        act.wait_ge(s[t_done], pairs * b + j + 1)
                        copy(dst[:, 2 * j:2 * j + 2, :].rearrange("p c t -> p (c t)"),
                             bank[2 * (L - 1) + n % 2][:, :].bitcast(BF16)).then_inc(s[t_read], 1)
                        n += 1

            def weight_scales(b, L):
                act.wait_ge(s[f"wsc{L}"], b + 1)
                if L == 1:
                    copy(wscale1[:, :], bank[0][:, :]).then_inc(s["wsc_e1"], 1)
                else:
                    nc.scalar.activation(wscale2[:, :], bank[2][:, :], ACT.Copy,
                                         scale=gates[:, 0:1]).then_inc(s["wsc_e2"], 1)

            def first_out(b):
                for r in range(ROWS):
                    act.wait_ge(s["mm1"], ROWS * b + r + 1)
                    nc.scalar.activation(hid[:, r, :], bank[1 - r % 2][:, :], ACT.Copy,
                                         scale=small[1]["q_scale"][:, 0, r:r + 1]).then_inc(
                                             s["mm_e1"], 1)

            def silu_gate(b):
                act.wait_ge(s["gate_half"], b + 1)
                nc.scalar.activation(hid[:, :, 0:I], hid[:, :, 0:I], ACT.Silu).then_inc(
                    s["silu_gate"], 1)

            def normed_halves(b):
                for r in range(ROWS):
                    act.wait_ge(s["xn2_t"], ROWS * b + r + 1)
                    copy(xt_hi[:, r, :], bank[4 + r % 2][:, :]).then_inc(s["xn2_hi"], 1)

            def copy_logits(b):
                act.wait_ge(s["logits_by_expert"], b + 1)
                copy(logits_t[:, :], bank[4][0:NE, :]).then_inc(s["logits_copied"], 1)

            def scores(b):
                act.wait_ge(s["logits"], b + 1)
                nc.scalar.activation(score[:, :], beside[:, 0:ROWS * NE], ACT.Exp,
                                     scale=-1.0).then_inc(s["exp_ready"], 1)

            def a1(t, r):
                act.wait_ge(s["sh_h"], t + 1)
                nc.scalar.activation(h1[r % 2][:, :], bank[4][:, 0:H], ACT.Silu).then_inc(
                    s["sh_h1"], 1)

            def a2(t, r):
                act.wait_ge(s["sh_t"], t + 1)
                copy(ht_hi[r % 2][:, :], bank[6][:, 0:len(HC) * P]).then_inc(s["sh_hi"], 1)

            expert_rows = expert_out.rearrange("(n t p) d -> n p t d", t=CLEAR, p=P)

            def clear_results(n):
                act.dma_start(expert_rows[bass.ds(n, 1)].rearrange("n p t d -> p (n t) d"),
                              zero_rows[:, 0:D].unsqueeze(1).to_broadcast([P, CLEAR, D])).then_inc(
                                  s["cleared"], 16)

            norm(0, 1)
            for i in range(STEPS):
                first, second, shared, late = parts(i)
                t = (i - 2) * ROWS
                linears = [2] * second + [1] * first
                if first and second:
                    for part in range(3):
                        clear_results((i - 1) * 3 + part)
                if shared:
                    norm(i - 2, 2)
                if late:
                    a1(t - 2, 2)
                    a1(t - 1, 3)
                if i == B + 1:
                    normed_halves(i - 2)
                if late:
                    a2(t - 2, 2)
                    a2(t - 1, 3)
                if shared and i <= B:
                    normed_halves(i - 2)
                for L in linears:
                    smooth_root(i + 1 - L, L)
                if shared:
                    copy_logits(i - 2)
                for L in linears:
                    copy_s(i + 1 - L, L)
                if second:
                    over_scales(i - 1, 2)
                if shared:
                    scores(i - 2)
                    a1(t, 0)
                if first:
                    over_scales(i, 1)
                if second:
                    quantised_copies(i - 1, 2)
                if shared:
                    a1(t + 1, 1)
                if second:
                    weight_scales(i - 1, 2)
                if first:
                    quantised_copies(i, 1)
                if i + 1 < B:
                    norm(i + 1, 1)
                if shared:
                    a2(t, 0)
                    a2(t + 1, 1)
                if first:
                    weight_scales(i, 1)
                    first_out(i)
                    silu_gate(i)

            def tile_step(t, k):
                fixed = isinstance(t, int)
                if not fixed or t >= 1:
                    act.wait_ge(s["d_t"], t)
                    copy(ht_hi[1 - k][:, :], bank[6][:, 0:len(HC) * P]).then_inc(s["d_hi"], 1)
                if not fixed or t < TILES:
                    act.wait_ge(s["d_h"], t + 1)
                    copy(h1[k][:, :], [bank[4], bank[0]][k][:, 0:H]).then_inc(s["d_h1"], 1)
                if not fixed or t + 1 < TILES:
                    act.wait_ge(s["xr_t"], t + 2)
                    copy(xr_hi[1 - k][:, :], bank[3 - k][:, :]).then_inc(s["xr_hi_s"], 1)
                if not fixed or t < TILES:
                    act.wait_ge(s["d_prod"], t + 1)
                    nc.scalar.activation(h3[k][:, :], h1[k][:, :], ACT.Silu).then_inc(
                        s["d_act"], 1)

            act.wait_ge(s["xr_t"], 1)
            act.wait_ge(s["tables_ready"], 1)
            copy(xr_hi[0][:, :], bank[2][:, :]).then_inc(s["xr_hi_s"], 1)
            for t in range(3):
                tile_step(t, t % 2)
            with act.Fori(3, TILES - 2, 2) as t:
                tile_step(t, 1)
                tile_step(t + 1, 0)
            for t in range(3 + 2 * len(range(3, TILES - 2, 2)), TILES + 1):
                tile_step(t, t % 2)

        @block.vector
        def _(dve):
            v = nc.vector
            chain = {"n": 0}

            def step(ins):
                chain["n"] += 1
                ins.then_inc(s["dve_chain"], 1)

            def settle():
                dve.wait_ge(s["dve_chain"], chain["n"])

            def link(ins):
                step(ins)
                settle()

            dve.wait_ge(s["gate_hi_ready"], 1)
            v.tensor_tensor(gate_lo[:, :, :].rearrange("p c e -> p (c e)"), bank[0][:, 0:KC * NE],
                            gate_hi[:, :, :].rearrange("p c e -> p (c e)").bitcast(F32),
                            ALU.subtract).then_inc(s["gate_lo_ready"], 1)
            link(v.memset(bank[6][:, 0:3 * P], 0.0))

            def norm_stats(b, n):
                m = small[n]
                for r in range(ROWS):
                    last = v.bn_stats(m["stats"][:, r, :], acc_tile(b * ROWS + r))
                link(last)
                for r in range(ROWS):
                    last = v.bn_aggr(m["mean_var"][:, r, :], m["stats"][:, r, :])
                last.then_inc(s[f"ln_var{n}"], 1)

            def norm(b, n, dst, ready):
                m = small[n]
                dve.wait_ge(s[f"ln_std{n}"], b + 1)
                link(v.reciprocal(m["rstd"][:, :], m["std"][:, :]))
                for r in range(ROWS):
                    v.tensor_scalar(dst[:, r, 0:D], acc_tile(b * ROWS + r),
                                    m["mean_var"][:, r, 0:1], m["rstd"][:, r:r + 1],
                                    ALU.subtract, ALU.mult).then_inc(s[ready], 1)

            def column_max(b, which, L):
                for c in range(LINEARS[L]):
                    dve.wait_ge(s[f"{which}_t{L}"], LINEARS[L] * b + c + 1)
                    j = {"x": 0, "w": 1}[which]
                    v.tensor_reduce(small[L]["amax"][:, j, c:c + 1],
                                    bank[2 * (L - 1) + c % 2][:, :], AX.X, ALU.max,
                                    apply_absolute_value=True).then_inc(s[f"{which}_max{L}"], 1)

            def smoothing(b, L):
                m = small[L]
                dve.wait_ge(s[f"w_max{L}"], LINEARS[L] * (b + 1))
                dve.wait_ge(s[f"x_max{L}"], LINEARS[L] * (b + 1))
                link(v.tensor_scalar(m["amax"][:, :, :], m["amax"][:, :, :], Q_EPS, None, ALU.max))
                link(v.reciprocal(m["amax"][:, 1, :], m["amax"][:, 1, :]))
                v.tensor_tensor(m["ratio"][:, :], m["amax"][:, 0, :], m["amax"][:, 1, :],
                                ALU.mult).then_inc(s[f"ratio{L}"], 1)

            def smoothed(b, L):
                m = small[L]
                dve.wait_ge(s[f"s_raw{L}"], b + 1)
                link(v.tensor_scalar(m["smooth"][:, 0, :], m["ratio"][:, :], Q_EPS, None, ALU.max))
                v.reciprocal(m["smooth"][:, 1, :], m["smooth"][:, 0, :]).then_inc(
                    s[f"smooth{L}"], 1)

            def smooth_and_scale(b, L):
                k, m = wide[L], small[L]
                dve.wait_ge(s[f"bc{L}"], 2 * b + 1)
                link(v.tensor_tensor(xa[L][:, :, :], xa[L][:, :, :],
                                     bank[2 * L - 1][:, 0:k].unsqueeze(1).to_broadcast(
                                         [P, ROWS, k]), ALU.mult))
                step(v.tensor_reduce(m["row_max"][:, 0, :], xa[L][:, :, :], AX.X, ALU.max,
                                     apply_absolute_value=True))
                dve.wait_ge(s[f"ws_ready{L}"], b + 1)
                link(v.tensor_reduce(m["row_max"][:, 1, :], wa[L][:, :, :], AX.X, ALU.max,
                                     apply_absolute_value=True))
                link(v.tensor_scalar(m["q_scale"][:, :, :], m["row_max"][:, :, :], Q_EPS,
                                     1.0 / QMAX, ALU.max, ALU.mult))
                v.reciprocal(m["q_inv"][:, :, :], m["q_scale"][:, :, :]).then_inc(
                    s[f"scales{L}"], 1)

            def quantise(b, L, which):
                t, q, scaled, ready = {"w": (wa[L], wq[L], f"wt{L}", f"wq_ready{L}"),
                                       "x": (xa[L], xq[L], f"xs{L}", f"xq_ready{L}")}[which]
                dve.wait_ge(s[scaled], b + 1)
                link(v.tensor_scalar(t[:, :, :], t[:, :, :], -QMAX, ROUND, ALU.max, ALU.add))
                v.tensor_scalar(q[:, :, :], t[:, :, :], ROUND, QMAX, ALU.subtract,
                                ALU.min).then_inc(s[ready], 1)

            def second_out(b):
                dve.wait_ge(s["wsc_e2"], b + 1)
                for r in range(ROWS):
                    dve.wait_ge(s["mm2"], ROWS * b + r + 1)
                    if b and r == 0:
                        dve.wait_ge(s["x1_done"], ROWS * b)
                    v.scalar_tensor_tensor(out2[r], bank[3 - r % 2][:, :],
                                           small[2]["q_scale"][:, 0, r:r + 1], wscale2[:, :],
                                           ALU.mult, ALU.mult).then_inc(s["mm_e2"], 1)

            def normed(b):
                dve.wait_ge(s["x1_done"], ROWS * b + ROWS)
                if 0 < b < B - 1:
                    dve.wait_ge(s["scattered"], 16 * SCATTERS * b)
                norm_stats(b, 2)
                norm(b, 2, xn2_of(b), "xn2_ready")

            def low_halves(b):
                for r in range(ROWS):
                    dve.wait_ge(s["xn2_hi"], ROWS * b + r + 1)
                    v.tensor_tensor(xt_lo[:, r, :], bank[4 + r % 2][:, :],
                                    xt_hi[:, r, :].bitcast(F32), ALU.subtract).then_inc(
                                        s["xn2_lo"], 1)

            def sh_product(t, r):
                dve.wait_ge(s["sh_h1"], t + 1)
                v.tensor_tensor(h3[r % 2][:, :], h1[r % 2][:, :], bank[5][:, 0:H],
                                ALU.mult).then_inc(s["sh_prod"], 1)

            def sh_low(t, r):
                dve.wait_ge(s["sh_hi"], t + 1)
                v.tensor_tensor(ht_lo[r % 2][:, :], bank[6][:, 0:len(HC) * P],
                                ht_hi[r % 2][:, :].bitcast(F32), ALU.subtract).then_inc(
                                    s["sh_lo"], 1)

            def sh_add(t, r):
                dve.wait_ge(s["sh_y"], t + 1)
                v.scalar_tensor_tensor(acc_tile(t), bank[7][:, :], gates[:, 1:2], acc_tile(t),
                                       ALU.mult, ALU.add).then_inc(s["sh_y_e"], 1)

            def choose(b):
                dve.wait_ge(s["exp_ready"], b + 1)
                by_expert = score[:, :].rearrange("p (r e) -> p r e", r=ROWS)
                link(v.tensor_scalar(score[:, :], score[:, :], 1.0, None, ALU.add))
                link(v.reciprocal(score[:, :], score[:, :]))
                link(v.tensor_tensor(by_expert, by_expert,
                                     bias_e[:, :].unsqueeze(1).to_broadcast([P, ROWS, NE]),
                                     ALU.add))
                for r in range(ROWS):
                    step(v.max(top8[:, r, :], by_expert[:, r, :]))
                settle()
                for r in range(ROWS):
                    step(v.max_index(top8_at[:, r, :], top8[:, r, :], by_expert[:, r, :]))
                settle()
                link(v.tensor_copy(top_at[:, :].rearrange("p (r k) -> p r k", r=ROWS),
                                   top8_at[:, :, 0:TOPK]))
                link(v.tensor_tensor(
                    onehot[:, :].rearrange("p (j e) -> p j e", e=NE),
                    iota_e[:, :].unsqueeze(1).to_broadcast([P, ROWS * TOPK, NE]),
                    top_at[:, :].unsqueeze(2).to_broadcast([P, ROWS * TOPK, NE]),
                    ALU.is_equal))
                with nc.allow_low_precision("zeros and ones"):
                    v.tensor_reduce(
                        taken[:, :].rearrange("p (r e) -> p r e", r=ROWS),
                        onehot[:, :].rearrange("p (r k e) -> p r e k", r=ROWS, k=TOPK),
                        AX.X, ALU.add).then_inc(s["taken_ready"], 1)
                link(v.tensor_reduce(total4[:, :], top8[:, :, 0:TOPK], AX.X, ALU.add))

            def place_rows(b):
                by_expert = score[:, :].rearrange("p (r e) -> p r e", r=ROWS)
                by_taken = taken[:, :].rearrange("p (r e) -> p r e", r=ROWS)
                dve.wait_ge(s["taken_ready"], b + 1)
                link(v.reciprocal(total4[:, :], total4[:, :]))
                link(v.tensor_tensor(weight[:, :, :], by_expert,
                                     total4[:, :].unsqueeze(2).to_broadcast([P, ROWS, NE]),
                                     ALU.mult))
                link(v.tensor_tensor(weight[:, :, :], weight[:, :, :], by_taken, ALU.mult))
                step(v.tensor_scalar(xn2_of(b)[:, :, D:ROW], weight[:, :, :], gates[:, 1:2], None,
                                     ALU.mult))
                link(v.tensor_tensor_scan(rank[:, :], not_first[:, :, :].rearrange(
                    "p r e -> p (r e)"), taken[:, :], 0.0, ALU.mult, ALU.add))
                link(v.tensor_tensor(rank[:, :], rank[:, :], taken[:, :], ALU.mult))
                shape = [P, ROWS, TOPK, NE]
                link(v.tensor_tensor(
                    onehot[:, :].rearrange("p (r k e) -> p r k e", r=ROWS, k=TOPK),
                    rank[:, :].rearrange("p (r e) -> p r e", r=ROWS).unsqueeze(2).to_broadcast(
                        shape),
                    iota_k[:, :].unsqueeze(1).unsqueeze(3).to_broadcast(shape), ALU.is_equal))
                step(v.tensor_copy(onehot_all[:, bass.ds(b * BE, BE)], onehot[:, :]))
                dve.wait_ge(s["prefix"], b + 1)
                link(v.tensor_tensor(pos[:, :].rearrange("p (r e) -> p r e", r=ROWS),
                                     beside[:, 0:ROWS * NE].rearrange("p (r e) -> p r e", r=ROWS),
                                     next_row[:, :].unsqueeze(1).to_broadcast([P, ROWS, NE]),
                                     ALU.add))
                step(v.tensor_tensor(next_row[:, :], next_row[:, :],
                                     beside[:, ROWS * NE:(ROWS + 1) * NE], ALU.add))
                step(v.tensor_tensor(
                    picked[:, :].rearrange("p (r k e) -> p r k e", r=ROWS, k=TOPK),
                    onehot[:, :].rearrange("p (r k e) -> p r k e", r=ROWS, k=TOPK),
                    pos[:, :].rearrange("p (r e) -> p r e", r=ROWS).unsqueeze(2).to_broadcast(
                        shape), ALU.mult))
                settle()
                link(v.tensor_reduce(row_f[:, :],
                                     picked[:, :].rearrange("p (j e) -> p j e", e=NE),
                                     AX.X, ALU.add))
                if b:
                    dve.wait_ge(s["scattered"], 16 * SCATTERS * b)
                v.tensor_copy(row_u[:, :], row_f[:, :]).then_inc(s["rows_ready"], 1)
                link(v.tensor_copy(row_all[:, bass.ds(b * ROWS * TOPK, ROWS * TOPK)],
                                   row_f[:, :]))

            def tables():
                link(v.tensor_tensor(count[:, :], next_row[:, :], first_row[:, :], ALU.subtract))
                link(v.tensor_scalar(tiles_i[:, :], count[:, :], float(P - 1), None, ALU.add))
                link(v.tensor_scalar(tiles_i[:, :], tiles_i[:, :], 7, None,
                                     ALU.arith_shift_right))
                link(v.tensor_scalar(tiles_f[:, :], tiles_i[:, :], 1.0, None, ALU.max))
                link(v.tensor_tensor_scan(tile_end[:, :], one_e[:, :], tiles_f[:, :], 0.0, ALU.mult,
                                          ALU.add))
                link(v.tensor_tensor(tile_start[:, :], tile_end[:, :], tiles_f[:, :], ALU.subtract))
                link(v.tensor_copy(tab_start[:, :], tile_start[0:1, :]))
                link(v.tensor_scalar(tab_stored[:, 0, :], tile_end[0:1, :], 1.0, None, ALU.add))
                link(v.tensor_copy(tab_stored[:, 1, :], tile_end[0:1, :]))
                link(v.tensor_scalar(tab_stored[:, :, :], tab_stored[:, :, :], 1, 4,
                                     ALU.arith_shift_right, ALU.logical_shift_left))
                link(v.scalar_tensor_tensor(row_base[:, :], tile_end[:, :], -float(P),
                                            next_row[:, :], ALU.mult, ALU.add))
                row3 = [1, TILES, NE]
                link(v.tensor_tensor(begun[:, :, :],
                                     tile_start[0:1, :].unsqueeze(1).to_broadcast(row3),
                                     iota_t[:, :].unsqueeze(2).to_broadcast(row3), ALU.is_le))
                link(v.tensor_reduce(tile_expert[:, :], begun[:, :, :], AX.X, ALU.add))

            def more_tables():
                row3 = [1, TILES, NE]
                link(v.tensor_tensor(begun[:, :, :], begun[:, :, :],
                                     row_base[0:1, :].unsqueeze(1).to_broadcast(row3), ALU.mult))
                link(v.tensor_reduce(tile_base[:, :], begun[:, :, :], AX.X, ALU.max))
                link(v.tensor_scalar(tab_need[:, :], tile_expert[:, :], 1.0, None, ALU.add))
                link(v.tensor_scalar(tab_expert[:, :], tile_expert[:, :], 1.0, None, ALU.subtract))
                link(v.tensor_copy(tab_slot[:, :], tile_expert[:, :]))
                link(v.tensor_scalar(tab_slot[:, :], tab_slot[:, :], 1, None, ALU.bitwise_and))
                link(v.tensor_scalar(last_tile[:, :], next_row[0:1, NE - 1:NE], float(P), None,
                                     ALU.subtract))
                link(v.scalar_tensor_tensor(tile_base[:, :], iota_t[:, :], float(P),
                                            tile_base[:, :], ALU.mult, ALU.add))
                v.tensor_scalar(tab_row[:, :], tile_base[:, :], last_tile[:, :], None,
                                ALU.min).then_inc(s["tables_ready"], 1)

            dve.wait_ge(s["gates_ready"], 1)
            dve.wait_ge(s["consts"], 1)
            dve.wait_ge(s["x_loaded"], 16)
            norm_stats(0, 1)
            norm(0, 1, xa1, "xn_ready")
            for i in range(STEPS):
                first, second, shared, late = parts(i)
                b = i - 2
                t = b * ROWS
                linears = [2] * second + [1] * first
                if second:
                    column_max(i - 1, "w", 2)
                if late:
                    sh_add(t - 4, 0)
                if i == STEPS - 1:
                    tables()
                if first:
                    column_max(i, "w", 1)
                if shared:
                    normed(b)
                if late:
                    sh_add(t - 3, 1)
                    sh_product(t - 2, 2)
                if i == STEPS - 1:
                    more_tables()
                if second:
                    column_max(i - 1, "x", 2)
                if late:
                    sh_product(t - 1, 3)
                if first:
                    column_max(i, "x", 1)
                if i == B + 1:
                    low_halves(b)
                if late:
                    sh_low(t - 2, 2)
                    sh_low(t - 1, 3)
                if shared and i <= B:
                    low_halves(b)
                for L in linears:
                    smoothing(i + 1 - L, L)
                for L in linears:
                    smoothed(i + 1 - L, L)
                if i == B + 1:
                    choose(b)
                if late:
                    sh_add(t - 2, 2)
                if second:
                    smooth_and_scale(i - 1, 2)
                if first:
                    smooth_and_scale(i, 1)
                if i == B + 1:
                    place_rows(b)
                elif late:
                    sh_add(t - 1, 3)
                if shared:
                    sh_product(t, 0)
                if second:
                    quantise(i - 1, 2, "w")
                    quantise(i - 1, 2, "x")
                if shared and i <= B:
                    choose(b)
                if first:
                    quantise(i, 1, "w")
                if i == B + 1:
                    sh_add(t - 1, 3)
                elif shared:
                    place_rows(b)
                if first:
                    quantise(i, 1, "x")
                if second:
                    second_out(i - 1)
                if i + 1 < B:
                    dve.wait_ge(s["x_loaded"], 16 * (i + 2))
                    norm_stats(i + 1, 1)
                if shared:
                    sh_product(t + 1, 1)
                    sh_low(t, 0)
                    sh_low(t + 1, 1)
                if i + 1 < B:
                    norm(i + 1, 1, xa1, "xn_ready")

            def wait_alone():
                dve.nop(nofuse=True)

            def low_rows(t, k):
                expert = dve.value_load(tab_expert[0:1, bass.ds(t, 1)], min_val=0, max_val=NE - 1)
                dve.wait_ge(s["xr_hi_s"], t + 1)
                v.tensor_tensor(xr_lo[k][:, :], bank[2 + k][:, :], xr_hi[k][:, :].bitcast(F32),
                                ALU.subtract).then_inc(s["xr_lo_s"], 1)
                v.tensor_copy(tile_weight[:, bass.ds(t, 1)],
                              x_in[k][:, bass.ds(expert + D, 1)]).then_inc(s["weight_picked"], 1)

            def tile_step(t, k):
                fixed = isinstance(t, int)
                if not fixed or t >= 1:
                    dve.wait_ge(s["d_hi"], t)
                    v.tensor_tensor(ht_lo[1 - k][:, :], bank[6][:, 0:len(HC) * P],
                                    ht_hi[1 - k][:, :].bitcast(F32), ALU.subtract).then_inc(
                                        s["d_lo"], 1)
                if not fixed or t < TILES:
                    dve.wait_ge(s["d_h1"], t + 1)
                    v.tensor_tensor(h1[k][:, :], h1[k][:, :], [bank[5], bank[1]][k][:, 0:H],
                                    ALU.mult).then_inc(s["d_prod"], 1)
                if not fixed or t + 1 < TILES:
                    low_rows(t + 1, 1 - k)
                if not fixed or t >= 1:
                    dve.wait_ge(s["d_y"], t)
                    if not fixed or t >= 3:
                        dve.wait_ge(y_stored[1 - k], (t + (k - 2)) * 8)
                    dve.wait_ge(s["weight_picked"], t)
                    wait_alone()
                    v.tensor_scalar(y_out[1 - k][:, :], bank[7][:, :],
                                    tile_weight[:, bass.ds(t - 1, 1)], None, ALU.mult).then_inc(
                                        s["d_y_e"], 1)

            low_rows(0, 0)

            link(v.tensor_tensor(
                shifted[:, :, :], onehot_all[:, :].rearrange("p (j e) -> p j e", e=NE),
                row_base[:, :].unsqueeze(1).to_broadcast([P, TT * TOPK, NE]), ALU.mult))
            link(v.tensor_reduce(out_row_f[:, :], shifted[:, :, :], AX.X, ALU.add))
            link(v.tensor_tensor(out_row_f[:, :], row_all[:, :], out_row_f[:, :], ALU.subtract))
            v.tensor_copy(out_row[:, :], out_row_f[:, :]).then_inc(s["out_rows_known"], 1)

            for t in range(3):
                tile_step(t, t % 2)
            with dve.Fori(3, TILES - 2, 2) as t:
                tile_step(t, 1)
                tile_step(t + 1, 0)
            for t in range(3 + 2 * len(range(3, TILES - 2, 2)), TILES + 1):
                tile_step(t, t % 2)


_INS = ["x", "fside_BxS2xS2_0", "ctx_1024", "g_xattn", "g_ffn", "L0_ffn_gate_w", "L0_ffn_gate_b",
        "L0_ffn_w1_shared", "L0_ffn_w2_shared", "L0_ffn_w3_shared", "L0_ffn_w1_routed",
        "L0_ffn_w2_routed", "L0_ffn_w3_routed"]
_OUTS = [((4, 512, 512), "float32")]


def kernel(**inputs):
    import numpy as _np
    import concourse.bacc as _bacc
    from concourse import mybir as _mybir
    from concourse.bass_utils import run_bass_kernel_spmd as _run

    nc = _bacc.Bacc("TRN2", target_bir_lowering=False, num_devices=1)
    arrays, args = {}, []
    for name in _INS:
        a = _np.ascontiguousarray(inputs[name])
        arrays[f"in_{name}_dram"] = a
        args.append(nc.dram_tensor(f"in_{name}_dram", a.shape, _mybir.dt.from_np(a.dtype),
                                   kind="ExternalInput").ap())
    for i, (shape, dtype) in enumerate(_OUTS):
        args.append(nc.dram_tensor(f"out_{i}_dram", shape, _mybir.dt.from_np(_np.dtype(dtype)),
                                   kind="ExternalOutput").ap())
    flamingo_moe(nc, *args)
    r = _run(nc, [arrays], core_ids=[0])
    return r.results[0]["out_0_dram"]
```
